# Optimizing a Trainium2 kernel written in Bass

```python
import numpy as np
import jax
import jax.numpy as jnp

def _softmax(x, axis=-1):
    return jax.nn.softmax(x, axis=axis)

def _gelu(x):
    return jax.nn.gelu(x, approximate=True)

def _silu(x):
    return jax.nn.silu(x)

def _sigmoid(x):
    return jax.nn.sigmoid(x)

def _layernorm(x, axis=-1, eps=1e-05):
    m = jnp.mean(x, axis=axis, keepdims=True)
    v = jnp.var(x, axis=axis, keepdims=True)
    return (x - m) / jnp.sqrt(v + eps)

def _scatter_add(tgt, idx, src, axis=0):
    return tgt.at[idx].add(src)

def _segment_sum(src, seg, n):
    return jax.ops.segment_sum(src, seg, n)
kernel_name = 'mk_xattn_seq_d2_seqx_r8_8d26d3'

def setup_inputs(seed: int=0):
    np.random.seed(seed)
    _w = jnp.asarray

    def _rec_inputs():
        import jax
        import jax.numpy as jnp
        _rk = jax.random.key(seed)
        x = -0.0002928 + 1 * jax.random.normal(jax.random.fold_in(_rk, 1), (8, 56, 128), jnp.float32)
        _lenS = 56 - jax.random.randint(jax.random.fold_in(_rk, 7), (8,), 0, max(1, 56 // 4) + 1, jnp.int32)
        _lenS2 = 1500 - jax.random.randint(jax.random.fold_in(_rk, 8), (8,), 0, max(1, 1500 // 4) + 1, jnp.int32)
        _ctx_1024P = jax.random.normal(jax.random.fold_in(_rk, 11), (8, 16, 128), jnp.float32)
        _ctx_1024c = jax.random.dirichlet(jax.random.fold_in(_rk, 511), 0.3 * jnp.ones((16,), jnp.float32), (8, 1500))
        _ctx_1024t = jnp.einsum('bsk,bkd->bsd', _ctx_1024c, _ctx_1024P)
        _ctx_1024t = _ctx_1024t * jax.lax.rsqrt(jnp.mean(jnp.square(_ctx_1024t)) + 1e-12) * 0.953939
        ctx_1024 = -1.39393e-06 + 0.999914 * (_ctx_1024t + 0.3 * jax.random.normal(jax.random.fold_in(_rk, 611), (8, 1500, 128), jnp.float32))
        _validS = jnp.arange(56)[None, :] < _lenS[:, None]
        _validS2 = jnp.arange(1500)[None, :] < _lenS2[:, None]
        _causal = jnp.tril(jnp.ones((56, 56), dtype=bool))
        mask_BxS2_bf1 = jnp.ones((8, 1500), dtype=bool)
        return (x, ctx_1024, mask_BxS2_bf1)
    x, ctx_1024, mask_BxS2_bf1 = _rec_inputs()

    def _L0_xattn_setup():
        import jax, jax.numpy as jnp
        import numpy as np
        B, S, SE, D, H, FF, E, K = (2, 256, 256, 128, 16, 512, 8, 2)
        HD = D // H

        def _layernorm(x, g, b):
            m = x.mean(-1, keepdims=True)
            v = ((x - m) ** 2).mean(-1, keepdims=True)
            return (x - m) / jnp.sqrt(v + 1e-05) * g + b

        def _attn(q_in, k_in, v_in, wq, bq, wk, bk, wv, bv, wo, bo, causal):
            Bq, Sq, Dm = q_in.shape
            Sk = k_in.shape[1]
            Q = (q_in @ wq + bq).reshape(Bq, Sq, H, HD)
            Kp = (k_in @ wk + bk).reshape(Bq, Sk, H, HD)
            V = (v_in @ wv + bv).reshape(Bq, Sk, H, HD)
            scores = jnp.einsum('bqhd,bkhd->bhqk', Q, Kp) / jnp.sqrt(jnp.float32(HD))
            if causal:
                mask = jnp.tril(jnp.ones((Sq, Sk), bool))
                scores = jnp.where(mask, scores, -jnp.inf)
            a = jax.nn.softmax(scores, axis=-1)
            o = jnp.einsum('bhqk,bkhd->bqhd', a, V).reshape(Bq, Sq, Dm)
            return o @ wo + bo

        def _moe(x, rw, rb, w1, b1, w2, b2):
            T = x.shape[0] * x.shape[1]
            xf = x.reshape(T, D)
            router_weights = jax.nn.softmax(xf @ rw + rb, axis=-1)
            topw, topi = jax.lax.top_k(router_weights, K)
            topw = jax.nn.softmax(topw, axis=-1)
            combine = jnp.zeros((T, E), xf.dtype).at[jnp.arange(T)[:, None], topi].add(topw)
            h = jax.nn.gelu(jnp.einsum('td,edf->etf', xf, w1) + b1[:, None, :], approximate=False)
            eo = jnp.einsum('etf,efd->etd', h, w2) + b2[:, None, :]
            out = jnp.einsum('etd,te->td', eo, combine)
            return out.reshape(x.shape)
        key = jax.random.key(seed)
        ks = jax.random.split(key, 32)
        w = lambda k, shape: jax.random.normal(k, shape, jnp.float32) * 0.02
        inp = {'x': jax.random.normal(ks[0], (B, S, D), jnp.float32), 'encoder_output': jax.random.normal(ks[1], (B, SE, D), jnp.float32), 'sa_wq': w(ks[2], (D, D)), 'sa_bq': jnp.zeros((D,), jnp.float32), 'sa_wk': w(ks[3], (D, D)), 'sa_bk': jnp.zeros((D,), jnp.float32), 'sa_wv': w(ks[4], (D, D)), 'sa_bv': jnp.zeros((D,), jnp.float32), 'sa_wo': w(ks[5], (D, D)), 'sa_bo': jnp.zeros((D,), jnp.float32), 'ca_wq': w(ks[6], (D, D)), 'ca_bq': jnp.zeros((D,), jnp.float32), 'ca_wk': w(ks[7], (D, D)), 'ca_bk': jnp.zeros((D,), jnp.float32), 'ca_wv': w(ks[8], (D, D)), 'ca_bv': jnp.zeros((D,), jnp.float32), 'ca_wo': w(ks[9], (D, D)), 'ca_bo': jnp.zeros((D,), jnp.float32), 'ln1_g': jnp.ones((D,), jnp.float32), 'ln1_b': jnp.zeros((D,), jnp.float32), 'ln2_g': jnp.ones((D,), jnp.float32), 'ln2_b': jnp.zeros((D,), jnp.float32), 'ln3_g': jnp.ones((D,), jnp.float32), 'ln3_b': jnp.zeros((D,), jnp.float32), 'router_w': w(ks[10], (D, E)), 'router_b': jnp.zeros((E,), jnp.float32), 'e_w1': w(ks[11], (E, D, FF)), 'e_b1': jnp.zeros((E, FF), jnp.float32), 'e_w2': w(ks[12], (E, FF, D)), 'e_b2': jnp.zeros((E, D), jnp.float32)}
        return inp
    _L0_xattn_all = _L0_xattn_setup()
    _L0_xattn_in = {k: v for k, v in _L0_xattn_all.items() if k in ('sa_wq', 'sa_bq', 'sa_wk', 'sa_bk', 'sa_wv', 'sa_bv', 'sa_wo', 'sa_bo', 'ca_wq', 'ca_bq', 'ca_wk', 'ca_bk', 'ca_wv', 'ca_bv', 'ca_wo', 'ca_bo', 'ln1_g', 'ln1_b', 'ln2_g', 'ln2_b', 'ln3_g', 'ln3_b', 'router_w', 'router_b', 'e_w1', 'e_b1', 'e_w2', 'e_b2')}
    del _L0_xattn_all

    def _L1_xattn_setup():
        import jax, jax.numpy as jnp
        import numpy as np
        EPS = 1e-06
        N_HEADS = 16

        def rmsnorm(x, g):
            return x * jax.lax.rsqrt(jnp.mean(x * x, axis=-1, keepdims=True) + EPS) * g
        key = jax.random.key(seed)
        ks = jax.random.split(key, 8)
        B, Tq, Tc, dq, dc, dm = (2, 256, 256, 128, 128, 128)
        query = jax.random.normal(ks[0], (B, Tq, dq), dtype=jnp.float32)
        context = jax.random.normal(ks[1], (B, Tc, dc), dtype=jnp.float32)
        context_mask = jnp.ones((B, Tc), dtype=bool)
        s = 0.02
        Wq = jax.random.normal(ks[2], (dq, dm), dtype=jnp.float32) * s
        Wk = jax.random.normal(ks[3], (dc, dm), dtype=jnp.float32) * s
        Wv = jax.random.normal(ks[4], (dc, dm), dtype=jnp.float32) * s
        Wo = jax.random.normal(ks[5], (dm, dq), dtype=jnp.float32) * s
        g_q = jnp.ones((dq,), dtype=jnp.float32)
        g_c = jnp.ones((dc,), dtype=jnp.float32)
        g_out = jnp.ones((dq,), dtype=jnp.float32)
        return dict(query=query, context=context, context_mask=context_mask, Wq=Wq, Wk=Wk, Wv=Wv, Wo=Wo, g_q=g_q, g_c=g_c, g_out=g_out)
    _L1_xattn_all = _L1_xattn_setup()
    _L1_xattn_in = {k: v for k, v in _L1_xattn_all.items() if k in ('Wq', 'Wk', 'Wv', 'Wo', 'g_q', 'g_c', 'g_out')}
    del _L1_xattn_all
    return {'x': x, 'ctx_1024': ctx_1024, 'mask_BxS2_bf1': mask_BxS2_bf1, 'L0_xattn_sa_wq': _L0_xattn_in['sa_wq'], 'L0_xattn_sa_bq': _L0_xattn_in['sa_bq'], 'L0_xattn_sa_wk': _L0_xattn_in['sa_wk'], 'L0_xattn_sa_bk': _L0_xattn_in['sa_bk'], 'L0_xattn_sa_wv': _L0_xattn_in['sa_wv'], 'L0_xattn_sa_bv': _L0_xattn_in['sa_bv'], 'L0_xattn_sa_wo': _L0_xattn_in['sa_wo'], 'L0_xattn_sa_bo': _L0_xattn_in['sa_bo'], 'L0_xattn_ca_wq': _L0_xattn_in['ca_wq'], 'L0_xattn_ca_bq': _L0_xattn_in['ca_bq'], 'L0_xattn_ca_wk': _L0_xattn_in['ca_wk'], 'L0_xattn_ca_bk': _L0_xattn_in['ca_bk'], 'L0_xattn_ca_wv': _L0_xattn_in['ca_wv'], 'L0_xattn_ca_bv': _L0_xattn_in['ca_bv'], 'L0_xattn_ca_wo': _L0_xattn_in['ca_wo'], 'L0_xattn_ca_bo': _L0_xattn_in['ca_bo'], 'L0_xattn_ln1_g': _L0_xattn_in['ln1_g'], 'L0_xattn_ln1_b': _L0_xattn_in['ln1_b'], 'L0_xattn_ln2_g': _L0_xattn_in['ln2_g'], 'L0_xattn_ln2_b': _L0_xattn_in['ln2_b'], 'L0_xattn_ln3_g': _L0_xattn_in['ln3_g'], 'L0_xattn_ln3_b': _L0_xattn_in['ln3_b'], 'L0_xattn_router_w': _L0_xattn_in['router_w'], 'L0_xattn_router_b': _L0_xattn_in['router_b'], 'L0_xattn_e_w1': _L0_xattn_in['e_w1'], 'L0_xattn_e_b1': _L0_xattn_in['e_b1'], 'L0_xattn_e_w2': _L0_xattn_in['e_w2'], 'L0_xattn_e_b2': _L0_xattn_in['e_b2'], 'L1_xattn_Wq': _L1_xattn_in['Wq'], 'L1_xattn_Wk': _L1_xattn_in['Wk'], 'L1_xattn_Wv': _L1_xattn_in['Wv'], 'L1_xattn_Wo': _L1_xattn_in['Wo'], 'L1_xattn_g_q': _L1_xattn_in['g_q'], 'L1_xattn_g_c': _L1_xattn_in['g_c'], 'L1_xattn_g_out': _L1_xattn_in['g_out']}

def reference(x, ctx_1024, mask_BxS2_bf1, L0_xattn_sa_wq, L0_xattn_sa_bq, L0_xattn_sa_wk, L0_xattn_sa_bk, L0_xattn_sa_wv, L0_xattn_sa_bv, L0_xattn_sa_wo, L0_xattn_sa_bo, L0_xattn_ca_wq, L0_xattn_ca_bq, L0_xattn_ca_wk, L0_xattn_ca_bk, L0_xattn_ca_wv, L0_xattn_ca_bv, L0_xattn_ca_wo, L0_xattn_ca_bo, L0_xattn_ln1_g, L0_xattn_ln1_b, L0_xattn_ln2_g, L0_xattn_ln2_b, L0_xattn_ln3_g, L0_xattn_ln3_b, L0_xattn_router_w, L0_xattn_router_b, L0_xattn_e_w1, L0_xattn_e_b1, L0_xattn_e_w2, L0_xattn_e_b2, L1_xattn_Wq, L1_xattn_Wk, L1_xattn_Wv, L1_xattn_Wo, L1_xattn_g_q, L1_xattn_g_c, L1_xattn_g_out):
    import jax
    import jax.numpy as jnp

    def _L0_xattn_ref(x, encoder_output, sa_wq, sa_bq, sa_wk, sa_bk, sa_wv, sa_bv, sa_wo, sa_bo, ca_wq, ca_bq, ca_wk, ca_bk, ca_wv, ca_bv, ca_wo, ca_bo, ln1_g, ln1_b, ln2_g, ln2_b, ln3_g, ln3_b, router_w, router_b, e_w1, e_b1, e_w2, e_b2):
        import jax, jax.numpy as jnp
        import numpy as np
        B, S, SE, D, H, FF, E, K = (2, 256, 256, 128, 16, 512, 8, 2)
        HD = D // H

        def _layernorm(x, g, b):
            m = x.mean(-1, keepdims=True)
            v = ((x - m) ** 2).mean(-1, keepdims=True)
            return (x - m) / jnp.sqrt(v + 1e-05) * g + b

        def _attn(q_in, k_in, v_in, wq, bq, wk, bk, wv, bv, wo, bo, causal):
            Bq, Sq, Dm = q_in.shape
            Sk = k_in.shape[1]
            Q = (q_in @ wq + bq).reshape(Bq, Sq, H, HD)
            Kp = (k_in @ wk + bk).reshape(Bq, Sk, H, HD)
            V = (v_in @ wv + bv).reshape(Bq, Sk, H, HD)
            scores = jnp.einsum('bqhd,bkhd->bhqk', Q, Kp) / jnp.sqrt(jnp.float32(HD))
            if causal:
                mask = jnp.tril(jnp.ones((Sq, Sk), bool))
                scores = jnp.where(mask, scores, -jnp.inf)
            a = jax.nn.softmax(scores, axis=-1)
            o = jnp.einsum('bhqk,bkhd->bqhd', a, V).reshape(Bq, Sq, Dm)
            return o @ wo + bo

        def _moe(x, rw, rb, w1, b1, w2, b2):
            T = x.shape[0] * x.shape[1]
            xf = x.reshape(T, D)
            router_weights = jax.nn.softmax(xf @ rw + rb, axis=-1)
            topw, topi = jax.lax.top_k(router_weights, K)
            topw = jax.nn.softmax(topw, axis=-1)
            combine = jnp.zeros((T, E), xf.dtype).at[jnp.arange(T)[:, None], topi].add(topw)
            h = jax.nn.gelu(jnp.einsum('td,edf->etf', xf, w1) + b1[:, None, :], approximate=False)
            eo = jnp.einsum('etf,efd->etd', h, w2) + b2[:, None, :]
            out = jnp.einsum('etd,te->td', eo, combine)
            return out.reshape(x.shape)
        x = _layernorm(x + _attn(x, x, x, sa_wq, sa_bq, sa_wk, sa_bk, sa_wv, sa_bv, sa_wo, sa_bo, True), ln1_g, ln1_b)
        x = _layernorm(x + _attn(x, encoder_output, encoder_output, ca_wq, ca_bq, ca_wk, ca_bk, ca_wv, ca_bv, ca_wo, ca_bo, False), ln2_g, ln2_b)
        x = _layernorm(x + _moe(x, router_w, router_b, e_w1, e_b1, e_w2, e_b2), ln3_g, ln3_b)
        return x

    def _L1_xattn_ref(query, context, context_mask, Wq, Wk, Wv, Wo, g_q, g_c, g_out):
        import jax, jax.numpy as jnp
        import numpy as np
        EPS = 1e-06
        N_HEADS = 16

        def rmsnorm(x, g):
            return x * jax.lax.rsqrt(jnp.mean(x * x, axis=-1, keepdims=True) + EPS) * g
        B, Tq, _ = query.shape
        Tc = context.shape[1]
        H = N_HEADS
        dm = Wq.shape[1]
        hd = dm // H
        scale = hd ** (-0.5)
        q_norm = rmsnorm(query, g_q)
        c_norm = rmsnorm(context, g_c)
        Q = (q_norm @ Wq).reshape(B, Tq, H, hd).transpose(0, 2, 1, 3)
        K = (c_norm @ Wk).reshape(B, Tc, H, hd).transpose(0, 2, 1, 3)
        V = (c_norm @ Wv).reshape(B, Tc, H, hd).transpose(0, 2, 1, 3)
        scores = jnp.einsum('bhqd,bhkd->bhqk', Q, K) * scale
        scores = jnp.where(context_mask[:, None, None, :], scores, -jnp.inf)
        attn = jax.nn.softmax(scores, axis=-1)
        attn = jnp.nan_to_num(attn, nan=0.0)
        out = jnp.einsum('bhqk,bhkd->bhqd', attn, V)
        out = out.transpose(0, 2, 1, 3).reshape(B, Tq, dm)
        out = out @ Wo
        return rmsnorm(query + out, g_out)
    x = _L0_xattn_ref(x, ctx_1024, L0_xattn_sa_wq, L0_xattn_sa_bq, L0_xattn_sa_wk, L0_xattn_sa_bk, L0_xattn_sa_wv, L0_xattn_sa_bv, L0_xattn_sa_wo, L0_xattn_sa_bo, L0_xattn_ca_wq, L0_xattn_ca_bq, L0_xattn_ca_wk, L0_xattn_ca_bk, L0_xattn_ca_wv, L0_xattn_ca_bv, L0_xattn_ca_wo, L0_xattn_ca_bo, L0_xattn_ln1_g, L0_xattn_ln1_b, L0_xattn_ln2_g, L0_xattn_ln2_b, L0_xattn_ln3_g, L0_xattn_ln3_b, L0_xattn_router_w, L0_xattn_router_b, L0_xattn_e_w1, L0_xattn_e_b1, L0_xattn_e_w2, L0_xattn_e_b2)
    x = _L1_xattn_ref(x, ctx_1024, mask_BxS2_bf1, L1_xattn_Wq, L1_xattn_Wk, L1_xattn_Wv, L1_xattn_Wo, L1_xattn_g_q, L1_xattn_g_c, L1_xattn_g_out)
    return x

_drawn_inputs = setup_inputs


def setup_inputs(seed=0):
    import zlib

    import numpy as np

    out = dict(_drawn_inputs(seed))
    spreads = {'L0_xattn_sa_bq': (0.0, 0.8),
     'L0_xattn_sa_bk': (0.0, 2.0),
     'L0_xattn_sa_bv': (0.0, 0.1),
     'L0_xattn_sa_bo': (0.0, 0.1),
     'L0_xattn_ca_bq': (0.0, 2.0),
     'L0_xattn_ca_bk': (0.0, 2.0),
     'L0_xattn_ca_bv': (0.0, 0.315),
     'L0_xattn_ca_bo': (0.0, 0.1),
     'L0_xattn_ln1_g': (1.0, 0.2),
     'L0_xattn_ln1_b': (0.0, 0.1),
     'L0_xattn_ln2_g': (1.0, 0.2),
     'L0_xattn_ln2_b': (0.0, 0.1),
     'L0_xattn_ln3_g': (1.0, 0.2),
     'L0_xattn_ln3_b': (0.0, 0.1),
     'L0_xattn_router_b': (0.0, 0.1),
     'L0_xattn_e_b1': (0.0, 0.514),
     'L0_xattn_e_b2': (0.0, 0.1),
     'L1_xattn_g_q': (1.0, 0.6),
     'L1_xattn_g_c': (1.0, 0.6),
     'L1_xattn_g_out': (1.0, 0.2)}
    factors = {'L0_xattn_sa_wq': 8.0,
     'L0_xattn_sa_wk': 8.0,
     'L0_xattn_sa_wv': 3.185,
     'L0_xattn_ca_wq': 8.0,
     'L0_xattn_ca_wk': 8.0,
     'L1_xattn_Wq': 8.0,
     'L1_xattn_Wk': 8.0}
    for name, (base, spread) in spreads.items():
        noise = np.random.default_rng([zlib.crc32(name.encode()), seed]).standard_normal(out[name].shape)
        drawn = base * np.exp(spread * noise) if base else spread * noise
        out[name] = jnp.asarray(drawn.astype(out[name].dtype))
    for name, factor in factors.items():
        out[name] = (out[name] * factor).astype(out[name].dtype)
    return out
```

```python
from contextlib import ExitStack

import concourse.bass as bass
import numpy as np
from concourse import mybir

F32 = mybir.dt.float32
BF16 = mybir.dt.bfloat16
U8 = mybir.dt.uint8
ALU = mybir.AluOpType
ACT = mybir.ActivationFunctionType
AX = mybir.AxisListType

B, S, D = 8, 56, 128
SK = 1500
H, HD = 16, 8
E, FF, TOPK = 8, 512, 2
TOK = B * S
TT, TP = 4, 112
KC = 12
KP = SK // KC
KB = 500
NKB = SK // KB
KW = SK + 4
HALVES = 2
U = B * HALVES
PAIRS = H // 2 // HALVES
PQ = 2 * S
UQ = PAIRS * PQ
PR = 2 * HD
QPARTS = (0, 1, 2, 0, 1, 0)
KPARTS = (0, 0, 0, 1, 1, 2)
NPROD = len(QPARTS)
MROW = NPROD * PR
VW = HD + 1
VROW = 160
SCALE = float(HD) ** -0.5
CREDIT = 1
BIG = 1e30
NEG = -1e30
TWO_ONES = float(np.array([0x3F803F80], np.uint32).view(np.float32)[0])

C_ID, C_SEL, C_HEAD, C_CAUSAL = 0, 128, 256, 272
C_LANE = C_CAUSAL + 7 * S
C_PAIR = C_LANE + 4
C_HALF = C_PAIR + 2
C_W = C_HALF + 2


def constants():
    c = np.zeros((128, C_W), np.float32)
    p = np.arange(128)
    c[:, C_ID:C_ID + 128] = np.eye(128)
    lane, row = p // 32, p % 32
    used = row < 2 * VW
    source = 32 * lane + np.where(used, VW * (row // VW), 0) + HD
    c[source, C_SEL + p] = 1.0
    c[p, C_HEAD + p // HD] = 1.0
    q = (128 * np.arange(7)[None, :] + p[:, None]) % S
    after = np.arange(S)[None, None, :] > q[:, :, None]
    c[:, C_CAUSAL:C_LANE] = np.where(after, NEG, 0.0).reshape(128, 7 * S)
    c[p, C_LANE + row // HD] = 1.0
    c[p, C_PAIR + (p // HD) % 2] = 1.0
    c[p[used], C_HALF + row[used] // VW] = 1.0
    return c


class Chain:

    def __init__(self, eng, sem, start=0):
        self.eng, self.sem, self.n = eng, sem, start

    def __call__(self, ins):
        ins.then_inc(self.sem, 1)
        self.n = self.n + 1
        self.eng.wait_ge(self.sem, self.n)


def build_program(nc, a, out):
    ctx = ExitStack()
    with ctx:
        def sb(name, shape, dt=F32):
            return ctx.enter_context(nc.sbuf_tensor(name, shape, dt))

        def sem(name):
            return ctx.enter_context(nc.semaphore(name))

        bank = [ctx.enter_context(nc.psum_tensor(f"bank{i}", [128, 512], F32)) for i in range(8)]
        ROWS, SCORES, OUT, MISC = bank[0:2], bank[2:5], bank[5], bank[6:8]

        k_scratch = [nc.dram_tensor(f"k_scratch{l}", (B, 3, 128, SK), BF16, kind="Internal").ap() for l in range(2)]
        q_scratch = [nc.dram_tensor(f"q_scratch{l}", (3, PR, B, H // 2, PQ), BF16, kind="Internal").ap()
                     for l in range(2)]
        mask_scratch = nc.dram_tensor("mask_scratch", (B, PAIRS, SK), BF16, kind="Internal").ap()

        cst = sb("cst", [128, C_W])
        identb = sb("identb", [128, 128], BF16)
        qrows = sb("qrows", [4, UQ], BF16)
        ident = cst[:, C_ID:C_ID + 128]
        sel = cst[:, C_SEL:C_SEL + 128]
        half_mask = cst[:, C_HALF:C_HALF + 2]
        pair_mask = cst[:, C_PAIR:C_PAIR + 2]
        W = {n: sb("w_" + n, [128, 128]) for n in
             ("sa_wq", "sa_wk", "sa_wv", "sa_wo", "ca_wq", "ca_wk", "ca_wv", "l1_wq", "l1_wk", "l1_wv")}
        wo9 = [sb(f"wo9_{l}", [128, HALVES, 128]) for l in range(2)]
        col = {n: sb("c_" + n, [128, 1]) for n in ("sa_bq", "sa_bk", "sa_bv", "ca_bq", "ca_bk", "g_q", "g_c")}
        bv9 = sb("bv9", [128, HALVES])
        bc = {n: sb("b_" + n, [TP, 128]) for n in
              ("sa_bo", "ca_bo", "ln1_g", "ln1_b", "ln2_g", "ln2_b", "ln3_g", "ln3_b", "g_out")}
        rw = sb("rw", [128, E])
        rb = sb("rb", [TP, E])
        b1T = sb("b1T", [128, E * 4])
        b2 = sb("b2", [E, 128])

        x_res = sb("x_res", [TP, TT, 128])
        x_new = sb("x_new", [TP, TT, 128])
        xT = sb("xT", [128, TOK])
        qT = sb("qT", [128, TOK])
        kT = sb("kT", [128, TOK])
        oT9 = sb("oT9", [128, HALVES, TOK])
        oT = kT
        stats = sb("stats", [TP, TT, 6])
        mv = sb("mv", [TP, TT, 2])
        rstd = sb("rstd", [TP, TT])
        neghalf, zero, inv_d, rms_eps = (sb(n, [128, KC]) for n in ("neghalf", "zero", "inv_d", "rms_eps"))

        krep = sb("krep", [128, 4, PAIRS, KW], BF16)
        Q = sb("Q", [100, U, UQ], BF16)
        qfix = sb("qfix", [100, 4, UQ], BF16)
        ctx_tile = sb("ctx_tile", [KP, 2, KC, 128])
        ctxT = sb("ctxT", [128, 2, SK])
        kparts = sb("kparts", [128, 2, 3, SK], BF16)
        k_rest = sb("k_rest", [128, SK])
        v9 = sb("v9", [KP, 2, KC, VROW])
        P = sb("P", [KP, 4, UQ])
        mx = sb("mx", [TP, 2, PAIRS, NKB])
        mt = sb("mt", [TP, 2, PAIRS])
        row_top = sb("row_top", [TP, 2, PAIRS])
        mparts = sb("mparts", [TP, 2, PAIRS, 4], BF16)
        o_first = sb("o_first", [128, S])
        comb = sb("comb", [128, S])
        rec = sb("rec", [128, S])
        key_ss = sb("key_ss", [KP, KC])
        key_rs = sb("key_rs", [KP, KC])
        mask_col8 = sb("mask_col8", [KP, B, KC], U8)
        mask_col = sb("mask_col", [KP, B, KC])
        mask_row8 = sb("mask_row8", [B, SK], U8)
        sq = sb("sq", [KP, KC, 128])
        mask_row = sq[0:B, :, :].rearrange("p c d -> p (c d)").bitcast(BF16)[:, 0:SK]

        SCR = 7424
        scratch = sb("scratch", [128, SCR])
        qbd = scratch[:, 0:1792].rearrange("p (r h q) -> p r h q", r=2, h=H)
        sc = scratch[:, 1792:1792 + 784].rearrange("p (r t k) -> p r t k", r=2, t=7)
        pT = scratch[:, 2576:2576 + 1792].rearrange("p (r n) -> p r n", r=2)
        vb = scratch[:, 4368:4368 + 256].rearrange("p (r n) -> p r n", r=2)
        row_m = scratch[:, 4624:4638].rearrange("p (r t) -> p r t", r=2)
        row_s = scratch[:, 4640:4654].rearrange("p (r t) -> p r t", r=2)
        om = scratch[:, 4656:4656 + 4 * TOK].rearrange("p (b i q) -> p b i q", b=B, i=4)
        qsplit = scratch[:, 0:TOK]
        q_part = scratch[:, 512:512 + 3 * TOK // 2].bitcast(BF16).rearrange("p (r n) -> p r n", r=3)
        q_wide = scratch[:, 1536:1536 + 3 * TOK].bitcast(BF16).rearrange("p (r b h q) -> p r b h q", r=3, b=B, h=2)
        w1 = scratch[:, 0:1024].rearrange("p (r f) -> p r f", r=2)
        w2 = scratch[:, 1024:2048].rearrange("p (r f n) -> p r f n", r=2, f=4)
        gate_bc = scratch[:, 2048:2048 + E * TOK].rearrange("p (e n) -> p e n", e=E)
        hid = scratch[:, 5632:5632 + 4 * TOK].rearrange("p (r n) -> p r n", r=4)
        yT = qT
        gateT = kT[0:E, :]
        v_all = P[0:S, :, :].rearrange("p c n -> p (c n)")[:, 0:B * 128].rearrange("p (b d) -> p b d", b=B)
        WT = 7 * S + 128 - S
        weights = sb("weights", [128, 2, WT])
        logit = sb("logit", [TP, TT, E])
        prob = sb("prob", [TP, TT, E])
        one1 = sb("one1", [TP, TT, E])
        one2 = sb("one2", [TP, TT, E])
        gtmp = sb("gtmp", [TP, TT, E])
        order = sb("order", [TP, TT, E])
        g1 = sb("g1", [TP, 8, TT])

        def wide(ap, n, at):
            shape = list(ap.shape)
            shape.insert(at, n)
            return ap.unsqueeze(at).to_broadcast(shape)

        names = ("in_cst", "in_x", "in_sa", "in_pipe", "in_tail", "in_mask", "in_wo", "identb_ok", "zeros_ok",
                 "pool_c", "dve_c", "act_c", "xT_ps", "xT_ok", "sa_proj", "qT_ok", "kT_ok", "v_ok", "qbd_ok",
                 "s_ps", "s_max", "s_exp", "s_norm", "vb_ok", "pt_ps", "pt_ok", "sa_o", "sa_om",
                 "oT_ok", "y_ps", "r_ok", "var_ok", "rstd_ok", "x_ok", "q_ps", "q_parts", "q_written", "q_first",
                 "q_rest", "q_rows", "wg_ok", "mask_ok", "mask_written", "krow_ok",
                 "rt_ps", "rt_ok", "rt_exp", "gate_ok", "gT_ps", "gT_ok", "gb_ps", "gb_ok", "w_in0", "w_in1", "h_ps",
                 "h_act", "h_ok", "y_part", "yT_ps", "yT_ok", "yt_ps", "out_done", "pre_ok", "sum_ok", "row_m_ok", "vb_zero")
        s = {n: sem(n) for n in names}
        layer_names = ("ctx_in0", "ctx_in1", "kw0", "kw1", "krep0", "krep1", "krep2", "krep3", "t_ps", "t_ok",
                       "k_ps", "k_high", "k_res", "k_mid", "k_low", "v_ps", "v_ok", "m_ps", "m_ok", "bc_ps",
                       "bc_ok", "row_ps", "row_max", "top_ok", "st_ps", "exp_ok", "pv_ok", "comb_ok", "fin_ok", "m_parts",
                       "qfix_ok", "sq_ok", "ss_ok", "ctx_ok", "pool_m", "pool_n", "dve_o")
        L = [{n: sem(f"l{l}_{n}") for n in layer_names} for l in range(2)]

        CREDITS = {"pe": (("s_ps", "sa_o", "pt_ps"), ("st_ps", "pv_ok", "m_ps")),
                   "act": (("pt_ok",), ()),
                   "dve": (("s_max", "sa_om"), ("comb_ok", "bc_ok")),
                   "pool": ((), ("fin_ok",))}

        def give_credits(eng, name):
            phase, layer = CREDITS[name]
            for n in phase:
                eng.sem_inc(s[n], CREDIT)
            for z in L:
                for n in layer:
                    eng.sem_inc(z[n], CREDIT)

        block = ctx.enter_context(nc.Block())

        STEP_ITEMS = [
            {0: [("T", 2, 0)], 1: [("T", 2, 1)], 2: [("T", 2, 2)], 4: [("K", 2, 0)], 5: [("M", 1)],
             6: [("K", 2, 1)], 7: [("K", 2, 2)]},
            {1: [("V", 1, 0)], 2: [("D", -1)], 4: [("M", 1)], 6: [("V", 1, 1)], 9: [("V", 1, 2)]},
            {0: [("T", 3, 0)], 1: [("T", 3, 1)], 2: [("T", 3, 2)], 3: [("D", -1)], 4: [("K", 3, 0)],
             5: [("M", 1)], 6: [("K", 3, 1)], 7: [("K", 3, 2)]},
            {1: [("V", 2, 0)], 2: [("D", -1)], 4: [("M", 1)], 6: [("V", 2, 1)], 9: [("V", 2, 2)],
             13: [("D", 0)]},
        ]

        def active(item, last):
            kind, n = item[0], item[1]
            if not last:
                return True
            if kind in "TK":
                return False
            return not (kind == "V" and n == 2)

        def items_of(j, last, s_):
            got = {}
            for slot, items in STEP_ITEMS[s_].items():
                for it in items:
                    if not active(it, last) or (it[0] == "M" and last and s_ == 3):
                        continue
                    n = (2 * j + it[1]) if it[0] in "TKV" else (4 * j + s_ + it[1])
                    par = it[1] % 2 if it[0] in "TKV" else (s_ + it[1]) % 4
                    got.setdefault(slot, []).append((it[0], n, it[2] if len(it) > 2 else 0, par))
            return got

        PROLOGUE = ([("T", 0, i, 0) for i in range(3)] + [("K", 0, i, 0) for i in range(3)]
                    + [("T", 1, i, 1) for i in range(3)] + [("K", 1, i, 1) for i in range(3)]
                    + [("V", 0, 0, 0), ("M", 0, 0, 0), ("V", 0, 1, 0), ("V", 0, 2, 0)])

        def full_order(j, last):
            order_ = []
            for s_ in range(4):
                got = items_of(j, last, s_)
                for slot in sorted(got):
                    order_ += got[slot]
            return order_

        def consumed(l, item):
            kind, n, i, _ = item
            if kind in "TKV":
                return L[l][{"T": "t_ok", "K": "k_res", "V": "v_ok"}[kind]], 3 * n + i + 1
            return (L[l]["m_ok"], n + 1) if kind == "M" else (L[l]["bc_ok"], n + 1 + CREDIT)

        def filled(l, item):
            kind, n, i, _ = item
            if kind in "TKV":
                return L[l][{"T": "t_ps", "K": "k_ps", "V": "v_ps"}[kind]], 3 * n + i + 1
            return (L[l]["m_ps"], n + 1 + CREDIT) if kind == "M" else (L[l]["bc_ps"], n + 1)

        def passes(eng, body, looped):
            with eng.Fori(0, looped) as j:
                body(j, True, False)
            for j in range(looped, 3):
                body(j, False, False)
            body(3, False, True)

        KR = [MROW, MROW + 4]
        KS = [MROW + 3, MROW + 4]

        def pe_item(pe, l, item, index, before):
            kind, n, i, par = item
            ps = MISC[index % 2]
            z = L[l]
            if before is not None:
                pe.wait_ge(*consumed(l, before))
            if kind == "T":
                if i == 0:
                    if l == 0:
                        pe.wait_ge(z[f"ctx_in{par}"], 16 * (n // 2 + 1) if isinstance(n, int) else (n - par) * 8 + 16)
                    else:
                        pe.wait_ge(z["ctx_ok"], n + 1)
                for k in range(4):
                    ins = nc.tensor.transpose(ps[:, k * KP:(k + 1) * KP], ctx_tile[:, par, 4 * i + k, :],
                                              cst[0:KP, C_ID:C_ID + KP])
                ins.then_inc(z["t_ps"], 1)
            if kind == "K":
                pe.wait_ge(z["t_ok"], 3 * n + i + 1)
                w = W["ca_wk"] if l == 0 else W["l1_wk"]
                nc.tensor.matmul(ps[:, 0:KB], w[:, :], ctxT[:, par, i * KB:(i + 1) * KB],
                                 start=True, stop=True).then_inc(z["k_ps"], 1)
            if kind == "V":
                w = W["ca_wv"] if l == 0 else W["l1_wv"]
                for k in range(4):
                    c = 4 * i + k
                    ins = nc.tensor.matmul(ps[0:KP, k * 128:(k + 1) * 128], ctxT[:, par, c * KP:(c + 1) * KP],
                                           w[:, :], start=True, stop=True)
                ins.then_inc(z["v_ps"], 1)
            if kind == "M":
                pe.wait_ge(z["m_parts"], n + 1)
                for p in range(PAIRS):
                    ins = nc.tensor.matmul(ps[96:100, p * PQ:(p + 1) * PQ], mparts[:, par % 2, p, :],
                                           identb[0:TP, 0:TP], start=True, stop=True)
                ins.then_inc(z["m_ps"], 1)
            if kind == "D":
                pe.wait_ge(z["comb_ok"], n + 1 + CREDIT)
                nc.tensor.matmul(ps[:, 0:S], sel, comb[:, :], start=True, stop=True).then_inc(z["bc_ps"], 1)

        def pe_row(pe, l, v, slot, c, first=False):
            z = L[l]
            if c == 0:
                gen = v // 4 + 1 if isinstance(v, int) else None
                pe.wait_ge(z[f"krep{slot}"], KREP_INC[l] * gen if gen is not None else
                           (v - slot) * (KREP_INC[l] // 4) + KREP_INC[l])
                pe.wait_ge(z["qfix_ok"], v + 1)
            if not first:
                pe.wait_ge(z["row_max"], 12 * v + c - 1)
            p, n = c // NKB, c % NKB
            nc.tensor.matmul(ROWS[c % 2][0:PQ, 0:KB], qfix[0:KR[l], slot, p * PQ:(p + 1) * PQ],
                             krep[0:KR[l], slot, p, n * KB:(n + 1) * KB], start=True, stop=True)\
                .then_inc(z["row_ps"], 1)

        def pe_st(pe, l, u, slot, c):
            z = L[l]
            if c == 0:
                pe.wait_ge(z["m_ok"], u + 1)
            if c >= 3:
                pe.wait_ge(z["exp_ok"], 12 * u + c - 2)
            for p in range(PAIRS):
                ins = nc.tensor.matmul(SCORES[c % 3][:, p * PQ:(p + 1) * PQ],
                                       krep[0:KS[l], slot, p, c * KP:c * KP + 128],
                                       qfix[0:KS[l], slot, p * PQ:(p + 1) * PQ], start=True, stop=True)
            ins.then_inc(z["st_ps"], 1)

        def pe_pv(pe, l, j, s_, c):
            z = L[l]
            u = 4 * j + s_
            if c == 0:
                pe.wait_ge(z["comb_ok"], u + CREDIT)
                if s_ % 2 == 0:
                    b = 2 * j + s_ // 2
                    pe.wait_ge(z["v_ok"], 3 * b + 3)
            pe.wait_ge(z["exp_ok"], 12 * u + c + 1)
            hf, par = s_ % 2, (s_ // 2) % 2
            for g in range(4):
                at = VW * (8 * hf + 2 * g)
                ins = nc.tensor.matmul(OUT[32 * g:32 * g + 32, 0:PQ], v9[:, par, c, at:at + 32],
                                       P[:, c % 4, g * PQ:(g + 1) * PQ], start=(c == 0), stop=(c == KC - 1))
            ins.then_inc(z["pv_ok"], 1)

        def pe_prepare(pe, l):
            for k, item in enumerate(PROLOGUE[:13]):
                pe_item(pe, l, item, k, PROLOGUE[k - 2] if k >= 2 else None)

        def pe_attend(pe, l):
            pe.wait_ge(s["identb_ok"], 11)
            for v in range(2):
                for c in range(12):
                    pe_row(pe, l, v, v, c, first=(v == 0 and c < 2))
            for k in range(13, 16):
                pe_item(pe, l, PROLOGUE[k], k, PROLOGUE[k - 2])

            def body(j, looped, last):
                before = [("V", 2 * j, 2, 0), ("D", 4 * j - 1, 0, 3)]
                order_ = before + full_order(j, last)
                k = 0
                for s_ in range(4):
                    got = items_of(j, last, s_)
                    u = 4 * j + s_
                    for slot in range(14):
                        if slot < 12 and (not last or s_ < 2):
                            pe_row(pe, l, u + 2, (s_ + 2) % 4, slot)
                        if slot < 12:
                            for item in got.get(slot, []):
                                pe_item(pe, l, item, k, order_[k])
                                k += 1
                            pe_st(pe, l, u, s_, slot)
                        if slot >= 2:
                            pe_pv(pe, l, j, s_, slot - 2)
                    for item in got.get(13, []):
                        pe_item(pe, l, item, k, order_[k])
                        k += 1
                assert last or k == 26

            passes(pe, body, 3)

        def act_item(act, l, item, index):
            kind, n, i, par = item
            ps = MISC[index % 2]
            z = L[l]
            act.wait_ge(*filled(l, item))
            if kind == "T":
                nc.scalar.copy(ctxT[:, par, i * KB:(i + 1) * KB], ps[:, 0:KB]).then_inc(z["t_ok"], 1)
            if kind == "K":
                if i == 0 and not (isinstance(n, int) and n < 2):
                    act.wait_ge(z[f"kw{par}"], 16 * (n // 2) if isinstance(n, int) else (n - par) * 8)
                hi = kparts[:, par, 0, i * KB:(i + 1) * KB]
                if l == 0:
                    nc.scalar.activation(hi, ps[:, 0:KB], ACT.Identity, bias=col["ca_bk"][:, 0:1])\
                        .then_inc(z["k_high"], 1)
                else:
                    nc.scalar.copy(hi, ps[:, 0:KB]).then_inc(z["k_high"], 1)
            if kind == "V":
                if i == 0 and not (isinstance(n, int) and n < 2):
                    act.wait_ge(z["pv_ok"], 24 * n - 24 + CREDIT)
                nc.scalar.copy(
                    v9[:, par, 4 * i:4 * i + 4, 0:H * VW].rearrange("p c (h w) -> p c h w", w=VW)[:, :, :, 0:HD],
                    ps[0:KP, :].rearrange("p (c h d) -> p c h d", c=4, d=HD)).then_inc(z["v_ok"], 1)
            if kind == "M":
                nc.scalar.copy(qfix[96:100, par, :], ps[96:100, 0:UQ])\
                    .then_inc(z["m_ok"], 1)

        def act_mid(act, l, n, i, par):
            z = L[l]
            act.wait_ge(z["k_res"], 3 * n + i + 1)
            nc.scalar.copy(kparts[:, par, 1, i * KB:(i + 1) * KB], k_rest[:, i * KB:(i + 1) * KB])\
                .then_inc(z["k_mid"], 1)

        def act_prepare(act, l):
            act.wait_ge(s["in_pipe"], 16 * 5)
            for k, item in enumerate(PROLOGUE[:13]):
                act_item(act, l, item, k)
                if item[0] == "K":
                    act_mid(act, l, item[1], item[2], item[3])

        def act_attend(act, l):
            z = L[l]
            for k in range(13, 16):
                act_item(act, l, PROLOGUE[k], k)

            def body(j, looped, last):
                k = 0
                for s_ in range(4):
                    got = items_of(j, last, s_)
                    u = 4 * j + s_
                    mids = {6: (4, 0), 8: (6, 1), 9: (7, 2)}
                    for slot in range(12):
                        act.wait_ge(z["st_ps"], 12 * u + slot + 1 + CREDIT)
                        if slot >= 4:
                            act.wait_ge(z["pv_ok"], 12 * u + slot - 3 + CREDIT)
                        nc.scalar.activation(P[:, slot % 4, :], SCORES[slot % 3][0:KP, 0:UQ], ACT.Exp,
                                             scale=SCALE).then_inc(z["exp_ok"], 1)
                        for item in got.get(slot, []):
                            if item[0] != "D":
                                act_item(act, l, item, k)
                            k += 1
                        if s_ in (0, 2) and not last and slot in mids:
                            b = 2 * j + 2 + s_ // 2
                            act_mid(act, l, b, mids[slot][1], (s_ // 2) % 2)
                    k += len(got.get(13, []))

            passes(act, body, 3)

        def dve_res(dve, l, n, i, par, index):
            z = L[l]
            dve.wait_ge(z["k_high"], 3 * n + i + 1)
            if not (isinstance(n, int) and n == 0):
                dve.wait_ge(z["k_low"], 3 * n + i - 2)
            hi = kparts[:, par, 0, i * KB:(i + 1) * KB]
            dst = k_rest[:, i * KB:(i + 1) * KB]
            ps = MISC[index % 2][:, 0:KB]
            if l == 0:
                nc.vector.scalar_tensor_tensor(out=dst, in0=ps, scalar=col["ca_bk"][:, 0:1], in1=hi,
                                               op0=ALU.add, op1=ALU.subtract).then_inc(z["k_res"], 1)
            else:
                nc.vector.tensor_tensor(dst, ps, hi, ALU.subtract).then_inc(z["k_res"], 1)

        def dve_qfix(dve, l, v, slot, rest):
            z = L[l]
            if rest:
                if slot != 3:
                    dve.wait_ge(s["q_rest"], 96 * (l + 1))
                dve.wait_ge(z["st_ps"], 12 * v - 36 + CREDIT)
            nc.vector.tensor_copy(qfix[:, slot, :], Q[:, v, :] if isinstance(v, int) else
                                  Q[:, bass.ds(v, 1), :].rearrange("p o n -> p (o n)")).then_inc(z["qfix_ok"], 1)

        def dve_row(dve, l, v, par, c):
            z = L[l]
            dve.wait_ge(z["row_ps"], 12 * v + c + 1)
            if c == 0 and not (isinstance(v, int) and v < 2):
                dve.wait_ge(z["m_parts"], v - 1)
            nc.vector.tensor_reduce(mx[:, par, c // NKB, c % NKB:c % NKB + 1], ROWS[c % 2][0:PQ, 0:KB],
                                    AX.X, ALU.max).then_inc(z["row_max"], 1)
            if c == 11:
                dve.wait_ge(z["row_max"], 12 * v + 12)
                nc.vector.tensor_reduce(row_top[:, par, :], mx[:, par, :, :], AX.X, ALU.max).then_inc(z["top_ok"], 1)

        def dve_comb(dve, l, v):
            z = L[l]
            dve.wait_ge(z["pv_ok"], 12 * v + 12 + CREDIT)
            nc.vector.tensor_scalar(o_first[:, :], OUT[:, 0:S], half_mask[:, 0:1], None, ALU.mult)\
                .then_inc(z["dve_o"], 1)
            dve.wait_ge(z["dve_o"], v + 1)
            dve.wait_ge(z["fin_ok"], v + CREDIT)
            nc.vector.scalar_tensor_tensor(out=comb[:, :], in0=OUT[:, S:PQ], scalar=half_mask[:, 1:2],
                                           in1=o_first[:, :], op0=ALU.mult, op1=ALU.add)\
                .then_inc(z["comb_ok"], 1)

        def dve_recip(dve, l, v, index):
            z = L[l]
            dve.wait_ge(z["bc_ps"], v + 1)
            nc.vector.reciprocal(rec[:, :], MISC[index % 2][:, 0:S]).then_inc(z["bc_ok"], 1)

        def dve_ss(dve, l, n):
            z = L[l]
            dve.wait_ge(z["sq_ok"], n + 1)
            nc.vector.tensor_reduce(key_ss[:, :], sq[:, :, :], AX.X, ALU.add).then_inc(z["ss_ok"], 1)

        def dve_prepare(dve, l):
            if l == 1:
                dve.wait_ge(L[0]["k_low"], 3 * B)
                dve_ss(dve, l, 0)
                dve_ss(dve, l, 1)
            for k, item in enumerate(PROLOGUE[:13]):
                if item[0] == "K":
                    dve_res(dve, l, item[1], item[2], item[3], k)
            if l == 1:
                dve_ss(dve, l, 2)

        def dve_attend(dve, l):
            dve.wait_ge(s["q_first"], 96 * (l + 1))
            for v in range(3):
                dve_qfix(dve, l, v, v, False)
            for v in range(2):
                for c in range(12):
                    dve_row(dve, l, v, v, c)

            def body(j, looped, last):
                k = 0
                for s_ in range(4):
                    got = items_of(j, last, s_)
                    u = 4 * j + s_
                    if s_ >= 1:
                        dve_comb(dve, l, u - 1)
                    late = {}
                    for slot in range(13):
                        if slot < 12 and (not last or s_ < 2):
                            dve_row(dve, l, u + 2, s_ % 2, slot)
                        for kind, n, i, par, index in late.get(slot, []):
                            if kind == "K":
                                dve_res(dve, l, n, i, par, index)
                            if kind == "D":
                                dve_recip(dve, l, n, index)
                        for item in got.get(slot, []):
                            if item[0] in "KD":
                                late.setdefault(slot + 1, []).append((*item, k))
                            k += 1
                        if slot == 5 and (not last or s_ == 0):
                            dve_qfix(dve, l, u + 3, (s_ + 3) % 4, True)
                        if slot == 9 and l == 1:
                            if s_ == 1 and not last:
                                dve_ss(dve, l, 2 * j + 3)
                            if s_ == 3 and (looped and not last):
                                dve_ss(dve, l, 2 * j + 4)
                    if s_ == 3:
                        dve_comb(dve, l, u)
                        dve_recip(dve, l, u, k)
                        k += 1

            passes(dve, body, 2)

        POOL_M = 4

        def pool_mparts(pool, l, v, par):
            z = L[l]
            link = Chain(pool, z["pool_m"], POOL_M * v)
            pool.wait_ge(z["top_ok"], v + 1)
            if not (isinstance(v, int) and v < 2):
                pool.wait_ge(z["m_ps"], v - 1 + CREDIT)
            neg, rest = mt[:, 0, :], mt[:, 1, :]
            part = [mparts[:, par, :, i] for i in range(3)]
            link(nc.gpsimd.tensor_tensor(neg, zero[0:TP, 0:PAIRS], row_top[:, par, :], ALU.subtract))
            link(nc.gpsimd.tensor_tensor(part[0], zero[0:TP, 0:PAIRS], row_top[:, par, :], ALU.subtract))
            link(nc.gpsimd.tensor_tensor(rest, neg, part[0], ALU.subtract))
            link(nc.gpsimd.tensor_tensor(part[1], rest, zero[0:TP, 0:PAIRS], ALU.add))
            nc.gpsimd.tensor_tensor(part[2], rest, part[1], ALU.subtract).then_inc(z["m_parts"], 1)

        def pool_low(pool, l, n, i, par):
            z = L[l]
            pool.wait_ge(z["k_mid"], 3 * n + i + 1)
            cols = slice(i * KB, (i + 1) * KB)
            nc.gpsimd.tensor_tensor(kparts[:, par, 2, cols], k_rest[:, cols], kparts[:, par, 1, cols],
                                    ALU.subtract).then_inc(z["k_low"], 1)

        def pool_fin(pool, l, v, hf):
            z = L[l]
            pool.wait_ge(z["bc_ok"], v + 1 + CREDIT)
            if isinstance(v, int):
                dst = oT9[:, hf, (v // 2) * S:(v // 2 + 1) * S]
            else:
                dst = oT9[:, hf, bass.ds((v - hf) * (S // 2), S)]
            nc.gpsimd.tensor_tensor(dst, comb[:, :], rec[:, :], ALU.mult).then_inc(z["fin_ok"], 1)

        POOL_N = 4

        def pool_norm(pool, l, n, par):
            z = L[l]
            link = Chain(pool, z["pool_n"], POOL_N * n)
            tile = ctx_tile[:, par, :, :]
            pool.wait_ge(z[f"ctx_in{par}"], 16 * (n // 2 + 1) if isinstance(n, int) else (n - par) * 8 + 16)
            nc.gpsimd.tensor_tensor(sq[:, :, :], tile, tile, ALU.mult).then_inc(z["sq_ok"], 1)
            pool.wait_ge(z["ss_ok"], n + 1)
            link(nc.gpsimd.tensor_tensor(key_rs[:, :], key_ss[:, :], inv_d[0:KP, :], ALU.mult))
            link(nc.gpsimd.tensor_tensor(key_rs[:, :], key_rs[:, :], rms_eps[0:KP, :], ALU.add))
            link(nc.gpsimd.tensor_tensor(key_rs[:, :], key_rs[:, :], neghalf[0:KP, :], ALU.pow))
            mask = mask_col[:, n, :] if isinstance(n, int) else \
                mask_col[:, bass.ds(n, 1), :].rearrange("p o c -> p (o c)")
            link(nc.gpsimd.tensor_tensor(key_rs[:, :], key_rs[:, :], mask, ALU.mult))
            nc.gpsimd.tensor_tensor(tile, tile, wide(key_rs[:, :], 128, 2), ALU.mult).then_inc(z["ctx_ok"], 1)

        def pool_prepare(pool, l):
            if l == 1:
                pool.wait_ge(s["identb_ok"], 11)
                pool_norm(pool, l, 0, 0)
                pool_norm(pool, l, 1, 1)
            for item in PROLOGUE[:13]:
                if item[0] == "K":
                    pool_low(pool, l, item[1], item[2], item[3])
            if l == 1:
                pool_norm(pool, l, 2, 0)

        def pool_attend(pool, l):
            pool_mparts(pool, l, 0, 0)

            def body(j, looped, last):
                for s_ in range(4):
                    u = 4 * j + s_
                    if not (last and s_ == 3):
                        pool_mparts(pool, l, u + 1, (s_ + 1) % 2)
                    if s_ >= 1:
                        pool_fin(pool, l, u - 1, (s_ - 1) % 2)
                    if s_ in (0, 2) and not last:
                        for i in range(3):
                            pool_low(pool, l, 2 * j + 2 + s_ // 2, i, (s_ // 2) % 2)
                    if l == 1 and s_ == 1 and not last:
                        pool_norm(pool, l, 2 * j + 3, 1)
                    if l == 1 and s_ == 3 and looped and not last:
                        pool_norm(pool, l, 2 * j + 4, 0)
                pool_fin(pool, l, 4 * j + 3, 1)

            passes(pool, body, 2)

        KREP_INC = [16 * NPROD, 16 * (NPROD + 1)]

        def sp_ctx(sp, l, n, par):
            z = L[l]
            src = a["ctx_1024"][n] if isinstance(n, int) else \
                a["ctx_1024"][bass.ds(n, 1)].rearrange("o k d -> (o k) d")
            sp.dma_start(ctx_tile[:, par, :, :], src.rearrange("(p c) d -> p c d", c=KC)).then_inc(z[f"ctx_in{par}"], 16)

        def k_dram(l, n):
            return k_scratch[l][n] if isinstance(n, int) else \
                k_scratch[l][bass.ds(n, 1)].rearrange("o r p n -> (o r) p n")

        def sp_kwrite(sp, l, n, par):
            z = L[l]
            sp.wait_ge(z["k_low"], 3 * n + 3)
            sp.dma_start(k_dram(l, n).rearrange("r p n -> p r n"), kparts[:, par, :, :]).then_inc(z[f"kw{par}"], 16)

        def sp_krep(sp, l, v, slot, n, par):
            z = L[l]
            hf = slot % 2
            sp.wait_ge(z[f"kw{par}"], 16 * (n // 2 + 1) if isinstance(n, int) else (n - par) * 8 + 16)
            if not (isinstance(v, int) and v < 4):
                sp.wait_ge(z["st_ps"], 12 * v - 36 + CREDIT)
            src = k_dram(l, n)
            for r in range(NPROD):
                sp.dma_start(krep[PR * r:PR * (r + 1), slot, :, 0:SK],
                             src[KPARTS[r], 64 * hf:64 * hf + 64, :].rearrange("(a x) n -> x a n", x=PR))\
                    .then_inc(z[f"krep{slot}"], 16)
            if l == 1:
                m = mask_scratch[n:n + 1] if isinstance(n, int) else mask_scratch[bass.ds(n, 1)]
                sp.dma_start(krep[MROW + 3:MROW + 4, slot, :, 0:SK], m).then_inc(z[f"krep{slot}"], 16)

        def sp_prepare(sp, l):
            z = L[l]
            sp_ctx(sp, l, 0, 0)
            sp_ctx(sp, l, 1, 1)
            sp.wait_ge(z["t_ps"], 3)
            sp_ctx(sp, l, 2, 0)
            if l == 1:
                sp.wait_ge(s["mask_written"], 16)
            else:
                sp.wait_ge(s["zeros_ok"], 4)
            sp_kwrite(sp, l, 0, 0)
            sp_krep(sp, l, 0, 0, 0, 0)
            sp_krep(sp, l, 1, 1, 0, 0)
            sp_kwrite(sp, l, 1, 1)
            sp_krep(sp, l, 2, 2, 1, 1)

        def sp_attend(sp, l):
            z = L[l]

            def body(j, looped, last):
                if not last:
                    sp.wait_ge(z["t_ps"], 6 * j + 6)
                    sp_ctx(sp, l, 2 * j + 3, 1)
                sp_krep(sp, l, 4 * j + 3, 3, 2 * j + 1, 1)
                if last:
                    return
                sp_kwrite(sp, l, 2 * j + 2, 0)
                sp_krep(sp, l, 4 * j + 4, 0, 2 * j + 2, 0)
                if looped:
                    sp.wait_ge(z["t_ps"], 6 * j + 9)
                    sp_ctx(sp, l, 2 * j + 4, 0)
                sp_krep(sp, l, 4 * j + 5, 1, 2 * j + 2, 0)
                sp_kwrite(sp, l, 2 * j + 3, 1)
                sp_krep(sp, l, 4 * j + 6, 2, 2 * j + 3, 1)

            passes(sp, body, 2)


        def pe_xT(pe, src, k):
            for t in range(TT):
                ins = nc.tensor.transpose(bank[0][:, t * TP:(t + 1) * TP], src[:, t, :], cst[0:TP, C_ID:C_ID + TP])
            ins.then_inc(s["xT_ps"], 1)

        def act_xT(act, k):
            act.wait_ge(s["xT_ps"], k + 1)
            nc.scalar.copy(xT[:, :], bank[0][:, 0:TOK]).then_inc(s["xT_ok"], 1)

        def layernorm(dve, link, g, b, k, dst):
            for t in range(TT):
                ins = nc.vector.bn_stats(stats[:, t, :], x_new[:, t, :])
            link(ins)
            for t in range(TT):
                ins = nc.vector.bn_aggr(mv[:, t, :], stats[:, t, :])
            ins.then_inc(s["var_ok"], 1)
            dve.wait_ge(s["rstd_ok"], k)
            for t in range(TT):
                ins = nc.vector.tensor_scalar(x_new[:, t, :], x_new[:, t, :], mv[:, t, 0:1], rstd[:, t:t + 1],
                                              ALU.subtract, ALU.mult)
            link(ins)
            link(nc.vector.tensor_tensor(x_new[:, :, :], x_new[:, :, :], wide(g[:, :], TT, 1), ALU.mult))
            nc.vector.tensor_tensor(dst[:, :, :], x_new[:, :, :], wide(b[:, :], TT, 1), ALU.add)\
                .then_inc(s["x_ok"], 1)

        def pool_rstd(pool, link, k, src, scale, eps):
            pool.wait_ge(s["var_ok"], k)
            link(nc.gpsimd.tensor_scalar(rstd[:, :], src, scale, eps, ALU.mult, ALU.add))
            nc.gpsimd.tensor_tensor(rstd[:, :], rstd[:, :], neghalf[0:TP, 0:TT], ALU.pow)\
                .then_inc(s["rstd_ok"], 1)

        def dve_qparts(dve, link, l):
            dve.wait_ge(s["q_ps"], l + 1)
            if l == 0:
                link(nc.vector.tensor_scalar(qsplit, bank[1][:, 0:TOK], col["ca_bq"][:, 0:1], None, ALU.add))
            else:
                link(nc.vector.tensor_copy(qsplit, bank[1][:, 0:TOK]))
            link(nc.vector.tensor_copy(q_part[:, 0, :], qsplit))
            link(nc.vector.tensor_tensor(qsplit, qsplit, q_part[:, 0, :], ALU.subtract))
            link(nc.vector.tensor_copy(q_part[:, 1, :], qsplit))
            link(nc.vector.tensor_tensor(q_part[:, 2, :], qsplit, q_part[:, 1, :], ALU.subtract))
            for hh in range(2):
                for r in range(3):
                    nc.vector.tensor_scalar(q_wide[:, r, :, hh, :],
                                            q_part[:, r, :].rearrange("p (b q) -> p b q", q=S),
                                            pair_mask[:, hh:hh + 1], None, ALU.mult).then_inc(s["q_parts"], 1)

        def sp_qparts(sp, l):
            sp.wait_ge(s["q_parts"], 6 * (l + 1))
            wide_q = q_wide.rearrange("p r b h q -> p r b (h q)")
            for p in range(H // 2):
                for r in range(3):
                    sp.dma_start(q_scratch[l][r, :, :, p, :], wide_q[PR * p:PR * (p + 1), r])\
                        .then_inc(s["q_written"], 16)
            sp.wait_ge(s["q_written"], 16 * 3 * (H // 2) * (l + 1))
            if l == 1:
                sp.wait_ge(L[0]["qfix_ok"], U)
            for name, lo, hi in (("q_first", 0, 2), ("q_rest", 2, B)):
                for r in range(NPROD):
                    sp.dma_start(
                        Q[PR * r:PR * (r + 1), 2 * lo:2 * hi, :].rearrange("x u n -> x (u n)"),
                        q_scratch[l][QPARTS[r], :, lo:hi].rearrange("x b p k -> x (b p k)")).then_inc(s[name], 16)

        def pe_project(pe, l, lhs, w, k):
            for t in range(TT):
                for i in range(len(lhs)):
                    ins = nc.tensor.matmul(bank[2][0:TP, t * 128:(t + 1) * 128], lhs[i][:, t * TP:(t + 1) * TP],
                                           w[i], start=(i == 0), stop=(i == len(lhs) - 1))
            ins.then_inc(s["y_ps"], 1)

        Y = bank[2][0:TP, :].rearrange("p (t d) -> p t d", t=TT)

        def sp_expert(sp, e, r):
            if isinstance(e, int):
                s1, s2 = a["L0_xattn_e_w1"][e], a["L0_xattn_e_w2"][e]
            else:
                s1 = a["L0_xattn_e_w1"][bass.ds(e, 1)].rearrange("o d f -> (o d) f")
                s2 = a["L0_xattn_e_w2"][bass.ds(e, 1)].rearrange("o f d -> (o f) d")
            sp.dma_start(w1[:, r, :], s1).then_inc(s[f"w_in{r}"], 16)
            sp.dma_start(w2[:, r, :, :], s2.rearrange("(f p) d -> p f d", p=128)).then_inc(s[f"w_in{r}"], 16)

        def sp_experts_first(sp):
            sp.wait_ge(L[0]["qfix_ok"], U)
            for e in range(2):
                sp_expert(sp, e, e)

        def sp_experts(sp):
            with sp.Fori(0, E // 2 - 1) as i:
                for r in range(2):
                    sp.wait_ge(s["y_part"], 8 * i + 4 * r + 4)
                    sp_expert(sp, 2 * i + 2 + r, r)

        @block.sync
        def _(sp):
            sp.dma_start(cst[:, :], a["consts"]).then_inc(s["in_cst"], 16)
            sp.dma_start(x_res[:, :, :], a["x"].rearrange("b q d -> (b q) d").rearrange("(t p) d -> p t d", p=TP))\
                .then_inc(s["in_x"], 16)
            for n in ("sa_wq", "sa_wk", "sa_wv", "sa_wo"):
                sp.dma_start(W[n][:, :], a["L0_xattn_" + n]).then_inc(s["in_sa"], 16)
            for n in ("sa_bq", "sa_bk", "sa_bv"):
                sp.dma_start(col[n][:, :], a["L0_xattn_" + n].rearrange("(p o) -> p o", o=1)).then_inc(s["in_sa"], 16)
            for n in ("ca_wq", "ca_wk", "ca_wv"):
                sp.dma_start(W[n][:, :], a["L0_xattn_" + n]).then_inc(s["in_pipe"], 16)
            for n in ("ca_bq", "ca_bk"):
                sp.dma_start(col[n][:, :], a["L0_xattn_" + n].rearrange("(p o) -> p o", o=1))\
                    .then_inc(s["in_pipe"], 16)
            for n in ("Wq", "Wk", "Wv"):
                sp.dma_start(W["l1_" + n.lower()][:, :], a["L1_xattn_" + n]).then_inc(s["in_tail"], 16)
            for n in ("g_q", "g_c"):
                sp.dma_start(col[n][:, :], a["L1_xattn_" + n].rearrange("(p o) -> p o", o=1))\
                    .then_inc(s["in_tail"], 16)
            sp.dma_start(mask_col8[:, :, :], a["mask_col"]).then_inc(s["in_mask"], 16)
            sp.dma_start(mask_row8[:, :], a["mask_row"]).then_inc(s["in_mask"], 16)
            for n in ("sa_bo", "ca_bo", "ln1_g", "ln1_b", "ln2_g", "ln2_b", "ln3_g", "ln3_b"):
                sp.dma_start(bc[n][:, :], a["L0_xattn_" + n].rearrange("(o d) -> o d", o=1).to_broadcast([TP, 128]))\
                    .then_inc(s["in_wo"], 16)
            sp.dma_start(bc["g_out"][:, :], a["L1_xattn_g_out"].rearrange("(o d) -> o d", o=1)
                         .to_broadcast([TP, 128])).then_inc(s["in_wo"], 16)
            for l in range(2):
                sp.dma_start(wo9[l][:, :, :], a[f"wo9_{l}"]).then_inc(s["in_wo"], 16)
            sp.dma_start(bv9[:, :], a["bv9"]).then_inc(s["in_wo"], 16)
            sp.dma_start(rw[:, :], a["L0_xattn_router_w"]).then_inc(s["in_wo"], 16)
            sp.dma_start(rb[:, :], a["L0_xattn_router_b"].rearrange("(o d) -> o d", o=1).to_broadcast([TP, E]))\
                .then_inc(s["in_wo"], 16)
            sp.dma_start(b1T[:, :], a["b1T"]).then_inc(s["in_wo"], 16)
            sp.dma_start(b2[:, :], a["L0_xattn_e_b2"]).then_inc(s["in_wo"], 16)
            sp_prepare(sp, 0)
            sp.wait_ge(s["krow_ok"], 1)
            sp.dma_start(Q[MROW:MROW + 4, :, :], wide(qrows[:, :], U, 1)).then_inc(s["q_rows"], 16)
            sp.wait_ge(s["mask_ok"], 1)
            sp.dma_start(mask_scratch, wide(mask_row, PAIRS, 1)).then_inc(s["mask_written"], 16)
            sp_qparts(sp, 0)
            sp_attend(sp, 0)

            sp.wait_ge(L[0]["st_ps"], 12 * U + CREDIT)
            sp_experts_first(sp)
            sp_prepare(sp, 1)
            sp_experts(sp)
            sp_qparts(sp, 1)
            sp_attend(sp, 1)
            sp.wait_ge(s["x_ok"], 5)
            sp.dma_start(out.rearrange("b q d -> (b q) d").rearrange("(t p) d -> p t d", p=TP), x_new[:, :, :])\
                .then_inc(s["out_done"], 16)
            sp.wait_ge(s["out_done"], 16)

        @block.tensor
        def _(pe):
            give_credits(pe, "pe")
            pe.wait_ge(s["in_cst"], 16)
            pe.wait_ge(s["in_x"], 16)
            pe_xT(pe, x_res, 0)
            pe.wait_ge(s["in_pipe"], 16 * 5)
            pe.wait_ge(s["in_sa"], 16 * 7)
            pe.wait_ge(s["xT_ok"], 1)
            nc.tensor.matmul(bank[1][:, 0:TOK], W["sa_wq"][:, :], xT[:, :], start=True, stop=True)\
                .then_inc(s["sa_proj"], 1)
            nc.tensor.matmul(bank[2][:, 0:TOK], W["sa_wk"][:, :], xT[:, :], start=True, stop=True)\
                .then_inc(s["sa_proj"], 1)
            for h in range(2):
                for i in range(4):
                    b = 4 * h + i
                    ins = nc.tensor.matmul(bank[3 + h][0:S, i * 128:(i + 1) * 128], xT[:, b * S:(b + 1) * S],
                                           W["sa_wv"][:, :], start=True, stop=True)
                ins.then_inc(s["sa_proj"], 1)
            pe_prepare(pe, 0)
            pe.wait_ge(s["kT_ok"], 1)
            pe.wait_ge(s["qT_ok"], 1)
            pe.wait_ge(s["vb_zero"], 2)
            with pe.Fori(0, B // 2) as i:
                for r in range(2):
                    pe.wait_ge(s["qbd_ok"], 2 * i + r + 1)
                    pe.wait_ge(s["s_max"], 2 * i + CREDIT)
                    for t in range(7):
                        ins = nc.tensor.matmul(
                            bank[1 + r][:, t * S:(t + 1) * S],
                            qbd[:, r].rearrange("p h q -> p (h q)")[:, t * 128:(t + 1) * 128],
                            kT[:, bass.ds((2 * i + r) * S, S)], start=True, stop=True)
                    ins.then_inc(s["s_ps"], 1)
                for r in range(2):
                    b = 2 * i + r
                    pe.wait_ge(s["s_norm"], b + 1)
                    pe.wait_ge(s["pt_ok"], 2 * b + CREDIT)
                    for h, n in enumerate((4, 3)):
                        for t in range(n):
                            at = (4 * h + t) * S
                            ins = nc.tensor.transpose(bank[3 + h][:, t * 128:(t + 1) * 128],
                                                      weights[:, r, at:at + 128], ident)
                        ins.then_inc(s["pt_ps"], 1)
                    pe.wait_ge(s["vb_ok"], b + 1)
                    pe.wait_ge(s["sa_om"], b + CREDIT)
                    pe.wait_ge(s["pt_ok"], 2 * b + 2 + CREDIT)
                    for g in range(4):
                        ins = nc.tensor.matmul(bank[5][32 * g:32 * g + 32, 0:4 * S], vb[:, r, 32 * g:32 * g + 32],
                                               pT[:, r, g * 4 * S:(g + 1) * 4 * S], start=True, stop=True)
                    ins.then_inc(s["sa_o"], 1)
            pe.wait_ge(s["oT_ok"], 1)
            pe_project(pe, 0, [oT], [W["sa_wo"][:, :]], 0)
            pe.wait_ge(s["x_ok"], 1)
            pe_xT(pe, x_res, 1)
            pe.wait_ge(s["xT_ok"], 2)
            nc.tensor.matmul(bank[1][:, 0:TOK], W["ca_wq"][:, :], xT[:, :], start=True, stop=True)\
                .then_inc(s["q_ps"], 1)
            pe.wait_ge(s["q_parts"], 1)
            pe_attend(pe, 0)
            pe.wait_ge(s["oT_ok"], 2)
            pe.wait_ge(s["in_wo"], 16 * 16)
            pe_project(pe, 0, [oT9[:, hf, :] for hf in range(HALVES)], [wo9[0][:, hf, :] for hf in range(HALVES)], 1)
            pe.wait_ge(s["x_ok"], 2)
            pe_xT(pe, x_res, 2)
            pe.wait_ge(s["xT_ok"], 3)
            for t in range(TT):
                ins = nc.tensor.matmul(bank[1][0:TP, t * E:(t + 1) * E], xT[:, t * TP:(t + 1) * TP], rw[:, :],
                                       start=True, stop=True)
            ins.then_inc(s["rt_ps"], 1)
            pe.wait_ge(s["wg_ok"], 3)
            pe_prepare(pe, 1)
            pe.wait_ge(s["gate_ok"], 1)
            for t in range(TT):
                ins = nc.tensor.transpose(bank[1][0:E, t * TP:(t + 1) * TP], logit[:, t, :],
                                          cst[0:TP, C_ID:C_ID + TP])
            ins.then_inc(s["gT_ps"], 1)
            pe.wait_ge(s["gT_ok"], 1)
            nc.tensor.matmul(bank[4][:, 0:TOK], b2[:, :], gateT, start=True, stop=False, skip_group_check=True)
            for e in range(E):
                if e >= 4:
                    pe.wait_ge(s["gb_ok"], e - 3)
                nc.tensor.matmul(bank[e % 4][:, 0:TOK], cst[0:E, C_ID + e:C_ID + e + 1].to_broadcast([E, 128]), gateT,
                                 start=True, stop=True).then_inc(s["gb_ps"], 1)
            pe.wait_ge(s["gb_ok"], E)
            with pe.Fori(0, E // 2) as i:
                def second(k):
                    v = 8 * i + k
                    pe.wait_ge(s["h_ok"], v + 1)
                    nc.tensor.matmul(bank[4][:, 0:TOK], w2[:, k // 4, k % 4, :], hid[:, k % 4, :],
                                     start=False, stop=False, skip_group_check=True).then_inc(s["y_part"], 1)

                for k in range(8):
                    v = 8 * i + k
                    if k % 4 == 0:
                        pe.wait_ge(s[f"w_in{k // 4}"], 32 * i + 32)
                    if k >= 4:
                        pe.wait_ge(s["h_act"], v - 3)
                    nc.tensor.matmul(bank[k % 4][:, 0:TOK], w1[:, k // 4, (k % 4) * 128:(k % 4 + 1) * 128],
                                     xT[:, :], start=True, stop=True).then_inc(s["h_ps"], 1)
                    if k >= 2:
                        second(k - 2)
                second(6)
                second(7)
            nc.tensor.matmul(bank[4][:, 0:TOK], ident, xT[:, :], start=False, stop=True, skip_group_check=True)\
                .then_inc(s["yT_ps"], 1)
            pe.wait_ge(s["yT_ok"], 1)
            for t in range(TT):
                ins = nc.tensor.transpose(bank[2][0:TP, t * 128:(t + 1) * 128], yT[:, t * TP:(t + 1) * TP], ident)
            ins.then_inc(s["yt_ps"], 1)
            pe.wait_ge(s["x_ok"], 4)
            pe_xT(pe, x_new, 3)
            pe.wait_ge(s["xT_ok"], 4)
            nc.tensor.matmul(bank[1][:, 0:TOK], W["l1_wq"][:, :], xT[:, :], start=True, stop=True)\
                .then_inc(s["q_ps"], 1)
            pe.wait_ge(s["q_parts"], 7)
            pe_attend(pe, 1)
            pe.wait_ge(L[1]["fin_ok"], U + CREDIT)
            pe_project(pe, 1, [oT9[:, hf, :] for hf in range(HALVES)], [wo9[1][:, hf, :] for hf in range(HALVES)], 2)

        @block.scalar
        def _(act):
            give_credits(act, "act")
            act_xT(act, 0)
            act.wait_ge(s["in_sa"], 16 * 7)
            act.wait_ge(s["sa_proj"], 1)
            nc.scalar.activation(qT[:, :], bank[1][:, 0:TOK], ACT.Identity, bias=col["sa_bq"][:, 0:1])\
                .then_inc(s["qT_ok"], 1)
            act.wait_ge(s["sa_proj"], 2)
            nc.scalar.activation(kT[:, :], bank[2][:, 0:TOK], ACT.Identity, bias=col["sa_bk"][:, 0:1])\
                .then_inc(s["kT_ok"], 1)
            for h in range(2):
                act.wait_ge(s["sa_proj"], 3 + h)
                nc.scalar.copy(v_all[:, 4 * h:4 * h + 4, :].rearrange("p b d -> p (b d)"), bank[3 + h][0:S, :])\
                    .then_inc(s["v_ok"], 1)
            act.wait_ge(s["zeros_ok"], 4)
            act_prepare(act, 0)
            act.wait_ge(s["vb_zero"], 2)
            with act.Fori(0, B // 2) as i:
                for r in range(2):
                    act.wait_ge(s["pre_ok"], 2 * i + r + 1)
                    rows = sc[:, r].rearrange("p t k -> p (t k)")
                    nc.scalar.activation(rows, rows, ACT.Exp, scale=SCALE).then_inc(s["s_exp"], 1)
                for r in range(2):
                    b = 2 * i + r
                    act.wait_ge(s["sa_o"], 2 * i + CREDIT)
                    nc.scalar.copy(vb[0:S, r, :], v_all[:, bass.ds(b, 1), :].rearrange("p o d -> p (o d)"))\
                        .then_inc(s["vb_ok"], 1)
                for r in range(2):
                    b = 2 * i + r
                    for h, n in enumerate((512, 384)):
                        act.wait_ge(s["pt_ps"], 2 * b + h + 1 + CREDIT)
                        nc.scalar.copy(pT[:, r, 512 * h:512 * h + n], bank[3 + h][:, 0:n]).then_inc(s["pt_ok"], 1)
            act_xT(act, 1)
            act_attend(act, 0)
            act_xT(act, 2)
            act.wait_ge(L[0]["kw0"], 16 * 4)
            act.wait_ge(L[0]["kw1"], 16 * 4)
            act.wait_ge(L[0]["pv_ok"], 12 * U + CREDIT)
            act_prepare(act, 1)
            act.wait_ge(s["rt_ok"], 1)
            nc.scalar.activation(prob[:, :, :], logit[:, :, :], ACT.Exp).then_inc(s["rt_exp"], 1)
            act.wait_ge(s["rt_ok"], 2)
            nc.scalar.activation(g1[:, 3, :], g1[:, 2, :], ACT.Exp).then_inc(s["rt_exp"], 1)
            act.wait_ge(s["gT_ps"], 1)
            nc.scalar.copy(gateT, bank[1][0:E, 0:TOK]).then_inc(s["gT_ok"], 1)
            for e in range(E):
                act.wait_ge(s["gb_ps"], e + 1)
                nc.scalar.copy(gate_bc[:, e, :], bank[e % 4][:, 0:TOK]).then_inc(s["gb_ok"], 1)
            with act.Fori(0, E // 2) as i:
                for k in range(8):
                    v = 8 * i + k
                    act.wait_ge(s["h_ps"], v + 1)
                    if k >= 4:
                        act.wait_ge(s["y_part"], v - 3)
                    nc.scalar.activation(hid[:, k % 4, :], bank[k % 4][:, 0:TOK], ACT.Gelu,
                                         bias=b1T[:, bass.ds(v, 1)]).then_inc(s["h_act"], 1)
            act.wait_ge(s["yT_ps"], 1)
            nc.scalar.copy(yT[:, :], bank[4][:, 0:TOK]).then_inc(s["yT_ok"], 1)
            act_xT(act, 3)
            act_attend(act, 1)

        @block.vector
        def _(dve):
            give_credits(dve, "dve")
            link = Chain(dve, s["dve_c"])
            nc.vector.memset(krep[96:128, :, :, :].rearrange("p s a n -> p (s a n)").bitcast(F32), TWO_ONES)\
                .then_inc(s["zeros_ok"], 1)
            dve.wait_ge(s["in_cst"], 16)
            nc.vector.tensor_copy(identb[:, :], ident).then_inc(s["identb_ok"], 1)
            dve.wait_ge(s["zeros_ok"], 4)
            dve.wait_ge(s["in_pipe"], 16 * 5)
            dve_prepare(dve, 0)
            with dve.Fori(0, B // 2) as i:
                for r in range(2):
                    b = 2 * i + r
                    rows = sc[:, r]
                    dve.wait_ge(s["s_ps"], b + 1 + CREDIT)
                    ps = bank[1 + r][:, 0:7 * S].rearrange("p (t k) -> p t k", k=S)
                    nc.vector.tensor_tensor(
                        rows, ps, cst[:, C_CAUSAL:C_LANE].rearrange("p (t k) -> p t k", k=S), ALU.add)\
                        .then_inc(s["s_max"], 1)
                    dve.wait_ge(s["s_max"], b + 1 + CREDIT)
                    nc.vector.tensor_reduce(row_m[:, r, :], rows, AX.X, ALU.max).then_inc(s["row_m_ok"], 1)
                    dve.wait_ge(s["row_m_ok"], b + 1)
                    nc.vector.tensor_tensor(rows, rows, wide(row_m[:, r, :], S, 2), ALU.subtract)\
                        .then_inc(s["pre_ok"], 1)
                for r in range(2):
                    b = 2 * i + r
                    rows = sc[:, r]
                    dve.wait_ge(s["s_exp"], b + 1)
                    nc.vector.tensor_reduce(row_s[:, r, :], rows, AX.X, ALU.add).then_inc(s["sum_ok"], 1)
                    dve.wait_ge(s["sum_ok"], 2 * b + 1)
                    nc.vector.reciprocal(row_m[:, r, :], row_s[:, r, :]).then_inc(s["sum_ok"], 1)
                    dve.wait_ge(s["sum_ok"], 2 * b + 2)
                    dve.wait_ge(s["pt_ps"], 4 * i + CREDIT)
                    nc.vector.tensor_tensor(weights[:, r, 0:7 * S].rearrange("p (t k) -> p t k", k=S), rows,
                                            wide(row_m[:, r, :], S, 2), ALU.mult).then_inc(s["s_norm"], 1)
                for r in range(2):
                    b = 2 * i + r
                    dve.wait_ge(s["sa_o"], b + 1 + CREDIT)
                    nc.vector.tensor_tensor(om[:, bass.ds(b, 1)].rearrange("p o i q -> p (o i) q"),
                                            bank[5][:, 0:4 * S].rearrange("p (i q) -> p i q", q=S),
                                            wide(cst[:, C_LANE:C_LANE + 4], S, 2), ALU.mult).then_inc(s["sa_om"], 1)
            dve.wait_ge(s["sa_om"], B + CREDIT)
            link(nc.vector.tensor_reduce(oT[:, :].rearrange("p (b q) -> p b q", q=S), om.rearrange("p b i q -> p b q i"),
                                         AX.X, ALU.add))
            nc.vector.tensor_scalar(oT[:, :], oT[:, :], col["sa_bv"][:, 0:1], None, ALU.add).then_inc(s["oT_ok"], 1)
            dve.wait_ge(s["in_wo"], 16 * 16)
            dve.wait_ge(s["y_ps"], 1)
            link(nc.vector.tensor_tensor(x_new[:, :, :], Y, x_res[:, :, :], ALU.add))
            link(nc.vector.tensor_tensor(x_new[:, :, :], x_new[:, :, :], wide(bc["sa_bo"][:, :], TT, 1), ALU.add))
            layernorm(dve, link, bc["ln1_g"], bc["ln1_b"], 1, x_res)
            dve_qparts(dve, link, 0)
            dve.wait_ge(s["q_rows"], 16)
            dve_attend(dve, 0)
            dve.wait_ge(L[0]["fin_ok"], U + CREDIT)
            for hf in range(HALVES):
                ins = nc.vector.tensor_scalar(oT9[:, hf, :], oT9[:, hf, :], bv9[:, hf:hf + 1], None, ALU.add)
            ins.then_inc(s["oT_ok"], 1)
            dve.wait_ge(s["y_ps"], 2)
            link(nc.vector.tensor_tensor(x_new[:, :, :], Y, x_res[:, :, :], ALU.add))
            link(nc.vector.tensor_tensor(x_new[:, :, :], x_new[:, :, :], wide(bc["ca_bo"][:, :], TT, 1), ALU.add))
            layernorm(dve, link, bc["ln2_g"], bc["ln2_b"], 2, x_res)
            dve.wait_ge(s["in_tail"], 16 * 5)
            for n, g in (("l1_wq", "g_q"), ("l1_wk", "g_c"), ("l1_wv", "g_c")):
                nc.vector.tensor_scalar(W[n][:, :], W[n][:, :], col[g][:, 0:1], None, ALU.mult)\
                    .then_inc(s["wg_ok"], 1)
            dve.wait_ge(s["identb_ok"], 11)
            dve.wait_ge(s["rt_ps"], 1)
            link(nc.vector.tensor_tensor(logit[:, :, :], bank[1][0:TP, 0:TT * E].rearrange("p (t e) -> p t e", e=E),
                                         wide(rb[:, :], TT, 1), ALU.add))
            link(nc.vector.tensor_reduce(g1[:, 0, :], logit[:, :, :], AX.X, ALU.max))
            nc.vector.tensor_tensor(logit[:, :, :], logit[:, :, :], wide(g1[:, 0, :], E, 2), ALU.subtract)\
                .then_inc(s["rt_ok"], 1)
            dve_prepare(dve, 1)
            dve.wait_ge(s["rt_exp"], 1)
            link(nc.vector.tensor_reduce(g1[:, 1, :], prob[:, :, :], AX.X, ALU.add))
            link(nc.vector.reciprocal(g1[:, 0, :], g1[:, 1, :]))
            link(nc.vector.tensor_tensor(prob[:, :, :], prob[:, :, :], wide(g1[:, 0, :], E, 2), ALU.mult))

            def first_best(one, top):
                link(nc.vector.tensor_reduce(top, prob[:, :, :], AX.X, ALU.max))
                link(nc.vector.tensor_tensor(gtmp[:, :, :], prob[:, :, :], wide(top, E, 2), ALU.is_equal))
                link(nc.vector.tensor_tensor(gtmp[:, :, :], gtmp[:, :, :], order[:, :, :], ALU.mult))
                link(nc.vector.tensor_reduce(g1[:, 7, :], gtmp[:, :, :], AX.X, ALU.max))
                link(nc.vector.tensor_tensor(one[:, :, :], order[:, :, :], wide(g1[:, 7, :], E, 2), ALU.is_equal))

            first_best(one1, g1[:, 4, :])
            link(nc.vector.scalar_tensor_tensor(out=prob[:, :, :], in0=one1[:, :, :], scalar=-2.0,
                                                in1=prob[:, :, :], op0=ALU.mult, op1=ALU.add))
            first_best(one2, g1[:, 5, :])
            nc.vector.tensor_tensor(g1[:, 2, :], g1[:, 5, :], g1[:, 4, :], ALU.subtract).then_inc(s["rt_ok"], 1)
            dve.wait_ge(s["rt_exp"], 2)
            link(nc.vector.tensor_scalar(g1[:, 0, :], g1[:, 3, :], 1.0, None, ALU.add))
            link(nc.vector.reciprocal(g1[:, 6, :], g1[:, 0, :]))
            link(nc.vector.tensor_tensor(g1[:, 1, :], g1[:, 3, :], g1[:, 6, :], ALU.mult))
            link(nc.vector.tensor_tensor(one1[:, :, :], one1[:, :, :], wide(g1[:, 6, :], E, 2), ALU.mult))
            link(nc.vector.tensor_tensor(one2[:, :, :], one2[:, :, :], wide(g1[:, 1, :], E, 2), ALU.mult))
            nc.vector.tensor_tensor(logit[:, :, :], one1[:, :, :], one2[:, :, :], ALU.add).then_inc(s["gate_ok"], 1)
            dve.wait_ge(s["gb_ok"], E)
            with dve.Fori(0, E // 2) as i:
                for k in range(8):
                    v = 8 * i + k
                    dve.wait_ge(s["h_act"], v + 1)
                    nc.vector.tensor_tensor(hid[:, k % 4, :], hid[:, k % 4, :],
                                            gate_bc[:, bass.ds(2 * i + k // 4, 1), :]
                                            .rearrange("p o n -> p (o n)"), ALU.mult).then_inc(s["h_ok"], 1)
            dve.wait_ge(s["yt_ps"], 1)
            link(nc.vector.tensor_copy(x_new[:, :, :], Y))
            layernorm(dve, link, bc["ln3_g"], bc["ln3_b"], 3, x_res)
            dve.wait_ge(s["x_ok"], 3)

            def sumsq(src):
                link(nc.vector.tensor_tensor(x_new[:, :, :], src, src, ALU.mult))
                nc.vector.tensor_reduce(mv[:, :, 1], x_new[:, :, :], AX.X, ALU.add).then_inc(s["var_ok"], 1)

            sumsq(x_res[:, :, :])
            dve.wait_ge(s["rstd_ok"], 4)
            nc.vector.tensor_tensor(x_new[:, :, :], x_res[:, :, :], wide(rstd[:, :], 128, 2), ALU.mult)\
                .then_inc(s["x_ok"], 1)
            dve_qparts(dve, link, 1)
            dve_attend(dve, 1)
            dve.wait_ge(s["y_ps"], 3)
            link(nc.vector.tensor_tensor(x_res[:, :, :], Y, x_res[:, :, :], ALU.add))
            sumsq(x_res[:, :, :])
            dve.wait_ge(s["rstd_ok"], 5)
            link(nc.vector.tensor_tensor(x_new[:, :, :], x_res[:, :, :], wide(rstd[:, :], 128, 2), ALU.mult))
            nc.vector.tensor_tensor(x_new[:, :, :], x_new[:, :, :], wide(bc["g_out"][:, :], TT, 1), ALU.mult)\
                .then_inc(s["x_ok"], 1)

        @block.gpsimd
        def _(pool):
            give_credits(pool, "pool")
            link = Chain(pool, s["pool_c"])
            nc.gpsimd.memset(krep[0:96, :, :, SK:KW], 0.0).then_inc(s["zeros_ok"], 1)
            nc.gpsimd.memset(v9[:, :, :, :], 1.0).then_inc(s["zeros_ok"], 1)
            for tile, value in ((neghalf, -0.5), (inv_d, 1.0 / D), (rms_eps, 1e-6), (zero, 0.0)):
                ins = nc.gpsimd.memset(tile[:, :], value)
            ins.then_inc(s["zeros_ok"], 1)
            nc.gpsimd.memset(mparts[:, :, :, :], 1.0).then_inc(s["identb_ok"], 1)
            for e in range(E):
                nc.gpsimd.memset(order[:, :, e], float(E - e)).then_inc(s["identb_ok"], 1)
            link(nc.gpsimd.memset(qrows[:, :], 1.0))
            nc.gpsimd.memset(qrows[0:3, :], 0.0).then_inc(s["krow_ok"], 1)
            pool.wait_ge(s["in_mask"], 32)
            nc.gpsimd.tensor_copy(mask_col[:, :, :], mask_col8[:, :, :]).then_inc(s["identb_ok"], 1)
            nc.gpsimd.tensor_scalar(mask_row, mask_row8[:, :], BIG, -BIG, ALU.mult, ALU.add).then_inc(s["mask_ok"], 1)
            nc.gpsimd.memset(vb[:, :, :], 0.0).then_inc(s["vb_zero"], 1)
            nc.gpsimd.memset(weights[:, :, 7 * S:WT], 0.0).then_inc(s["vb_zero"], 1)
            pool_prepare(pool, 0)
            pool.wait_ge(s["in_cst"], 16)
            pool.wait_ge(s["qT_ok"], 1)
            pool.wait_ge(s["v_ok"], 2)
            with pool.Fori(0, B // 2) as i:
                for r in range(2):
                    b = 2 * i + r
                    pool.wait_ge(s["s_ps"], 2 * i + CREDIT)
                    nc.gpsimd.tensor_tensor(
                        qbd[:, r], wide(qT[:, bass.ds(b * S, S)], H, 1),
                        wide(cst[:, C_HEAD:C_HEAD + H], S, 2), ALU.mult).then_inc(s["qbd_ok"], 1)
            pool_rstd(pool, link, 1, mv[:, :, 1], 1.0, 1e-5)
            pool_attend(pool, 0)
            pool_rstd(pool, link, 2, mv[:, :, 1], 1.0, 1e-5)
            pool_prepare(pool, 1)
            pool_rstd(pool, link, 3, mv[:, :, 1], 1.0, 1e-5)
            pool_rstd(pool, link, 4, mv[:, :, 1], 1.0 / D, 1e-6)
            pool_attend(pool, 1)
            pool_rstd(pool, link, 5, mv[:, :, 1], 1.0 / D, 1e-6)


_INS = ["x", "ctx_1024"] + ["L0_xattn_" + n for n in (
    "sa_wq", "sa_bq", "sa_wk", "sa_bk", "sa_wv", "sa_bv", "sa_wo", "sa_bo", "ca_wq", "ca_bq", "ca_wk", "ca_bk",
    "ca_wv", "ca_bo", "ln1_g", "ln1_b", "ln2_g", "ln2_b", "ln3_g", "ln3_b", "router_w", "router_b",
    "e_w1", "e_w2", "e_b2")] + ["L1_xattn_" + n for n in ("Wq", "Wk", "Wv", "g_q", "g_c", "g_out")]


def _rows9(w):
    out = np.zeros((128, HALVES, w.shape[1]), w.dtype)
    for h in range(H):
        hf, g, j = h // 8, (h % 8) // 2, h % 2
        at = 32 * g + VW * j
        out[at:at + HD, hf] = w[h * HD:(h + 1) * HD]
    return out


def kernel(**inputs):
    import concourse.bacc as _bacc
    from concourse.bass_utils import run_bass_kernel_spmd as _run

    v = {n: np.ascontiguousarray(inputs[n]) for n in _INS}
    mask = np.ascontiguousarray(inputs["mask_BxS2_bf1"]).view(np.uint8).reshape(B, KP, KC)
    v["mask_col"] = np.ascontiguousarray(mask.transpose(1, 0, 2))
    v["mask_row"] = np.ascontiguousarray(mask.transpose(0, 2, 1)).reshape(B, SK)
    v["wo9_0"] = _rows9(np.asarray(inputs["L0_xattn_ca_wo"] if "L0_xattn_ca_wo" in inputs else None))
    v["wo9_1"] = _rows9(np.asarray(inputs["L1_xattn_Wo"]))
    v["bv9"] = np.ascontiguousarray(_rows9(np.asarray(inputs["L0_xattn_ca_bv"]).reshape(128, 1))[:, :, 0])
    v["b1T"] = np.ascontiguousarray(np.asarray(inputs["L0_xattn_e_b1"]).reshape(E * 4, 128).T)
    v["consts"] = constants()
    nc = _bacc.Bacc("TRN2", target_bir_lowering=False, num_devices=1)
    arrays, a = {}, {}
    for name, array in v.items():
        arrays[f"in_{name}"] = array
        a[name] = nc.dram_tensor(f"in_{name}", array.shape, mybir.dt.from_np(array.dtype), kind="ExternalInput").ap()
    out = nc.dram_tensor("out_0", (B, S, D), F32, kind="ExternalOutput").ap()
    build_program(nc, a, out)
    r = _run(nc, [arrays], core_ids=[0])
    return r.results[0]["out_0"]
```

```python
from contextlib import ExitStack

import concourse.bass as bass
import numpy as np
from concourse import mybir

F32 = mybir.dt.float32
BF16 = mybir.dt.bfloat16
U8 = mybir.dt.uint8
ALU = mybir.AluOpType
ACT = mybir.ActivationFunctionType
AX = mybir.AxisListType

B, S, D = 8, 56, 128
SK = 1500
H, HD = 16, 8
E, FF, TOPK = 8, 512, 2
TOK = B * S
TT, TP = 4, 112
KC = 12
KP = SK // KC
KB = 500
NKB = SK // KB
KW = SK + 4
HALVES = 2
U = B * HALVES
PAIRS = H // 2 // HALVES
PQ = 2 * S
UQ = PAIRS * PQ
PR = 2 * HD
QPARTS = (0, 1, 2, 0, 1, 0)
KPARTS = (0, 0, 0, 1, 1, 2)
NPROD = len(QPARTS)
MROW = NPROD * PR
VW = HD + 1
VROW = 160
SCALE = float(HD) ** -0.5
CREDIT = 1
BIG = 1e30
NEG = -1e30
TWO_ONES = float(np.array([0x3F803F80], np.uint32).view(np.float32)[0])

C_ID, C_SEL, C_HEAD, C_CAUSAL = 0, 128, 256, 272
C_LANE = C_CAUSAL + 7 * S
C_PAIR = C_LANE + 4
C_HALF = C_PAIR + 2
C_W = C_HALF + 2


def constants():
    c = np.zeros((128, C_W), np.float32)
    p = np.arange(128)
    c[:, C_ID:C_ID + 128] = np.eye(128)
    lane, row = p // 32, p % 32
    used = row < 2 * VW
    source = 32 * lane + np.where(used, VW * (row // VW), 0) + HD
    c[source, C_SEL + p] = 1.0
    c[p, C_HEAD + p // HD] = 1.0
    q = (128 * np.arange(7)[None, :] + p[:, None]) % S
    after = np.arange(S)[None, None, :] > q[:, :, None]
    c[:, C_CAUSAL:C_LANE] = np.where(after, NEG, 0.0).reshape(128, 7 * S)
    c[p, C_LANE + row // HD] = 1.0
    c[p, C_PAIR + (p // HD) % 2] = 1.0
    c[p[used], C_HALF + row[used] // VW] = 1.0
    return c


class Chain:

    def __init__(self, eng, sem, start=0):
        self.eng, self.sem, self.n = eng, sem, start

    def __call__(self, ins):
        ins.then_inc(self.sem, 1)
        self.n = self.n + 1
        self.eng.wait_ge(self.sem, self.n)


def build_program(nc, a, out):
    ctx = ExitStack()
    with ctx:
        def sb(name, shape, dt=F32):
            return ctx.enter_context(nc.sbuf_tensor(name, shape, dt))

        def sem(name):
            return ctx.enter_context(nc.semaphore(name))

        bank = [ctx.enter_context(nc.psum_tensor(f"bank{i}", [128, 512], F32)) for i in range(8)]
        ROWS, SCORES, OUT, MISC = bank[0:2], bank[2:5], bank[5], bank[6:8]

        k_scratch = [nc.dram_tensor(f"k_scratch{l}", (B, 3, 128, SK), BF16, kind="Internal").ap() for l in range(2)]
        q_scratch = [nc.dram_tensor(f"q_scratch{l}", (3, 128, B * PQ), BF16, kind="Internal").ap()
                     for l in range(2)]
        mask_scratch = nc.dram_tensor("mask_scratch", (B, PAIRS, SK), BF16, kind="Internal").ap()

        cst = sb("cst", [128, C_W])
        identb = sb("identb", [128, 128], BF16)
        qrows = sb("qrows", [4, UQ], BF16)
        ident = cst[:, C_ID:C_ID + 128]
        sel = cst[:, C_SEL:C_SEL + 128]
        half_mask = cst[:, C_HALF:C_HALF + 2]
        pair_mask = cst[:, C_PAIR:C_PAIR + 2]
        W = {n: sb("w_" + n, [128, 128]) for n in
             ("sa_wq", "sa_wk", "sa_wv", "sa_wo", "ca_wq", "ca_wk", "ca_wv", "l1_wq", "l1_wk", "l1_wv")}
        wo9 = [sb(f"wo9_{l}", [128, HALVES, 128]) for l in range(2)]
        col = {n: sb("c_" + n, [128, 1]) for n in ("sa_bq", "sa_bk", "sa_bv", "ca_bq", "ca_bk", "g_q", "g_c")}
        bv9 = sb("bv9", [128, HALVES])
        bc = {n: sb("b_" + n, [TP, 128]) for n in
              ("sa_bo", "ca_bo", "ln1_g", "ln1_b", "ln2_g", "ln2_b", "ln3_g", "ln3_b", "g_out")}
        rw = sb("rw", [128, E])
        rb = sb("rb", [TP, E])
        b1T = sb("b1T", [128, E * 4])
        b2 = sb("b2", [E, 128])

        x_res = sb("x_res", [TP, TT, 128])
        x_new = sb("x_new", [TP, TT, 128])
        xT = sb("xT", [128, TOK])
        qT = sb("qT", [128, TOK])
        kT = sb("kT", [128, TOK])
        oT9 = sb("oT9", [128, HALVES, TOK])
        oT = kT
        stats = sb("stats", [TP, TT, 6])
        mv = sb("mv", [TP, TT, 2])
        rstd = sb("rstd", [TP, TT])
        neghalf, zero, inv_d, rms_eps = (sb(n, [128, KC]) for n in ("neghalf", "zero", "inv_d", "rms_eps"))

        krep = sb("krep", [128, 4, PAIRS, KW], BF16)
        Q = sb("Q", [100, H // 2, B * PQ], BF16)
        qfix = sb("qfix", [100, 4, UQ], BF16)
        ctx_tile = sb("ctx_tile", [KP, 2, KC, 128])
        ctxT = sb("ctxT", [128, 2, SK])
        kparts = sb("kparts", [128, 2, 3, SK], BF16)
        k_rest = sb("k_rest", [128, SK])
        v9 = sb("v9", [KP, 2, KC, VROW])
        P = sb("P", [KP, 4, UQ])
        mx = sb("mx", [TP, 2, PAIRS, NKB])
        mt = sb("mt", [TP, 2, PAIRS])
        row_top = sb("row_top", [TP, 2, PAIRS])
        mparts = sb("mparts", [TP, 2, PAIRS, 4], BF16)
        o_first = sb("o_first", [128, S])
        comb = sb("comb", [128, S])
        rec = sb("rec", [128, S])
        key_ss = sb("key_ss", [KP, KC])
        key_rs = sb("key_rs", [KP, KC])
        mask_col8 = sb("mask_col8", [KP, B, KC], U8)
        mask_col = sb("mask_col", [KP, B, KC])
        mask_row8 = sb("mask_row8", [B, SK], U8)
        sq = sb("sq", [KP, KC, 128])
        mask_row = sq[0:B, :, :].rearrange("p c d -> p (c d)").bitcast(BF16)[:, 0:SK]

        SCR = 7424
        scratch = sb("scratch", [128, SCR])
        qbd = scratch[:, 0:1792].rearrange("p (r h q) -> p r h q", r=2, h=H)
        sc = scratch[:, 1792:1792 + 784].rearrange("p (r t k) -> p r t k", r=2, t=7)
        pT = scratch[:, 2576:2576 + 1792].rearrange("p (r n) -> p r n", r=2)
        vb = scratch[:, 4368:4368 + 256].rearrange("p (r n) -> p r n", r=2)
        row_m = scratch[:, 4624:4638].rearrange("p (r t) -> p r t", r=2)
        kb = scratch[:, 6448:6448 + 2 * S].rearrange("p (r k) -> p r k", r=2)
        row_s = scratch[:, 4640:4654].rearrange("p (r t) -> p r t", r=2)
        om = scratch[:, 4656:4656 + 4 * TOK].rearrange("p (b i q) -> p b i q", b=B, i=4)
        qsplit = scratch[:, 0:TOK]
        q_part = scratch[:, 512:512 + 3 * TOK // 2].bitcast(BF16).rearrange("p (r n) -> p r n", r=3)
        q_wide = scratch[:, 1536:1536 + 3 * TOK].bitcast(BF16).rearrange("p (r b h q) -> p r b h q", r=3, b=B, h=2)
        w1 = scratch[:, 0:1024].rearrange("p (r f) -> p r f", r=2)
        w2 = scratch[:, 1024:2048].rearrange("p (r f n) -> p r f n", r=2, f=4)
        gate_bc = scratch[:, 2048:2048 + E * TOK].rearrange("p (e n) -> p e n", e=E)
        hid = scratch[:, 5632:5632 + 4 * TOK].rearrange("p (r n) -> p r n", r=4)
        yT = qT
        gateT = kT[0:E, :]
        v_all = P[0:S, :, :].rearrange("p c n -> p (c n)")[:, 0:B * 128].rearrange("p (b d) -> p b d", b=B)
        WT = 7 * S + 128 - S
        weights = sb("weights", [128, 2, WT])
        logit = sb("logit", [TP, TT, E])
        prob = sb("prob", [TP, TT, E])
        one1 = sb("one1", [TP, TT, E])
        one2 = sb("one2", [TP, TT, E])
        gtmp = sb("gtmp", [TP, TT, E])
        order = sb("order", [TP, TT, E])
        g1 = sb("g1", [TP, 8, TT])

        def wide(ap, n, at):
            shape = list(ap.shape)
            shape.insert(at, n)
            return ap.unsqueeze(at).to_broadcast(shape)

        names = ("in_cst", "in_x", "in_sa", "in_pipe", "in_tail", "in_mask", "in_wo", "identb_ok", "zeros_ok",
                 "pool_c", "dve_c", "act_c", "xT_ps", "xT_ok", "sa_proj", "qT_ok", "kT_ok", "v_ok", "qbd_ok",
                 "s_ps", "s_max", "s_exp", "s_norm", "vb_ok", "pt_ps", "pt_ok", "sa_o", "sa_om",
                 "oT_ok", "y_ps", "r_ok", "var_ok", "rstd_ok", "x_ok", "q_ps", "q_parts", "q_written", "q_first",
                 "q_rest", "q_rows", "wg_ok", "mask_ok", "mask_written", "krow_ok",
                 "rt_ps", "rt_ok", "rt_exp", "gate_ok", "gT_ps", "gT_ok", "gb_ps", "gb_ok", "w_in0", "w_in1", "h_ps",
                 "h_act", "h_ok", "y_part", "yT_ps", "yT_ok", "yt_ps", "out_done", "pre_ok", "sum_ok", "row_m_ok", "vb_zero")
        s = {n: sem(n) for n in names}
        layer_names = ("ctx_in0", "ctx_in1", "kw0", "kw1", "krep0", "krep1", "krep2", "krep3", "t_ps", "t_ok",
                       "k_ps", "k_high", "k_res", "k_mid", "k_low", "v_ps", "v_ok", "m_ps", "m_ok", "bc_ps",
                       "bc_ok", "row_ps", "row_max", "top_ok", "st_ps", "exp_ok", "pv_ok", "comb_ok", "fin_ok", "m_parts",
                       "qfix_ok", "sq_ok", "ss_ok", "ctx_ok", "pool_m", "pool_n", "dve_o")
        L = [{n: sem(f"l{l}_{n}") for n in layer_names} for l in range(2)]

        CREDITS = {"pe": (("s_ps", "sa_o", "pt_ps"), ("st_ps", "pv_ok", "m_ps")),
                   "act": (("pt_ok",), ()),
                   "dve": (("sa_om",), ("comb_ok", "bc_ok")),
                   "pool": ((), ("fin_ok",))}

        def give_credits(eng, name):
            phase, layer = CREDITS[name]
            for n in phase:
                eng.sem_inc(s[n], CREDIT)
            for z in L:
                for n in layer:
                    eng.sem_inc(z[n], CREDIT)

        block = ctx.enter_context(nc.Block())

        STEP_ITEMS = [
            {0: [("T", 2, 0)], 1: [("T", 2, 1)], 2: [("T", 2, 2)], 4: [("K", 2, 0)],
             6: [("K", 2, 1)], 8: [("K", 2, 2)], 10: [("M", 1)]},
            {1: [("V", 1, 0)], 3: [("D", -1)], 5: [("V", 1, 1)], 8: [("V", 1, 2)], 10: [("M", 1)]},
            {0: [("T", 3, 0)], 1: [("T", 3, 1)], 2: [("T", 3, 2)], 3: [("D", -1)], 4: [("K", 3, 0)],
             6: [("K", 3, 1)], 8: [("K", 3, 2)], 10: [("M", 1)]},
            {1: [("V", 2, 0)], 3: [("D", -1)], 5: [("V", 2, 1)], 8: [("V", 2, 2)], 10: [("M", 1)],
             13: [("D", 0)]},
        ]
        LEAD = 4

        def row_of(u, s_, slot):
            k = slot + LEAD
            v, c = u + 1 + k // 12, k % 12
            return None if isinstance(u, int) and v >= U else (v, (s_ + 1 + k // 12) % 4, c)

        def where(l, n):
            return (l + 1, n - B) if isinstance(n, int) and n >= B else (l, n)

        def items_of(l, j, s_):
            got = {}
            for slot, items in STEP_ITEMS[s_].items():
                for it in items:
                    if it[0] in "TKV":
                        layer, n = where(l, 2 * j + it[1])
                        par = it[1] % 2
                    else:
                        layer, n = l, 4 * j + s_ + it[1]
                        par = (s_ + it[1]) % 4
                    if layer > 1 or (isinstance(n, int) and n >= U):
                        continue
                    got.setdefault(slot, []).append((it[0], n, it[2] if len(it) > 2 else 0, par, layer))
            return got

        PROLOGUE = ([("T", 0, i, 0, 0) for i in range(3)] + [("K", 0, i, 0, 0) for i in range(3)]
                    + [("T", 1, i, 1, 0) for i in range(3)] + [("K", 1, i, 1, 0) for i in range(3)]
                    + [("V", 0, i, 0, 0) for i in range(3)] + [("M", 0, 0, 0, 0)])

        def full_order(l, j):
            order_ = []
            for s_ in range(4):
                got = items_of(l, j, s_)
                for slot in sorted(got):
                    order_ += got[slot]
            return order_

        def consumed(item):
            kind, n, i, _, l = item
            if kind in "TKV":
                return L[l][{"T": "t_ok", "K": "k_res", "V": "v_ok"}[kind]], 3 * n + i + 1
            return (L[l]["m_ok"], n + 1) if kind == "M" else (L[l]["bc_ok"], n + 1 + CREDIT)

        def filled(item):
            kind, n, i, _, l = item
            if kind in "TKV":
                return L[l][{"T": "t_ps", "K": "k_ps", "V": "v_ps"}[kind]], 3 * n + i + 1
            return (L[l]["m_ps"], n + 1 + CREDIT) if kind == "M" else (L[l]["bc_ps"], n + 1)

        def passes(eng, body, looped):
            with eng.Fori(0, looped) as j:
                body(j)
            for j in range(looped, 4):
                body(j)

        KR = [MROW, MROW + 4]
        KS = [MROW + 3, MROW + 4]

        def pe_item(pe, item, index, before):
            kind, n, i, par, l = item
            ps = MISC[index % 2]
            z = L[l]
            if before is not None:
                pe.wait_ge(*consumed(before))
            if kind == "T":
                if i == 0:
                    if l == 0:
                        pe.wait_ge(z[f"ctx_in{par}"], 16 * (n // 2 + 1) if isinstance(n, int) else (n - par) * 8 + 16)
                    else:
                        pe.wait_ge(z["ctx_ok"], n + 1)
                for k in range(4):
                    ins = nc.tensor.transpose(ps[:, k * KP:(k + 1) * KP], ctx_tile[:, par, 4 * i + k, :],
                                              cst[0:KP, C_ID:C_ID + KP])
                ins.then_inc(z["t_ps"], 1)
            if kind == "K":
                pe.wait_ge(z["t_ok"], 3 * n + i + 1)
                w = W["ca_wk"] if l == 0 else W["l1_wk"]
                nc.tensor.matmul(ps[:, 0:KB], w[:, :], ctxT[:, par, i * KB:(i + 1) * KB],
                                 start=True, stop=True).then_inc(z["k_ps"], 1)
            if kind == "V":
                w = W["ca_wv"] if l == 0 else W["l1_wv"]
                for k in range(4):
                    c = 4 * i + k
                    ins = nc.tensor.matmul(ps[0:KP, k * 128:(k + 1) * 128], ctxT[:, par, c * KP:(c + 1) * KP],
                                           w[:, :], start=True, stop=True)
                ins.then_inc(z["v_ps"], 1)
            if kind == "M":
                pe.wait_ge(z["m_parts"], n + 1)
                for p in range(PAIRS):
                    ins = nc.tensor.matmul(ps[96:100, p * PQ:(p + 1) * PQ], mparts[:, par % 2, p, :],
                                           identb[0:TP, 0:TP], start=True, stop=True)
                ins.then_inc(z["m_ps"], 1)
            if kind == "D":
                pe.wait_ge(z["comb_ok"], n + 1 + CREDIT)
                nc.tensor.matmul(ps[:, 0:S], sel, comb[:, :], start=True, stop=True).then_inc(z["bc_ps"], 1)

        def pe_row(pe, l, v, slot, c, first=False):
            z = L[l]
            if c == 0:
                gen = v // 4 + 1 if isinstance(v, int) else None
                pe.wait_ge(z[f"krep{slot}"], KREP_INC[l] * gen if gen is not None else
                           (v - slot) * (KREP_INC[l] // 4) + KREP_INC[l])
                pe.wait_ge(z["qfix_ok"], v + 1)
            if not first:
                pe.wait_ge(z["row_max"], 12 * v + c - 1)
            p, n = c // NKB, c % NKB
            nc.tensor.matmul(ROWS[c % 2][0:PQ, 0:KB], qfix[0:KR[l], slot, p * PQ:(p + 1) * PQ],
                             krep[0:KR[l], slot, p, n * KB:(n + 1) * KB], start=True, stop=True)\
                .then_inc(z["row_ps"], 1)

        def pe_st(pe, l, u, slot, c):
            z = L[l]
            if c == 0:
                pe.wait_ge(z["m_ok"], u + 1)
            if c >= 3:
                pe.wait_ge(z["exp_ok"], 12 * u + c - 2)
            for p in range(PAIRS):
                ins = nc.tensor.matmul(SCORES[c % 3][:, p * PQ:(p + 1) * PQ],
                                       krep[0:KS[l], slot, p, c * KP:c * KP + 128],
                                       qfix[0:KS[l], slot, p * PQ:(p + 1) * PQ], start=True, stop=True)
            ins.then_inc(z["st_ps"], 1)

        def pe_pv(pe, l, j, s_, c):
            z = L[l]
            u = 4 * j + s_
            if c == 0:
                pe.wait_ge(z["comb_ok"], u + CREDIT)
                if s_ % 2 == 0:
                    b = 2 * j + s_ // 2
                    pe.wait_ge(z["v_ok"], 3 * b + 3)
            pe.wait_ge(z["exp_ok"], 12 * u + c + 1)
            hf, par = s_ % 2, (s_ // 2) % 2
            for g in range(4):
                at = VW * (8 * hf + 2 * g)
                ins = nc.tensor.matmul(OUT[32 * g:32 * g + 32, 0:PQ], v9[:, par, c, at:at + 32],
                                       P[:, c % 4, g * PQ:(g + 1) * PQ], start=(c == 0), stop=(c == KC - 1))
            ins.then_inc(z["pv_ok"], 1)

        def pe_prepare(pe):
            for k, item in enumerate(PROLOGUE[:-1]):
                pe_item(pe, item, k, PROLOGUE[k - 2] if k >= 2 else None)

        def pe_attend(pe, l):
            pe.wait_ge(s["identb_ok"], 11)
            for k in range(12 + LEAD):
                pe_row(pe, l, k // 12, k // 12, k % 12, first=(k < 2))
            pe_item(pe, ("M", 0, 0, 0, l), 1, PROLOGUE[-3] if l == 0 else ("D", U - 1, 0, 3, 0))

            def body(j):
                last = isinstance(j, int)
                before = [("V", 2 * j, 2, 0, l), ("D", 4 * j - 1, 0, 3, l)]
                order_ = before + full_order(l, j)
                k = 0
                for s_ in range(4):
                    got = items_of(l, j, s_)
                    u = 4 * j + s_
                    for slot in range(14):
                        if slot < 12 and row_of(u, s_, slot):
                            v, v_slot, c = row_of(u, s_, slot)
                            pe_row(pe, l, v, v_slot, c)
                        if slot < 12:
                            for item in got.get(slot, []):
                                pe_item(pe, item, k, order_[k])
                                k += 1
                            pe_st(pe, l, u, s_, slot)
                        if slot >= 2:
                            pe_pv(pe, l, j, s_, slot - 2)
                    for item in got.get(13, []):
                        pe_item(pe, item, k, order_[k])
                        k += 1
                assert last or k == 26

            passes(pe, body, 3)

        def act_item(act, item, index):
            kind, n, i, par, l = item
            ps = MISC[index % 2]
            z = L[l]
            act.wait_ge(*filled(item))
            if kind == "T":
                nc.scalar.copy(ctxT[:, par, i * KB:(i + 1) * KB], ps[:, 0:KB]).then_inc(z["t_ok"], 1)
            if kind == "K":
                if i == 0 and l == 1 and isinstance(n, int) and n < 2:
                    act.wait_ge(L[0][f"kw{par}"], 16 * (B // 2))
                elif i == 0 and not (isinstance(n, int) and n < 2):
                    act.wait_ge(z[f"kw{par}"], 16 * (n // 2) if isinstance(n, int) else (n - par) * 8)
                hi = kparts[:, par, 0, i * KB:(i + 1) * KB]
                if l == 0:
                    nc.scalar.activation(hi, ps[:, 0:KB], ACT.Identity, bias=col["ca_bk"][:, 0:1])\
                        .then_inc(z["k_high"], 1)
                else:
                    nc.scalar.copy(hi, ps[:, 0:KB]).then_inc(z["k_high"], 1)
            if kind == "V":
                if i == 0 and l == 1 and isinstance(n, int) and n == 0:
                    act.wait_ge(L[0]["pv_ok"], 12 * (U - 2) + CREDIT)
                elif i == 0 and not (isinstance(n, int) and n < 2):
                    act.wait_ge(z["pv_ok"], 24 * n - 24 + CREDIT)
                nc.scalar.copy(
                    v9[:, par, 4 * i:4 * i + 4, 0:H * VW].rearrange("p c (h w) -> p c h w", w=VW)[:, :, :, 0:HD],
                    ps[0:KP, :].rearrange("p (c h d) -> p c h d", c=4, d=HD)).then_inc(z["v_ok"], 1)
            if kind == "M":
                nc.scalar.copy(qfix[96:100, par, :], ps[96:100, 0:UQ])\
                    .then_inc(z["m_ok"], 1)

        def act_mid(act, l, n, i, par):
            z = L[l]
            act.wait_ge(z["k_res"], 3 * n + i + 1)
            nc.scalar.copy(kparts[:, par, 1, i * KB:(i + 1) * KB], k_rest[:, i * KB:(i + 1) * KB])\
                .then_inc(z["k_mid"], 1)

        def act_prepare(act):
            act.wait_ge(s["in_pipe"], 16 * 5)
            for k, item in enumerate(PROLOGUE[:-1]):
                act_item(act, item, k)
                if item[0] == "K":
                    act_mid(act, 0, item[1], item[2], item[3])

        def act_attend(act, l):
            z = L[l]
            act_item(act, ("M", 0, 0, 0, l), 1)

            def body(j):
                k = 0
                for s_ in range(4):
                    got = items_of(l, j, s_)
                    u = 4 * j + s_
                    mids = {6: (4, 0), 8: (6, 1), 11: (8, 2)}
                    for slot in range(12):
                        act.wait_ge(z["st_ps"], 12 * u + slot + 1 + CREDIT)
                        if slot >= 4:
                            act.wait_ge(z["pv_ok"], 12 * u + slot - 3 + CREDIT)
                        nc.scalar.activation(P[:, slot % 4, :], SCORES[slot % 3][0:KP, 0:UQ], ACT.Exp,
                                             scale=SCALE).then_inc(z["exp_ok"], 1)
                        for item in got.get(slot, []):
                            if item[0] != "D":
                                act_item(act, item, k)
                            k += 1
                        layer, b = where(l, 2 * j + 2 + s_ // 2)
                        if s_ in (0, 2) and layer < 2 and slot in mids:
                            act_mid(act, layer, b, mids[slot][1], (s_ // 2) % 2)
                    k += len(got.get(13, []))

            passes(act, body, 3)

        def dve_res(dve, l, n, i, par, index):
            z = L[l]
            dve.wait_ge(z["k_high"], 3 * n + i + 1)
            if not (isinstance(n, int) and n == 0):
                dve.wait_ge(z["k_low"], 3 * n + i - 2)
            elif l == 1:
                dve.wait_ge(L[0]["k_low"], 3 * B + i - 2)
            hi = kparts[:, par, 0, i * KB:(i + 1) * KB]
            dst = k_rest[:, i * KB:(i + 1) * KB]
            ps = MISC[index % 2][:, 0:KB]
            if l == 0:
                nc.vector.scalar_tensor_tensor(out=dst, in0=ps, scalar=col["ca_bk"][:, 0:1], in1=hi,
                                               op0=ALU.add, op1=ALU.subtract).then_inc(z["k_res"], 1)
            else:
                nc.vector.tensor_tensor(dst, ps, hi, ALU.subtract).then_inc(z["k_res"], 1)

        def dve_qfix(dve, l, v, slot, rest):
            z = L[l]
            if rest:
                if slot != 3:
                    dve.wait_ge(s["q_rest"], 96 * (l + 1))
                dve.wait_ge(z["st_ps"], 12 * v - 36 + CREDIT)
            hf = slot % 2
            at = slice((v // 2) * PQ, (v // 2 + 1) * PQ) if isinstance(v, int) else bass.ds((v - hf) * S, PQ)
            nc.vector.tensor_copy(qfix[:, slot, :].rearrange("p (a n) -> p a n", n=PQ),
                                  Q[:, PAIRS * hf:PAIRS * (hf + 1), at]).then_inc(z["qfix_ok"], 1)

        def dve_row(dve, l, v, par, c):
            z = L[l]
            dve.wait_ge(z["row_ps"], 12 * v + c + 1)
            if c == 0 and not (isinstance(v, int) and v < 2):
                dve.wait_ge(z["m_parts"], v - 1)
            nc.vector.tensor_reduce(mx[:, par, c // NKB, c % NKB:c % NKB + 1], ROWS[c % 2][0:PQ, 0:KB],
                                    AX.X, ALU.max).then_inc(z["row_max"], 1)
            if c == 11:
                dve.wait_ge(z["row_max"], 12 * v + 12)
                nc.vector.tensor_reduce(row_top[:, par, :], mx[:, par, :, :], AX.X, ALU.max).then_inc(z["top_ok"], 1)

        def dve_comb(dve, l, v):
            z = L[l]
            dve.wait_ge(z["pv_ok"], 12 * v + 12 + CREDIT)
            nc.vector.tensor_scalar(o_first[:, :], OUT[:, 0:S], half_mask[:, 0:1], None, ALU.mult)\
                .then_inc(z["dve_o"], 1)
            dve.wait_ge(z["dve_o"], v + 1)
            dve.wait_ge(z["fin_ok"], v + CREDIT)
            nc.vector.scalar_tensor_tensor(out=comb[:, :], in0=OUT[:, S:PQ], scalar=half_mask[:, 1:2],
                                           in1=o_first[:, :], op0=ALU.mult, op1=ALU.add)\
                .then_inc(z["comb_ok"], 1)

        def dve_recip(dve, l, v, index):
            z = L[l]
            dve.wait_ge(z["bc_ps"], v + 1)
            nc.vector.reciprocal(rec[:, :], MISC[index % 2][:, 0:S]).then_inc(z["bc_ok"], 1)

        def norm_here(layer, n):
            return layer == 1 and not (isinstance(n, int) and n == 2)

        def dve_ss(dve, l, n):
            z = L[l]
            dve.wait_ge(z["sq_ok"], n + 1)
            nc.vector.tensor_reduce(key_ss[:, :], sq[:, :, :], AX.X, ALU.add).then_inc(z["ss_ok"], 1)

        def dve_prepare(dve):
            for k, item in enumerate(PROLOGUE[:-1]):
                if item[0] == "K":
                    dve_res(dve, 0, item[1], item[2], item[3], k)

        def dve_attend(dve, l):
            dve.wait_ge(s["q_first"], 96 * (l + 1))
            for v in range(3):
                dve_qfix(dve, l, v, v, False)
            for k in range(12 + LEAD):
                dve_row(dve, l, k // 12, k // 12, k % 12)

            def body(j):
                last = isinstance(j, int) and j == 3
                k = 0
                for s_ in range(4):
                    got = items_of(l, j, s_)
                    u = 4 * j + s_
                    if s_ >= 1:
                        dve_comb(dve, l, u - 1)
                    late = {}
                    for slot in range(13):
                        if slot < 12 and row_of(u, s_, slot):
                            v, v_slot, c = row_of(u, s_, slot)
                            dve_row(dve, l, v, v_slot % 2, c)
                        for kind, n, i, par, layer, index in late.get(slot, []):
                            if kind == "K":
                                dve_res(dve, layer, n, i, par, index)
                            if kind == "D":
                                dve_recip(dve, layer, n, index)
                        for item in got.get(slot, []):
                            if item[0] in "KD":
                                late.setdefault(slot + 1, []).append((*item, k))
                            k += 1
                        if slot == 5 and (not last or s_ == 0):
                            dve_qfix(dve, l, u + 3, (s_ + 3) % 4, True)
                        if slot == 10 and s_ in (0, 2):
                            layer, n = where(l, 2 * j + 3 + s_ // 2)
                            if norm_here(layer, n):
                                dve_ss(dve, layer, n)
                    if s_ == 3:
                        dve_comb(dve, l, u)
                        dve_recip(dve, l, u, k)
                        k += 1

            passes(dve, body, 2)

        POOL_M = 4

        def pool_mparts(pool, l, v, par):
            z = L[l]
            link = Chain(pool, z["pool_m"], POOL_M * v)
            pool.wait_ge(z["top_ok"], v + 1)
            if not (isinstance(v, int) and v < 2):
                pool.wait_ge(z["m_ps"], v - 1 + CREDIT)
            neg, rest = mt[:, 0, :], mt[:, 1, :]
            part = [mparts[:, par, :, i] for i in range(3)]
            link(nc.gpsimd.tensor_tensor(neg, zero[0:TP, 0:PAIRS], row_top[:, par, :], ALU.subtract))
            link(nc.gpsimd.tensor_tensor(part[0], zero[0:TP, 0:PAIRS], row_top[:, par, :], ALU.subtract))
            link(nc.gpsimd.tensor_tensor(rest, neg, part[0], ALU.subtract))
            link(nc.gpsimd.tensor_tensor(part[1], rest, zero[0:TP, 0:PAIRS], ALU.add))
            nc.gpsimd.tensor_tensor(part[2], rest, part[1], ALU.subtract).then_inc(z["m_parts"], 1)

        def pool_low(pool, l, n, i, par):
            z = L[l]
            pool.wait_ge(z["k_mid"], 3 * n + i + 1)
            cols = slice(i * KB, (i + 1) * KB)
            nc.gpsimd.tensor_tensor(kparts[:, par, 2, cols], k_rest[:, cols], kparts[:, par, 1, cols],
                                    ALU.subtract).then_inc(z["k_low"], 1)

        def pool_fin(pool, l, v, hf):
            z = L[l]
            pool.wait_ge(z["bc_ok"], v + 1 + CREDIT)
            if isinstance(v, int):
                dst = oT9[:, hf, (v // 2) * S:(v // 2 + 1) * S]
            else:
                dst = oT9[:, hf, bass.ds((v - hf) * (S // 2), S)]
            nc.gpsimd.tensor_tensor(dst, comb[:, :], rec[:, :], ALU.mult).then_inc(z["fin_ok"], 1)

        POOL_N = 4

        def pool_squares(pool, l, n, par):
            z = L[l]
            pool.wait_ge(z[f"ctx_in{par}"], 16 * (n // 2 + 1) if isinstance(n, int) else (n - par) * 8 + 16)
            tile = ctx_tile[:, par, :, :]
            nc.gpsimd.tensor_tensor(sq[:, :, :], tile, tile, ALU.mult).then_inc(z["sq_ok"], 1)

        def pool_norm(pool, l, n, par):
            z = L[l]
            link = Chain(pool, z["pool_n"], POOL_N * n)
            tile = ctx_tile[:, par, :, :]
            pool.wait_ge(z["ss_ok"], n + 1)
            link(nc.gpsimd.tensor_tensor(key_rs[:, :], key_ss[:, :], inv_d[0:KP, :], ALU.mult))
            link(nc.gpsimd.tensor_tensor(key_rs[:, :], key_rs[:, :], rms_eps[0:KP, :], ALU.add))
            link(nc.gpsimd.tensor_tensor(key_rs[:, :], key_rs[:, :], neghalf[0:KP, :], ALU.pow))
            mask = mask_col[:, n, :] if isinstance(n, int) else \
                mask_col[:, bass.ds(n, 1), :].rearrange("p o c -> p (o c)")
            link(nc.gpsimd.tensor_tensor(key_rs[:, :], key_rs[:, :], mask, ALU.mult))
            nc.gpsimd.tensor_tensor(tile, tile, wide(key_rs[:, :], 128, 2), ALU.mult).then_inc(z["ctx_ok"], 1)

        def pool_prepare(pool):
            for item in PROLOGUE[:-1]:
                if item[0] == "K":
                    pool_low(pool, 0, item[1], item[2], item[3])

        def pool_attend(pool, l):
            pool_mparts(pool, l, 0, 0)

            def body(j):
                last = isinstance(j, int) and j == 3
                for s_ in range(4):
                    u = 4 * j + s_
                    layer_n, m = where(l, 2 * j + 3 + s_ // 2)
                    if s_ in (0, 2) and norm_here(layer_n, m):
                        pool_squares(pool, layer_n, m, s_ // 2 ^ 1)
                    if s_ in (1, 3) and norm_here(layer_n, m):
                        pool_norm(pool, layer_n, m, s_ // 2 ^ 1)
                    if s_ >= 1:
                        pool_fin(pool, l, u - 1, (s_ - 1) % 2)
                    layer, n = where(l, 2 * j + 2 + s_ // 2)
                    if not (last and s_ == 3):
                        pool_mparts(pool, l, u + 1, (s_ + 1) % 2)
                    for i in range(3) if s_ in (0, 2) and layer < 2 else ():
                        pool_low(pool, layer, n, i, (s_ // 2) % 2)
                pool_fin(pool, l, 4 * j + 3, 1)

            passes(pool, body, 2)

        KREP_INC = [16 * NPROD, 16 * (NPROD + 1)]

        def sp_ctx(sp, l, n, par):
            z = L[l]
            src = a["ctx_1024"][n] if isinstance(n, int) else \
                a["ctx_1024"][bass.ds(n, 1)].rearrange("o k d -> (o k) d")
            sp.dma_start(ctx_tile[:, par, :, :], src.rearrange("(p c) d -> p c d", c=KC)).then_inc(z[f"ctx_in{par}"], 16)

        def k_dram(l, n):
            return k_scratch[l][n] if isinstance(n, int) else \
                k_scratch[l][bass.ds(n, 1)].rearrange("o r p n -> (o r) p n")

        def sp_kwrite(sp, l, n, par):
            z = L[l]
            sp.wait_ge(z["k_low"], 3 * n + 3)
            sp.dma_start(k_dram(l, n).rearrange("r p n -> p r n"), kparts[:, par, :, :]).then_inc(z[f"kw{par}"], 16)

        def sp_krep(sp, l, v, slot, n, par):
            z = L[l]
            hf = slot % 2
            sp.wait_ge(z[f"kw{par}"], 16 * (n // 2 + 1) if isinstance(n, int) else (n - par) * 8 + 16)
            if not (isinstance(v, int) and v < 4):
                sp.wait_ge(z["st_ps"], 12 * v - 36 + CREDIT)
            elif l == 1:
                sp.wait_ge(L[0]["st_ps"], 12 * (v + U) - 36 + CREDIT)
            src = k_dram(l, n)
            for r in range(NPROD):
                sp.dma_start(krep[PR * r:PR * (r + 1), slot, :, 0:SK],
                             src[KPARTS[r], 64 * hf:64 * hf + 64, :].rearrange("(a x) n -> x a n", x=PR))\
                    .then_inc(z[f"krep{slot}"], 16)
            if l == 1:
                m = mask_scratch[n:n + 1] if isinstance(n, int) else mask_scratch[bass.ds(n, 1)]
                sp.dma_start(krep[MROW + 3:MROW + 4, slot, :, 0:SK], m).then_inc(z[f"krep{slot}"], 16)

        def sp_prepare(sp):
            z = L[0]
            sp_ctx(sp, 0, 0, 0)
            sp_ctx(sp, 0, 1, 1)
            sp.wait_ge(z["t_ps"], 3)
            sp_ctx(sp, 0, 2, 0)
            sp.wait_ge(s["zeros_ok"], 4)
            sp_kwrite(sp, 0, 0, 0)
            sp_krep(sp, 0, 0, 0, 0, 0)
            sp_krep(sp, 0, 1, 1, 0, 0)
            sp.wait_ge(z["t_ps"], 6)
            sp_ctx(sp, 0, 3, 1)
            sp_kwrite(sp, 0, 1, 1)
            sp_krep(sp, 0, 2, 2, 1, 1)

        def sp_attend(sp, l):
            def context(n, par):
                layer, b = where(l, n)
                if layer < 2:
                    before, last_b = where(l, n - 2)
                    sp.wait_ge(L[before]["t_ps"], 3 * last_b + 3)
                    sp_ctx(sp, layer, b, par)

            def body(j):
                sp_krep(sp, l, 4 * j + 3, 3, 2 * j + 1, 1)
                layer, n = where(l, 2 * j + 2)
                if layer == 2:
                    return
                v = n * HALVES
                context(2 * j + 4, 0)
                sp_kwrite(sp, layer, n, 0)
                sp_krep(sp, layer, v, 0, n, 0)
                sp_krep(sp, layer, v + 1, 1, n, 0)
                context(2 * j + 5, 1)
                sp_kwrite(sp, layer, n + 1, 1)
                sp_krep(sp, layer, v + 2, 2, n + 1, 1)

            passes(sp, body, 2)


        def pe_xT(pe, src, k):
            for t in range(TT):
                ins = nc.tensor.transpose(bank[0][:, t * TP:(t + 1) * TP], src[:, t, :], cst[0:TP, C_ID:C_ID + TP])
            ins.then_inc(s["xT_ps"], 1)

        def act_xT(act, k):
            act.wait_ge(s["xT_ps"], k + 1)
            nc.scalar.copy(xT[:, :], bank[0][:, 0:TOK]).then_inc(s["xT_ok"], 1)

        def layernorm(dve, link, g, b, k, dst):
            for t in range(TT):
                ins = nc.vector.bn_stats(stats[:, t, :], x_new[:, t, :])
            link(ins)
            for t in range(TT):
                ins = nc.vector.bn_aggr(mv[:, t, :], stats[:, t, :])
            ins.then_inc(s["var_ok"], 1)
            dve.wait_ge(s["rstd_ok"], k)
            for t in range(TT):
                ins = nc.vector.tensor_scalar(x_new[:, t, :], x_new[:, t, :], mv[:, t, 0:1], rstd[:, t:t + 1],
                                              ALU.subtract, ALU.mult)
            link(ins)
            link(nc.vector.tensor_tensor(x_new[:, :, :], x_new[:, :, :], wide(g[:, :], TT, 1), ALU.mult))
            nc.vector.tensor_tensor(dst[:, :, :], x_new[:, :, :], wide(b[:, :], TT, 1), ALU.add)\
                .then_inc(s["x_ok"], 1)

        def pool_rstd(pool, link, k, src, scale, eps):
            pool.wait_ge(s["var_ok"], k)
            link(nc.gpsimd.tensor_scalar(rstd[:, :], src, scale, eps, ALU.mult, ALU.add))
            nc.gpsimd.tensor_tensor(rstd[:, :], rstd[:, :], neghalf[0:TP, 0:TT], ALU.pow)\
                .then_inc(s["rstd_ok"], 1)

        def dve_qparts(dve, link, l):
            dve.wait_ge(s["q_ps"], l + 1)
            if l == 0:
                link(nc.vector.tensor_scalar(qsplit, bank[1][:, 0:TOK], col["ca_bq"][:, 0:1], None, ALU.add))
            else:
                link(nc.vector.tensor_copy(qsplit, bank[1][:, 0:TOK]))
            link(nc.vector.tensor_copy(q_part[:, 0, :], qsplit))
            link(nc.vector.tensor_tensor(qsplit, qsplit, q_part[:, 0, :], ALU.subtract))
            link(nc.vector.tensor_copy(q_part[:, 1, :], qsplit))
            link(nc.vector.tensor_tensor(q_part[:, 2, :], qsplit, q_part[:, 1, :], ALU.subtract))
            for hh in range(2):
                for r in range(3):
                    nc.vector.tensor_scalar(q_wide[:, r, :, hh, :],
                                            q_part[:, r, :].rearrange("p (b q) -> p b q", q=S),
                                            pair_mask[:, hh:hh + 1], None, ALU.mult).then_inc(s["q_parts"], 1)

        def sp_qparts(sp, l):
            sp.wait_ge(s["q_parts"], 6 * (l + 1))
            sp.dma_start(q_scratch[l].rearrange("r p n -> p r n"), q_wide.rearrange("p r b h q -> p r (b h q)"))\
                .then_inc(s["q_written"], 16)
            sp.wait_ge(s["q_written"], 16 * (l + 1))
            if l == 1:
                sp.wait_ge(L[0]["qfix_ok"], U)
            for name, lo, hi in (("q_first", 0, 2), ("q_rest", 2, B)):
                for r in range(NPROD):
                    sp.dma_start(
                        Q[PR * r:PR * (r + 1), :, lo * PQ:hi * PQ],
                        q_scratch[l][QPARTS[r], :, lo * PQ:hi * PQ].rearrange("(a x) n -> x a n", x=PR))\
                        .then_inc(s[name], 16)

        def pe_project(pe, l, lhs, w, k):
            for t in range(TT):
                for i in range(len(lhs)):
                    ins = nc.tensor.matmul(bank[2][0:TP, t * 128:(t + 1) * 128], lhs[i][:, t * TP:(t + 1) * TP],
                                           w[i], start=(i == 0), stop=(i == len(lhs) - 1))
            ins.then_inc(s["y_ps"], 1)

        Y = bank[2][0:TP, :].rearrange("p (t d) -> p t d", t=TT)

        def sp_expert(sp, e, r):
            if isinstance(e, int):
                s1, s2 = a["L0_xattn_e_w1"][e], a["L0_xattn_e_w2"][e]
            else:
                s1 = a["L0_xattn_e_w1"][bass.ds(e, 1)].rearrange("o d f -> (o d) f")
                s2 = a["L0_xattn_e_w2"][bass.ds(e, 1)].rearrange("o f d -> (o f) d")
            sp.dma_start(w1[:, r, :], s1).then_inc(s[f"w_in{r}"], 16)
            sp.dma_start(w2[:, r, :, :], s2.rearrange("(f p) d -> p f d", p=128)).then_inc(s[f"w_in{r}"], 16)

        def sp_experts_first(sp):
            for e in range(2):
                sp_expert(sp, e, e)

        def sp_experts(sp):
            with sp.Fori(0, E // 2 - 1) as i:
                for r in range(2):
                    sp.wait_ge(s["y_part"], 8 * i + 4 * r + 4)
                    sp_expert(sp, 2 * i + 2 + r, r)

        @block.sync
        def _(sp):
            sp.dma_start(cst[:, :], a["consts"]).then_inc(s["in_cst"], 16)
            sp.dma_start(x_res[:, :, :], a["x"].rearrange("b q d -> (b q) d").rearrange("(t p) d -> p t d", p=TP))\
                .then_inc(s["in_x"], 16)
            for n in ("sa_wq", "sa_wk", "sa_wv", "sa_wo"):
                sp.dma_start(W[n][:, :], a["L0_xattn_" + n]).then_inc(s["in_sa"], 16)
            for n in ("sa_bq", "sa_bk", "sa_bv"):
                sp.dma_start(col[n][:, :], a["L0_xattn_" + n].rearrange("(p o) -> p o", o=1)).then_inc(s["in_sa"], 16)
            for n in ("ca_wq", "ca_wk", "ca_wv"):
                sp.dma_start(W[n][:, :], a["L0_xattn_" + n]).then_inc(s["in_pipe"], 16)
            for n in ("ca_bq", "ca_bk"):
                sp.dma_start(col[n][:, :], a["L0_xattn_" + n].rearrange("(p o) -> p o", o=1))\
                    .then_inc(s["in_pipe"], 16)
            for n in ("Wq", "Wk", "Wv"):
                sp.dma_start(W["l1_" + n.lower()][:, :], a["L1_xattn_" + n]).then_inc(s["in_tail"], 16)
            for n in ("g_q", "g_c"):
                sp.dma_start(col[n][:, :], a["L1_xattn_" + n].rearrange("(p o) -> p o", o=1))\
                    .then_inc(s["in_tail"], 16)
            sp.dma_start(mask_col8[:, :, :], a["mask_col"]).then_inc(s["in_mask"], 16)
            sp.dma_start(mask_row8[:, :], a["mask_row"]).then_inc(s["in_mask"], 16)
            for n in ("sa_bo", "ca_bo", "ln1_g", "ln1_b", "ln2_g", "ln2_b", "ln3_g", "ln3_b"):
                sp.dma_start(bc[n][:, :], a["L0_xattn_" + n].rearrange("(o d) -> o d", o=1).to_broadcast([TP, 128]))\
                    .then_inc(s["in_wo"], 16)
            sp.dma_start(bc["g_out"][:, :], a["L1_xattn_g_out"].rearrange("(o d) -> o d", o=1)
                         .to_broadcast([TP, 128])).then_inc(s["in_wo"], 16)
            for l in range(2):
                sp.dma_start(wo9[l][:, :, :], a[f"wo9_{l}"]).then_inc(s["in_wo"], 16)
            sp.dma_start(bv9[:, :], a["bv9"]).then_inc(s["in_wo"], 16)
            sp.dma_start(rw[:, :], a["L0_xattn_router_w"]).then_inc(s["in_wo"], 16)
            sp.dma_start(rb[:, :], a["L0_xattn_router_b"].rearrange("(o d) -> o d", o=1).to_broadcast([TP, E]))\
                .then_inc(s["in_wo"], 16)
            sp.dma_start(b1T[:, :], a["b1T"]).then_inc(s["in_wo"], 16)
            sp.dma_start(b2[:, :], a["L0_xattn_e_b2"]).then_inc(s["in_wo"], 16)
            sp_prepare(sp)
            sp.wait_ge(s["krow_ok"], 1)
            sp.dma_start(Q[MROW:MROW + 4, :, :].rearrange("p a n -> p (a n)").rearrange("p (u n) -> p u n", n=UQ),
                         wide(qrows[:, :], U, 1)).then_inc(s["q_rows"], 16)
            sp.wait_ge(s["mask_ok"], 1)
            sp.dma_start(mask_scratch, wide(mask_row, PAIRS, 1)).then_inc(s["mask_written"], 16)
            sp_qparts(sp, 0)
            sp_experts_first(sp)
            sp.wait_ge(s["mask_written"], 16)
            sp_attend(sp, 0)

            sp_experts(sp)
            sp_qparts(sp, 1)
            sp_attend(sp, 1)
            sp.wait_ge(s["x_ok"], 5)
            sp.dma_start(out.rearrange("b q d -> (b q) d").rearrange("(t p) d -> p t d", p=TP), x_new[:, :, :])\
                .then_inc(s["out_done"], 16)
            sp.wait_ge(s["out_done"], 16)

        @block.tensor
        def _(pe):
            give_credits(pe, "pe")
            pe.wait_ge(s["in_cst"], 16)
            pe.wait_ge(s["in_x"], 16)
            pe_xT(pe, x_res, 0)
            pe.wait_ge(s["in_pipe"], 16 * 5)
            pe.wait_ge(s["in_sa"], 16 * 7)
            pe.wait_ge(s["xT_ok"], 1)
            nc.tensor.matmul(bank[1][:, 0:TOK], W["sa_wq"][:, :], xT[:, :], start=True, stop=True)\
                .then_inc(s["sa_proj"], 1)
            nc.tensor.matmul(bank[2][:, 0:TOK], W["sa_wk"][:, :], xT[:, :], start=True, stop=True)\
                .then_inc(s["sa_proj"], 1)
            for h in range(2):
                for i in range(4):
                    b = 4 * h + i
                    ins = nc.tensor.matmul(bank[3 + h][0:S, i * 128:(i + 1) * 128], xT[:, b * S:(b + 1) * S],
                                           W["sa_wv"][:, :], start=True, stop=True)
                ins.then_inc(s["sa_proj"], 1)
            pe_prepare(pe)
            pe.wait_ge(s["vb_zero"], 2)
            def scores(b, r):
                pe.wait_ge(s["qbd_ok"], b + 1)
                if not (isinstance(b, int) and b < 2):
                    pe.wait_ge(s["s_max"], b - 1)
                for t in range(7):
                    ins = nc.tensor.matmul(
                        bank[1 + r][:, t * S:(t + 1) * S],
                        qbd[:, r].rearrange("p h q -> p (h q)")[:, t * 128:(t + 1) * 128],
                        kb[:, r, :], start=True, stop=True)
                ins.then_inc(s["s_ps"], 1)

            def transposes(b, r):
                pe.wait_ge(s["s_norm"], b + 1)
                pe.wait_ge(s["pt_ok"], 2 * b + CREDIT)
                for h, n in enumerate((4, 3)):
                    for t in range(n):
                        at = (4 * h + t) * S
                        ins = nc.tensor.transpose(bank[3 + h][:, t * 128:(t + 1) * 128],
                                                  weights[:, r, at:at + 128], ident)
                    ins.then_inc(s["pt_ps"], 1)

            def outputs(b, r):
                pe.wait_ge(s["vb_ok"], b + 1)
                pe.wait_ge(s["sa_om"], b + CREDIT)
                pe.wait_ge(s["pt_ok"], 2 * b + 2 + CREDIT)
                for g in range(4):
                    ins = nc.tensor.matmul(bank[5][32 * g:32 * g + 32, 0:4 * S], vb[:, r, 32 * g:32 * g + 32],
                                           pT[:, r, g * 4 * S:(g + 1) * 4 * S], start=True, stop=True)
                ins.then_inc(s["sa_o"], 1)

            scores(0, 0)
            scores(1, 1)
            with pe.Fori(0, B // 2 - 1) as i:
                scores(2 * i + 2, 0)
                transposes(2 * i, 0)
                scores(2 * i + 3, 1)
                outputs(2 * i, 0)
                transposes(2 * i + 1, 1)
                outputs(2 * i + 1, 1)
            transposes(B - 2, 0)
            transposes(B - 1, 1)
            outputs(B - 2, 0)
            outputs(B - 1, 1)
            pe.wait_ge(s["oT_ok"], 1)
            pe_project(pe, 0, [oT], [W["sa_wo"][:, :]], 0)
            pe.wait_ge(s["x_ok"], 1)
            pe_xT(pe, x_res, 1)
            pe.wait_ge(s["xT_ok"], 2)
            nc.tensor.matmul(bank[1][:, 0:TOK], W["ca_wq"][:, :], xT[:, :], start=True, stop=True)\
                .then_inc(s["q_ps"], 1)
            pe.wait_ge(s["q_parts"], 1)
            pe.wait_ge(s["wg_ok"], 3)
            pe_attend(pe, 0)
            pe.wait_ge(s["oT_ok"], 2)
            pe.wait_ge(s["in_wo"], 16 * 16)
            pe_project(pe, 0, [oT9[:, hf, :] for hf in range(HALVES)], [wo9[0][:, hf, :] for hf in range(HALVES)], 1)
            pe.wait_ge(s["x_ok"], 2)
            pe_xT(pe, x_res, 2)
            pe.wait_ge(s["xT_ok"], 3)
            for t in range(TT):
                ins = nc.tensor.matmul(bank[1][0:TP, t * E:(t + 1) * E], xT[:, t * TP:(t + 1) * TP], rw[:, :],
                                       start=True, stop=True)
            ins.then_inc(s["rt_ps"], 1)
            pe.wait_ge(s["gate_ok"], 1)
            for t in range(TT):
                ins = nc.tensor.transpose(bank[1][0:E, t * TP:(t + 1) * TP], logit[:, t, :],
                                          cst[0:TP, C_ID:C_ID + TP])
            ins.then_inc(s["gT_ps"], 1)
            pe.wait_ge(s["gT_ok"], 1)
            nc.tensor.matmul(bank[4][:, 0:TOK], b2[:, :], gateT, start=True, stop=False, skip_group_check=True)
            for e in range(E):
                if e >= 4:
                    pe.wait_ge(s["gb_ok"], e - 3)
                nc.tensor.matmul(bank[e % 4][:, 0:TOK], cst[0:E, C_ID + e:C_ID + e + 1].to_broadcast([E, 128]), gateT,
                                 start=True, stop=True).then_inc(s["gb_ps"], 1)
            pe.wait_ge(s["gb_ok"], E)
            with pe.Fori(0, E // 2) as i:
                def second(k):
                    v = 8 * i + k
                    pe.wait_ge(s["h_ok"], v + 1)
                    nc.tensor.matmul(bank[4][:, 0:TOK], w2[:, k // 4, k % 4, :], hid[:, k % 4, :],
                                     start=False, stop=False, skip_group_check=True).then_inc(s["y_part"], 1)

                for k in range(8):
                    v = 8 * i + k
                    if k % 4 == 0:
                        pe.wait_ge(s[f"w_in{k // 4}"], 32 * i + 32)
                    if k >= 4:
                        pe.wait_ge(s["h_act"], v - 3)
                    nc.tensor.matmul(bank[k % 4][:, 0:TOK], w1[:, k // 4, (k % 4) * 128:(k % 4 + 1) * 128],
                                     xT[:, :], start=True, stop=True).then_inc(s["h_ps"], 1)
                    if k >= 2:
                        second(k - 2)
                second(6)
                second(7)
            nc.tensor.matmul(bank[4][:, 0:TOK], ident, xT[:, :], start=False, stop=True, skip_group_check=True)\
                .then_inc(s["yT_ps"], 1)
            pe.wait_ge(s["yT_ok"], 1)
            for t in range(TT):
                ins = nc.tensor.transpose(bank[2][0:TP, t * 128:(t + 1) * 128], yT[:, t * TP:(t + 1) * TP], ident)
            ins.then_inc(s["yt_ps"], 1)
            pe.wait_ge(s["x_ok"], 4)
            pe_xT(pe, x_new, 3)
            pe.wait_ge(s["xT_ok"], 4)
            nc.tensor.matmul(bank[1][:, 0:TOK], W["l1_wq"][:, :], xT[:, :], start=True, stop=True)\
                .then_inc(s["q_ps"], 1)
            pe.wait_ge(s["q_parts"], 7)
            pe_attend(pe, 1)
            pe.wait_ge(L[1]["fin_ok"], U + CREDIT)
            pe_project(pe, 1, [oT9[:, hf, :] for hf in range(HALVES)], [wo9[1][:, hf, :] for hf in range(HALVES)], 2)

        @block.scalar
        def _(act):
            give_credits(act, "act")
            act_xT(act, 0)
            act.wait_ge(s["in_sa"], 16 * 7)
            act.wait_ge(s["sa_proj"], 1)
            nc.scalar.activation(qT[:, :], bank[1][:, 0:TOK], ACT.Identity, bias=col["sa_bq"][:, 0:1])\
                .then_inc(s["qT_ok"], 1)
            act.wait_ge(s["sa_proj"], 2)
            nc.scalar.activation(kT[:, :], bank[2][:, 0:TOK], ACT.Identity, bias=col["sa_bk"][:, 0:1])\
                .then_inc(s["kT_ok"], 1)
            for h in range(2):
                act.wait_ge(s["sa_proj"], 3 + h)
                nc.scalar.copy(v_all[:, 4 * h:4 * h + 4, :].rearrange("p b d -> p (b d)"), bank[3 + h][0:S, :])\
                    .then_inc(s["v_ok"], 1)
            act.wait_ge(s["zeros_ok"], 4)
            act_prepare(act)
            act.wait_ge(s["vb_zero"], 2)
            def exp(b, r):
                act.wait_ge(s["pre_ok"], b + 1)
                rows = sc[:, r].rearrange("p t k -> p (t k)")
                nc.scalar.activation(rows, rows, ACT.Exp, scale=SCALE).then_inc(s["s_exp"], 1)

            def values(i, b, r):
                act.wait_ge(s["sa_o"], 2 * i + CREDIT)
                which = slice(b, b + 1) if isinstance(b, int) else bass.ds(b, 1)
                nc.scalar.copy(vb[0:S, r, :], v_all[:, which, :].rearrange("p o d -> p (o d)"))\
                    .then_inc(s["vb_ok"], 1)

            def transposed(b, r):
                for h, n in enumerate((512, 384)):
                    act.wait_ge(s["pt_ps"], 2 * b + h + 1 + CREDIT)
                    nc.scalar.copy(pT[:, r, 512 * h:512 * h + n], bank[3 + h][:, 0:n]).then_inc(s["pt_ok"], 1)

            exp(0, 0)
            exp(1, 1)
            with act.Fori(0, B // 2 - 1) as i:
                for r in range(2):
                    values(i, 2 * i + r, r)
                for r in range(2):
                    transposed(2 * i + r, r)
                    exp(2 * i + 2 + r, r)
            for r in range(2):
                values(B // 2 - 1, B - 2 + r, r)
            for r in range(2):
                transposed(B - 2 + r, r)
            act_xT(act, 1)
            act_attend(act, 0)
            act_xT(act, 2)
            act.wait_ge(s["rt_ok"], 1)
            nc.scalar.activation(prob[:, :, :], logit[:, :, :], ACT.Exp).then_inc(s["rt_exp"], 1)
            act.wait_ge(s["rt_ok"], 2)
            nc.scalar.activation(g1[:, 3, :], g1[:, 2, :], ACT.Exp).then_inc(s["rt_exp"], 1)
            act.wait_ge(s["gT_ps"], 1)
            nc.scalar.copy(gateT, bank[1][0:E, 0:TOK]).then_inc(s["gT_ok"], 1)
            for e in range(E):
                act.wait_ge(s["gb_ps"], e + 1)
                nc.scalar.copy(gate_bc[:, e, :], bank[e % 4][:, 0:TOK]).then_inc(s["gb_ok"], 1)
            with act.Fori(0, E // 2) as i:
                for k in range(8):
                    v = 8 * i + k
                    act.wait_ge(s["h_ps"], v + 1)
                    if k >= 4:
                        act.wait_ge(s["y_part"], v - 3)
                    nc.scalar.activation(hid[:, k % 4, :], bank[k % 4][:, 0:TOK], ACT.Gelu,
                                         bias=b1T[:, bass.ds(v, 1)]).then_inc(s["h_act"], 1)
            act.wait_ge(s["yT_ps"], 1)
            nc.scalar.copy(yT[:, :], bank[4][:, 0:TOK]).then_inc(s["yT_ok"], 1)
            act_xT(act, 3)
            act_attend(act, 1)

        @block.vector
        def _(dve):
            give_credits(dve, "dve")
            link = Chain(dve, s["dve_c"])
            nc.vector.memset(krep[96:128, :, :, :].rearrange("p s a n -> p (s a n)").bitcast(F32), TWO_ONES)\
                .then_inc(s["zeros_ok"], 1)
            dve.wait_ge(s["in_cst"], 16)
            nc.vector.tensor_copy(identb[:, :], ident).then_inc(s["identb_ok"], 1)
            dve.wait_ge(s["zeros_ok"], 4)
            dve.wait_ge(s["in_pipe"], 16 * 5)
            dve_prepare(dve)
            def shifted(b, r):
                rows = sc[:, r]
                if not (isinstance(b, int) and b < 2):
                    dve.wait_ge(s["s_norm"], b - 1)
                dve.wait_ge(s["s_ps"], b + 1 + CREDIT)
                ps = bank[1 + r][:, 0:7 * S].rearrange("p (t k) -> p t k", k=S)
                nc.vector.tensor_tensor(
                    rows, ps, cst[:, C_CAUSAL:C_LANE].rearrange("p (t k) -> p t k", k=S), ALU.add)\
                    .then_inc(s["s_max"], 1)
                dve.wait_ge(s["s_max"], b + 1)
                nc.vector.tensor_reduce(row_m[:, r, :], rows, AX.X, ALU.max).then_inc(s["row_m_ok"], 1)
                dve.wait_ge(s["row_m_ok"], b + 1)
                nc.vector.tensor_tensor(rows, rows, wide(row_m[:, r, :], S, 2), ALU.subtract)\
                    .then_inc(s["pre_ok"], 1)

            def normalised(i, b, r):
                rows = sc[:, r]
                dve.wait_ge(s["s_exp"], b + 1)
                nc.vector.tensor_reduce(row_s[:, r, :], rows, AX.X, ALU.add).then_inc(s["sum_ok"], 1)
                dve.wait_ge(s["sum_ok"], 2 * b + 1)
                nc.vector.reciprocal(row_m[:, r, :], row_s[:, r, :]).then_inc(s["sum_ok"], 1)
                dve.wait_ge(s["sum_ok"], 2 * b + 2)
                dve.wait_ge(s["pt_ps"], 4 * i + CREDIT)
                nc.vector.tensor_tensor(weights[:, r, 0:7 * S].rearrange("p (t k) -> p t k", k=S), rows,
                                        wide(row_m[:, r, :], S, 2), ALU.mult).then_inc(s["s_norm"], 1)

            def own_lanes(b):
                dve.wait_ge(s["sa_o"], b + 1 + CREDIT)
                which = slice(b, b + 1) if isinstance(b, int) else bass.ds(b, 1)
                nc.vector.tensor_tensor(om[:, which].rearrange("p o i q -> p (o i) q"),
                                        bank[5][:, 0:4 * S].rearrange("p (i q) -> p i q", q=S),
                                        wide(cst[:, C_LANE:C_LANE + 4], S, 2), ALU.mult).then_inc(s["sa_om"], 1)

            shifted(0, 0)
            shifted(1, 1)
            with dve.Fori(0, B // 2 - 1) as i:
                for r in range(2):
                    normalised(i, 2 * i + r, r)
                    shifted(2 * i + 2 + r, r)
                for r in range(2):
                    own_lanes(2 * i + r)
            for r in range(2):
                normalised(B // 2 - 1, B - 2 + r, r)
            for r in range(2):
                own_lanes(B - 2 + r)
            dve.wait_ge(s["sa_om"], B + CREDIT)
            link(nc.vector.tensor_reduce(oT[:, :].rearrange("p (b q) -> p b q", q=S), om.rearrange("p b i q -> p b q i"),
                                         AX.X, ALU.add))
            nc.vector.tensor_scalar(oT[:, :], oT[:, :], col["sa_bv"][:, 0:1], None, ALU.add).then_inc(s["oT_ok"], 1)
            dve.wait_ge(s["in_wo"], 16 * 16)
            dve.wait_ge(s["y_ps"], 1)
            link(nc.vector.tensor_tensor(x_new[:, :, :], Y, x_res[:, :, :], ALU.add))
            link(nc.vector.tensor_tensor(x_new[:, :, :], x_new[:, :, :], wide(bc["sa_bo"][:, :], TT, 1), ALU.add))
            layernorm(dve, link, bc["ln1_g"], bc["ln1_b"], 1, x_res)
            dve_qparts(dve, link, 0)
            dve.wait_ge(s["in_tail"], 16 * 5)
            for n, g in (("l1_wq", "g_q"), ("l1_wk", "g_c"), ("l1_wv", "g_c")):
                nc.vector.tensor_scalar(W[n][:, :], W[n][:, :], col[g][:, 0:1], None, ALU.mult)\
                    .then_inc(s["wg_ok"], 1)
            dve.wait_ge(s["q_rows"], 16)
            dve_attend(dve, 0)
            dve.wait_ge(L[0]["fin_ok"], U + CREDIT)
            for hf in range(HALVES):
                ins = nc.vector.tensor_scalar(oT9[:, hf, :], oT9[:, hf, :], bv9[:, hf:hf + 1], None, ALU.add)
            ins.then_inc(s["oT_ok"], 1)
            dve.wait_ge(s["y_ps"], 2)
            link(nc.vector.tensor_tensor(x_new[:, :, :], Y, x_res[:, :, :], ALU.add))
            link(nc.vector.tensor_tensor(x_new[:, :, :], x_new[:, :, :], wide(bc["ca_bo"][:, :], TT, 1), ALU.add))
            layernorm(dve, link, bc["ln2_g"], bc["ln2_b"], 2, x_res)
            dve_ss(dve, 1, 2)
            dve.wait_ge(s["identb_ok"], 11)
            dve.wait_ge(s["rt_ps"], 1)
            link(nc.vector.tensor_tensor(logit[:, :, :], bank[1][0:TP, 0:TT * E].rearrange("p (t e) -> p t e", e=E),
                                         wide(rb[:, :], TT, 1), ALU.add))
            link(nc.vector.tensor_reduce(g1[:, 0, :], logit[:, :, :], AX.X, ALU.max))
            nc.vector.tensor_tensor(logit[:, :, :], logit[:, :, :], wide(g1[:, 0, :], E, 2), ALU.subtract)\
                .then_inc(s["rt_ok"], 1)
            dve.wait_ge(s["rt_exp"], 1)
            link(nc.vector.tensor_reduce(g1[:, 1, :], prob[:, :, :], AX.X, ALU.add))
            link(nc.vector.reciprocal(g1[:, 0, :], g1[:, 1, :]))
            link(nc.vector.tensor_tensor(prob[:, :, :], prob[:, :, :], wide(g1[:, 0, :], E, 2), ALU.mult))

            def first_best(one, top):
                link(nc.vector.tensor_reduce(top, prob[:, :, :], AX.X, ALU.max))
                link(nc.vector.tensor_tensor(gtmp[:, :, :], prob[:, :, :], wide(top, E, 2), ALU.is_equal))
                link(nc.vector.tensor_tensor(gtmp[:, :, :], gtmp[:, :, :], order[:, :, :], ALU.mult))
                link(nc.vector.tensor_reduce(g1[:, 7, :], gtmp[:, :, :], AX.X, ALU.max))
                link(nc.vector.tensor_tensor(one[:, :, :], order[:, :, :], wide(g1[:, 7, :], E, 2), ALU.is_equal))

            first_best(one1, g1[:, 4, :])
            link(nc.vector.scalar_tensor_tensor(out=prob[:, :, :], in0=one1[:, :, :], scalar=-2.0,
                                                in1=prob[:, :, :], op0=ALU.mult, op1=ALU.add))
            first_best(one2, g1[:, 5, :])
            nc.vector.tensor_tensor(g1[:, 2, :], g1[:, 5, :], g1[:, 4, :], ALU.subtract).then_inc(s["rt_ok"], 1)
            dve.wait_ge(s["rt_exp"], 2)
            link(nc.vector.tensor_scalar(g1[:, 0, :], g1[:, 3, :], 1.0, None, ALU.add))
            link(nc.vector.reciprocal(g1[:, 6, :], g1[:, 0, :]))
            link(nc.vector.tensor_tensor(g1[:, 1, :], g1[:, 3, :], g1[:, 6, :], ALU.mult))
            link(nc.vector.tensor_tensor(one1[:, :, :], one1[:, :, :], wide(g1[:, 6, :], E, 2), ALU.mult))
            link(nc.vector.tensor_tensor(one2[:, :, :], one2[:, :, :], wide(g1[:, 1, :], E, 2), ALU.mult))
            nc.vector.tensor_tensor(logit[:, :, :], one1[:, :, :], one2[:, :, :], ALU.add).then_inc(s["gate_ok"], 1)
            dve.wait_ge(s["gb_ok"], E)
            with dve.Fori(0, E // 2) as i:
                for k in range(8):
                    v = 8 * i + k
                    dve.wait_ge(s["h_act"], v + 1)
                    nc.vector.tensor_tensor(hid[:, k % 4, :], hid[:, k % 4, :],
                                            gate_bc[:, bass.ds(2 * i + k // 4, 1), :]
                                            .rearrange("p o n -> p (o n)"), ALU.mult).then_inc(s["h_ok"], 1)
            dve.wait_ge(s["yt_ps"], 1)
            link(nc.vector.tensor_copy(x_new[:, :, :], Y))
            layernorm(dve, link, bc["ln3_g"], bc["ln3_b"], 3, x_res)
            dve.wait_ge(s["x_ok"], 3)

            def sumsq(src):
                link(nc.vector.tensor_tensor(x_new[:, :, :], src, src, ALU.mult))
                nc.vector.tensor_reduce(mv[:, :, 1], x_new[:, :, :], AX.X, ALU.add).then_inc(s["var_ok"], 1)

            sumsq(x_res[:, :, :])
            dve.wait_ge(s["rstd_ok"], 4)
            nc.vector.tensor_tensor(x_new[:, :, :], x_res[:, :, :], wide(rstd[:, :], 128, 2), ALU.mult)\
                .then_inc(s["x_ok"], 1)
            dve_qparts(dve, link, 1)
            dve_attend(dve, 1)
            dve.wait_ge(s["y_ps"], 3)
            link(nc.vector.tensor_tensor(x_res[:, :, :], Y, x_res[:, :, :], ALU.add))
            sumsq(x_res[:, :, :])
            dve.wait_ge(s["rstd_ok"], 5)
            link(nc.vector.tensor_tensor(x_new[:, :, :], x_res[:, :, :], wide(rstd[:, :], 128, 2), ALU.mult))
            nc.vector.tensor_tensor(x_new[:, :, :], x_new[:, :, :], wide(bc["g_out"][:, :], TT, 1), ALU.mult)\
                .then_inc(s["x_ok"], 1)

        @block.gpsimd
        def _(pool):
            give_credits(pool, "pool")
            link = Chain(pool, s["pool_c"])
            nc.gpsimd.memset(krep[0:96, :, :, SK:KW], 0.0).then_inc(s["zeros_ok"], 1)
            nc.gpsimd.memset(v9[:, :, :, :], 1.0).then_inc(s["zeros_ok"], 1)
            for tile, value in ((neghalf, -0.5), (inv_d, 1.0 / D), (rms_eps, 1e-6), (zero, 0.0)):
                ins = nc.gpsimd.memset(tile[:, :], value)
            ins.then_inc(s["zeros_ok"], 1)
            nc.gpsimd.memset(mparts[:, :, :, :], 1.0).then_inc(s["identb_ok"], 1)
            for e in range(E):
                nc.gpsimd.memset(order[:, :, e], float(E - e)).then_inc(s["identb_ok"], 1)
            link(nc.gpsimd.memset(qrows[:, :], 1.0))
            nc.gpsimd.memset(qrows[0:3, :], 0.0).then_inc(s["krow_ok"], 1)
            pool.wait_ge(s["in_mask"], 32)
            nc.gpsimd.tensor_copy(mask_col[:, :, :], mask_col8[:, :, :]).then_inc(s["identb_ok"], 1)
            nc.gpsimd.tensor_scalar(mask_row, mask_row8[:, :], BIG, -BIG, ALU.mult, ALU.add).then_inc(s["mask_ok"], 1)
            nc.gpsimd.memset(vb[:, :, :], 0.0).then_inc(s["vb_zero"], 1)
            nc.gpsimd.memset(weights[:, :, 7 * S:WT], 0.0).then_inc(s["vb_zero"], 1)
            pool.wait_ge(s["in_cst"], 16)
            pool.wait_ge(s["qT_ok"], 1)
            pool.wait_ge(s["kT_ok"], 1)

            def block_diagonal(b, r):
                batch = slice(b * S, (b + 1) * S) if isinstance(b, int) else bass.ds(b * S, S)
                queries = qT[:, batch]
                nc.gpsimd.tensor_tensor(kb[:, r, :], kT[:, batch], zero[:, 0:1].to_broadcast([128, S]), ALU.add)
                nc.gpsimd.tensor_tensor(qbd[:, r], wide(queries, H, 1), wide(cst[:, C_HEAD:C_HEAD + H], S, 2),
                                        ALU.mult).then_inc(s["qbd_ok"], 1)

            block_diagonal(0, 0)
            block_diagonal(1, 1)
            pool_prepare(pool)
            with pool.Fori(0, B // 2 - 1) as i:
                for r in range(2):
                    pool.wait_ge(s["s_ps"], 2 * i + r + 1 + CREDIT)
                    block_diagonal(2 * i + 2 + r, r)
            pool_rstd(pool, link, 1, mv[:, :, 1], 1.0, 1e-5)
            pool.wait_ge(s["mask_written"], 16)
            pool_attend(pool, 0)
            pool_rstd(pool, link, 2, mv[:, :, 1], 1.0, 1e-5)
            pool_squares(pool, 1, 2, 0)
            pool_norm(pool, 1, 2, 0)
            pool_rstd(pool, link, 3, mv[:, :, 1], 1.0, 1e-5)
            pool_rstd(pool, link, 4, mv[:, :, 1], 1.0 / D, 1e-6)
            pool_attend(pool, 1)
            pool_rstd(pool, link, 5, mv[:, :, 1], 1.0 / D, 1e-6)


_INS = ["x", "ctx_1024"] + ["L0_xattn_" + n for n in (
    "sa_wq", "sa_bq", "sa_wk", "sa_bk", "sa_wv", "sa_bv", "sa_wo", "sa_bo", "ca_wq", "ca_bq", "ca_wk", "ca_bk",
    "ca_wv", "ca_bo", "ln1_g", "ln1_b", "ln2_g", "ln2_b", "ln3_g", "ln3_b", "router_w", "router_b",
    "e_w1", "e_w2", "e_b2")] + ["L1_xattn_" + n for n in ("Wq", "Wk", "Wv", "g_q", "g_c", "g_out")]


def _rows9(w):
    out = np.zeros((128, HALVES, w.shape[1]), w.dtype)
    for h in range(H):
        hf, g, j = h // 8, (h % 8) // 2, h % 2
        at = 32 * g + VW * j
        out[at:at + HD, hf] = w[h * HD:(h + 1) * HD]
    return out


def kernel(**inputs):
    import concourse.bacc as _bacc
    from concourse.bass_utils import run_bass_kernel_spmd as _run

    v = {n: np.ascontiguousarray(inputs[n]) for n in _INS}
    mask = np.ascontiguousarray(inputs["mask_BxS2_bf1"]).view(np.uint8).reshape(B, KP, KC)
    v["mask_col"] = np.ascontiguousarray(mask.transpose(1, 0, 2))
    v["mask_row"] = np.ascontiguousarray(mask.transpose(0, 2, 1)).reshape(B, SK)
    v["wo9_0"] = _rows9(np.asarray(inputs["L0_xattn_ca_wo"] if "L0_xattn_ca_wo" in inputs else None))
    v["wo9_1"] = _rows9(np.asarray(inputs["L1_xattn_Wo"]))
    v["bv9"] = np.ascontiguousarray(_rows9(np.asarray(inputs["L0_xattn_ca_bv"]).reshape(128, 1))[:, :, 0])
    v["b1T"] = np.ascontiguousarray(np.asarray(inputs["L0_xattn_e_b1"]).reshape(E * 4, 128).T)
    v["consts"] = constants()
    nc = _bacc.Bacc("TRN2", target_bir_lowering=False, num_devices=1)
    arrays, a = {}, {}
    for name, array in v.items():
        arrays[f"in_{name}"] = array
        a[name] = nc.dram_tensor(f"in_{name}", array.shape, mybir.dt.from_np(array.dtype), kind="ExternalInput").ap()
    out = nc.dram_tensor("out_0", (B, S, D), F32, kind="ExternalOutput").ap()
    build_program(nc, a, out)
    r = _run(nc, [arrays], core_ids=[0])
    return r.results[0]["out_0"]
```

```python
from contextlib import ExitStack

import concourse.bass as bass
import numpy as np
from concourse import mybir

F32 = mybir.dt.float32
BF16 = mybir.dt.bfloat16
U8 = mybir.dt.uint8
ALU = mybir.AluOpType
ACT = mybir.ActivationFunctionType
AX = mybir.AxisListType

B, S, D = 8, 56, 128
SK = 1500
H, HD = 16, 8
E, FF = 8, 512
TOK = B * S
TT, TP = 4, 112
KC = 12
KP = SK // KC
KB = 500
NKB = SK // KB
KW = SK + 4
HALVES = 2
U = B * HALVES
PAIRS = H // 2 // HALVES
PQ = 2 * S
UQ = PAIRS * PQ
PR = 2 * HD
QPARTS = (0, 1, 2, 0, 1, 0)
KPARTS = (0, 0, 0, 1, 1, 2)
NPROD = len(QPARTS)
MROW = NPROD * PR
VW = HD + 1
VROW = 160
SCALE = float(HD) ** -0.5
CREDIT = 1
BIG = 1e30
NEG = -1e30
TWO_ONES = float(np.array([0x3F803F80], np.uint32).view(np.float32)[0])

C_ID, C_SEL, C_HEAD, C_CAUSAL = 0, 128, 256, 272
C_LANE = C_CAUSAL + 7 * S
C_PAIR = C_LANE + 4
C_HALF = C_PAIR + 2
C_W = C_HALF + 2


def constants():
    c = np.zeros((128, C_W), np.float32)
    p = np.arange(128)
    c[:, C_ID:C_ID + 128] = np.eye(128)
    lane, row = p // 32, p % 32
    used = row < 2 * VW
    source = 32 * lane + np.where(used, VW * (row // VW), 0) + HD
    c[source, C_SEL + p] = 1.0
    c[p, C_HEAD + p // HD] = 1.0
    q = (128 * np.arange(7)[None, :] + p[:, None]) % S
    after = np.arange(S)[None, None, :] > q[:, :, None]
    c[:, C_CAUSAL:C_LANE] = np.where(after, NEG, 0.0).reshape(128, 7 * S)
    c[p, C_LANE + row // HD] = 1.0
    c[p, C_PAIR + (p // HD) % 2] = 1.0
    c[p[used], C_HALF + row[used] // VW] = 1.0
    return c


def query_selection():
    c = np.zeros((128, 3, PAIRS, MROW), np.float32)
    for r, part in enumerate(QPARTS):
        for p in range(PAIRS):
            for x in range(PR):
                c[PR * p + x, part, p, PR * r + x] = 1.0
    return c.reshape(128, 3 * PAIRS * MROW)


class Chain:

    def __init__(self, eng, sem, start=0):
        self.eng, self.sem, self.n = eng, sem, start

    def __call__(self, ins):
        ins.then_inc(self.sem, 1)
        self.n = self.n + 1
        self.eng.wait_ge(self.sem, self.n)


def build_program(nc, a, out):
    ctx = ExitStack()
    with ctx:
        def sb(name, shape, dt=F32):
            return ctx.enter_context(nc.sbuf_tensor(name, shape, dt))

        def sem(name):
            return ctx.enter_context(nc.semaphore(name))

        bank = [ctx.enter_context(nc.psum_tensor(f"bank{i}", [128, 512], F32)) for i in range(8)]
        ROWS, SCORES, OUT, MISC = bank[0:2], bank[2:5], bank[5], bank[6:8]

        k_scratch = [nc.dram_tensor(f"k_scratch{l}", (B, 3, 128, SK), BF16, kind="Internal").ap() for l in range(2)]
        q_scratch = [nc.dram_tensor(f"q_scratch{l}", (3, 128, B * PQ), BF16, kind="Internal").ap()
                     for l in range(2)]
        mask_scratch = nc.dram_tensor("mask_scratch", (B, PAIRS, SK), BF16, kind="Internal").ap()

        cst = sb("cst", [128, C_W])
        identb = sb("identb", [128, 128], BF16)
        selq = sb("selq", [128, 3, PAIRS, MROW], BF16)
        qrows = sb("qrows", [4, UQ], BF16)
        ident = cst[:, C_ID:C_ID + 128]
        sel = cst[:, C_SEL:C_SEL + 128]
        half_mask = cst[:, C_HALF:C_HALF + 2]
        pair_mask = cst[:, C_PAIR:C_PAIR + 2]
        W = {n: sb("w_" + n, [128, 128]) for n in
             ("sa_wq", "sa_wk", "sa_wv", "sa_wo", "ca_wq", "ca_wk", "ca_wv", "l1_wq", "l1_wk", "l1_wv")}
        wo9 = [sb(f"wo9_{l}", [128, HALVES, 128]) for l in range(2)]
        col = {n: sb("c_" + n, [128, 1]) for n in ("sa_bq", "sa_bk", "sa_bv", "ca_bq", "ca_bk", "g_q", "g_c",
                                                  "ln1_g", "ln1_b", "ln2_g", "ln2_b")}
        IN_WO = 20
        bv9 = sb("bv9", [128, HALVES])
        bc = {n: sb("b_" + n, [TP, 128]) for n in
              ("sa_bo", "ca_bo", "ln1_g", "ln1_b", "ln2_g", "ln2_b", "ln3_g", "ln3_b", "g_out")}
        rw = sb("rw", [128, E])
        rb = sb("rb", [TP, E])
        b1T = sb("b1T", [128, E * 4])
        b2 = sb("b2", [E, 128])

        x_res = sb("x_res", [TP, TT, 128])
        x_new = sb("x_new", [TP, TT, 128])
        xT = sb("xT", [128, TOK])
        qT = sb("qT", [128, TOK])
        kT = sb("kT", [128, TOK])
        oT9 = sb("oT9", [128, HALVES, TOK])
        oT = kT
        stats = sb("stats", [TP, TT, 6])
        mv = sb("mv", [TP, TT, 2])
        rstd = sb("rstd", [TP, TT])
        neghalf, zero, inv_d, rms_eps, euler = (
            sb(n, [128, KC]) for n in ("neghalf", "zero", "inv_d", "rms_eps", "euler"))

        krep = sb("krep", [128, 4, PAIRS, KW], BF16)
        Q = sb("Q", [100, H // 2, B * PQ], BF16)
        qfix = sb("qfix", [100, 4, UQ], BF16)
        ctx_tile = sb("ctx_tile", [KP, 2, KC, 128])
        ctxT = sb("ctxT", [128, 2, SK])
        kparts = sb("kparts", [128, 2, 3, SK], BF16)
        k_rest = sb("k_rest", [128, SK])
        v9 = sb("v9", [KP, 2, KC, VROW])
        P = sb("P", [KP, 4, UQ])
        mx = sb("mx", [TP, 2, PAIRS, NKB])
        mt = sb("mt", [TP, 2, PAIRS])
        row_top = sb("row_top", [TP, 2, PAIRS])
        mparts = sb("mparts", [TP, 2, PAIRS, 4], BF16)
        o_first = sb("o_first", [128, S])
        comb = sb("comb", [128, S])
        rec = sb("rec", [128, S])
        key_ss = sb("key_ss", [KP, KC])
        key_rs = sb("key_rs", [KP, KC])
        mask_col8 = sb("mask_col8", [KP, B, KC], U8)
        mask_col = sb("mask_col", [KP, B, KC])
        mask_row8 = sb("mask_row8", [B, SK], U8)
        sq = sb("sq", [KP, KC, 128])
        mask_row = sq[0:B, :, :].rearrange("p c d -> p (c d)").bitcast(BF16)[:, 0:SK]

        SCR = 7424
        scratch = sb("scratch", [128, SCR])
        qbd = scratch[:, 0:1792].rearrange("p (r h q) -> p r h q", r=2, h=H)
        sc = scratch[:, 1792:1792 + 784].rearrange("p (r t k) -> p r t k", r=2, t=7)
        pT = scratch[:, 2576:2576 + 1792].rearrange("p (r n) -> p r n", r=2)
        vb = scratch[:, 4368:4368 + 256].rearrange("p (r n) -> p r n", r=2)
        row_m = scratch[:, 4624:4638].rearrange("p (r t) -> p r t", r=2)
        row_s = scratch[:, 4640:4654].rearrange("p (r t) -> p r t", r=2)
        om = scratch[:, 4656:4656 + 4 * TOK].rearrange("p (b i q) -> p b i q", b=B, i=4)
        qsplit = scratch[:, 0:TOK]
        q_part = scratch[:, 512:512 + 3 * TOK // 2].bitcast(BF16).rearrange("p (r n) -> p r n", r=3)
        q_wide = scratch[:, 1536:1536 + 3 * TOK].bitcast(BF16).rearrange("p (r b h q) -> p r b h q", r=3, b=B, h=2)
        w1 = scratch[:, 0:1024].rearrange("p (r f) -> p r f", r=2)
        w2 = scratch[:, 1024:2048].rearrange("p (r f n) -> p r f n", r=2, f=4)
        hid = scratch[:, 5632:5632 + 4 * TOK].rearrange("p (r n) -> p r n", r=4)
        gateT = kT[0:E, :]
        v_all = P[0:S, :, :].rearrange("p c n -> p (c n)")[:, 0:B * 128].rearrange("p (b d) -> p b d", b=B)
        WT = 7 * S + 128 - S
        weights = sb("weights", [128, 2, WT])
        logit = sb("logit", [TP, TT, E])
        prob = sb("prob", [TP, TT, E])
        one1 = sb("one1", [TP, TT, E])
        one2 = sb("one2", [TP, TT, E])
        gtmp = scratch[0:TP, 3200:3200 + TT * E].rearrange("p (t e) -> p t e", t=TT)
        order = sb("order", [TP, TT, E])
        g1 = sb("g1", [TP, 8, TT])

        def wide(ap, n, at):
            shape = list(ap.shape)
            shape.insert(at, n)
            return ap.unsqueeze(at).to_broadcast(shape)

        names = ("in_cst", "in_x", "in_sa", "in_pipe", "in_tail", "in_mask", "in_wo", "identb_ok", "zeros_ok",
                 "pool_c", "dve_c", "xT_ps", "xT_ok", "sa_proj", "qT_ok", "kT_ok", "v_ok", "qbd_ok",
                 "s_ps", "s_max", "s_exp", "s_norm", "vb_ok", "pt_ps", "pt_ok", "sa_o", "sa_om",
                 "oT_ok", "y_ps", "var_ok", "rstd_ok", "x_ok", "q_ps", "q_part", "q_part_b",
                 "q_even", "q_odd", "q_even_b", "q_odd_b",
                 "q_sb", "q0_ps", "in_selq", "selq_ok", "q_written0", "q_written1", "q_written2", "q_first",
                 "q_rest", "q_rows", "wg_ok", "mask_ok", "mask_written", "krow_ok",
                 "rt_ps", "rt_ok", "rt_exp", "gate_ok", "gT_ps", "gT_ok", "y_used", "b2_ps", "w_in0", "w_in1", "h_ps",
                 "h_act", "y_part", "out_done", "pre_ok", "sum_ok", "row_m_ok", "vb_zero", "bias_ok", "y_early")
        s = {n: sem(n) for n in names}
        layer_names = ("ctx_in0", "ctx_in1", "kw0", "kw1", "krep0", "krep1", "krep2", "krep3", "t_ps", "t_ok",
                       "k_ps", "k_high", "k_res", "k_mid", "k_low", "v_ps", "v_ok", "m_ps", "m_ok", "bc_ps",
                       "bc_ok", "row_ps", "row_max", "top_ok", "st_ps", "exp_ok", "pv_ok", "comb_ok", "fin_ok",
                       "m_parts", "qfix_ok", "sq_ok", "ss_ok", "ctx_ok", "pool_m", "pool_n", "dve_o")
        L = [{n: sem(f"l{l}_{n}") for n in layer_names} for l in range(2)]

        CREDITS = {"pe": ((), ("st_ps", "pv_ok", "m_ps")),
                   "dve": (("y_used",), ("comb_ok", "bc_ok")),
                   "pool": ((), ("fin_ok",))}

        def give_credits(eng, name):
            phase, layer = CREDITS[name]
            for n in phase:
                eng.sem_inc(s[n], CREDIT)
            for z in L:
                for n in layer:
                    eng.sem_inc(z[n], CREDIT)

        block = ctx.enter_context(nc.Block())

        STEP_ITEMS = [
            {0: [("T", 2, 0)], 1: [("T", 2, 1)], 2: [("T", 2, 2)], 4: [("K", 2, 0)],
             6: [("K", 2, 1)], 8: [("K", 2, 2)], 10: [("M", 1)]},
            {1: [("V", 1, 0)], 3: [("D", -1)], 5: [("V", 1, 1)], 8: [("V", 1, 2)], 10: [("M", 1)]},
            {0: [("T", 3, 0)], 1: [("T", 3, 1)], 2: [("T", 3, 2)], 3: [("D", -1)], 4: [("K", 3, 0)],
             6: [("K", 3, 1)], 8: [("K", 3, 2)], 10: [("M", 1)]},
            {1: [("V", 2, 0)], 3: [("D", -1)], 5: [("V", 2, 1)], 8: [("V", 2, 2)], 10: [("M", 1)],
             13: [("D", 0)]},
        ]
        LEAD = 4

        def row_of(u, s_, slot):
            k = slot + LEAD
            v, c = u + 1 + k // 12, k % 12
            return None if isinstance(u, int) and v >= U else (v, (s_ + 1 + k // 12) % 4, c)

        def where(l, n):
            return (l + 1, n - B) if isinstance(n, int) and n >= B else (l, n)

        def items_of(l, j, s_):
            got = {}
            for slot, items in STEP_ITEMS[s_].items():
                for it in items:
                    if it[0] in "TKV":
                        layer, n = where(l, 2 * j + it[1])
                        par = it[1] % 2
                    else:
                        layer, n = l, 4 * j + s_ + it[1]
                        par = (s_ + it[1]) % 4
                    if layer > 1 or (isinstance(n, int) and n >= U):
                        continue
                    got.setdefault(slot, []).append((it[0], n, it[2] if len(it) > 2 else 0, par, layer))
            return got

        PROLOGUE = ([("T", 0, i, 0, 0) for i in range(3)] + [("K", 0, i, 0, 0) for i in range(3)]
                    + [("T", 1, i, 1, 0) for i in range(3)] + [("K", 1, i, 1, 0) for i in range(3)]
                    + [("V", 0, i, 0, 0) for i in range(3)] + [("M", 0, 0, 0, 0)])

        def full_order(l, j):
            order_ = []
            for s_ in range(4):
                got = items_of(l, j, s_)
                for slot in sorted(got):
                    order_ += got[slot]
            return order_

        def consumed(item):
            kind, n, i, _, l = item
            if kind in "TKV":
                return L[l][{"T": "t_ok", "K": "k_res", "V": "v_ok"}[kind]], 3 * n + i + 1
            return (L[l]["m_ok"], n + 1) if kind == "M" else (L[l]["bc_ok"], n + 1 + CREDIT)

        def filled(item):
            kind, n, i, _, l = item
            if kind in "TKV":
                return L[l][{"T": "t_ps", "K": "k_ps", "V": "v_ps"}[kind]], 3 * n + i + 1
            return (L[l]["m_ps"], n + 1 + CREDIT) if kind == "M" else (L[l]["bc_ps"], n + 1)

        def passes(eng, body, looped):
            with eng.Fori(0, looped) as j:
                body(j)
            for j in range(looped, 4):
                body(j)

        KR = [MROW, MROW + 4]
        KS = [MROW + 3, MROW + 4]

        def pe_item(pe, item, index, before):
            kind, n, i, par, l = item
            ps = MISC[index % 2]
            z = L[l]
            if before is not None:
                pe.wait_ge(*consumed(before))
            if kind == "T":
                if i == 0:
                    if l == 0:
                        pe.wait_ge(z[f"ctx_in{par}"], 16 * (n // 2 + 1) if isinstance(n, int) else (n - par) * 8 + 16)
                    else:
                        pe.wait_ge(z["ctx_ok"], n + 1)
                for k in range(4):
                    ins = nc.tensor.transpose(ps[:, k * KP:(k + 1) * KP], ctx_tile[:, par, 4 * i + k, :],
                                              cst[0:KP, C_ID:C_ID + KP])
                ins.then_inc(z["t_ps"], 1)
            if kind == "K":
                pe.wait_ge(z["t_ok"], 3 * n + i + 1)
                w = W["ca_wk"] if l == 0 else W["l1_wk"]
                nc.tensor.matmul(ps[:, 0:KB], w[:, :], ctxT[:, par, i * KB:(i + 1) * KB],
                                 start=True, stop=True).then_inc(z["k_ps"], 1)
            if kind == "V":
                w = W["ca_wv"] if l == 0 else W["l1_wv"]
                for k in range(4):
                    c = 4 * i + k
                    ins = nc.tensor.matmul(ps[0:KP, k * 128:(k + 1) * 128], ctxT[:, par, c * KP:(c + 1) * KP],
                                           w[:, :], start=True, stop=True)
                ins.then_inc(z["v_ps"], 1)
            if kind == "M":
                pe.wait_ge(z["m_parts"], n + 1)
                for p in range(PAIRS):
                    ins = nc.tensor.matmul(ps[96:100, p * PQ:(p + 1) * PQ], mparts[:, par % 2, p, :],
                                           identb[0:TP, 0:TP], start=True, stop=True)
                ins.then_inc(z["m_ps"], 1)
            if kind == "D":
                pe.wait_ge(z["comb_ok"], n + 1 + CREDIT)
                nc.tensor.matmul(ps[:, 0:S], sel, comb[:, :], start=True, stop=True).then_inc(z["bc_ps"], 1)

        def row_bank(v, c, lead):
            return ([*ROWS, *SCORES])[(12 * v + c + 1) % 5] if lead else ROWS[c % 2]

        def pe_row(pe, l, v, slot, c, lead=False):
            z = L[l]
            if c == 0:
                gen = v // 4 + 1 if isinstance(v, int) else None
                pe.wait_ge(z[f"krep{slot}"], KREP_INC[l] * gen if gen is not None else
                           (v - slot) * (KREP_INC[l] // 4) + KREP_INC[l])
                pe.wait_ge(z["qfix_ok"], v + 1)
            if not lead:
                pe.wait_ge(z["row_max"], 12 * v + c - 1)
            elif 12 * v + c >= 5:
                pe.wait_ge(z["row_max"], 12 * v + c - 4)
            p, n = c // NKB, c % NKB
            nc.tensor.matmul(row_bank(v, c, lead)[0:PQ, 0:KB], qfix[0:KR[l], slot, p * PQ:(p + 1) * PQ],
                             krep[0:KR[l], slot, p, n * KB:(n + 1) * KB], start=True, stop=True)\
                .then_inc(z["row_ps"], 1)

        def pe_st(pe, l, u, slot, c):
            z = L[l]
            if c == 0:
                pe.wait_ge(z["m_ok"], u + 1)
            if c >= 3:
                pe.wait_ge(z["exp_ok"], 12 * u + c - 2)
            for p in range(PAIRS):
                ins = nc.tensor.matmul(SCORES[c % 3][:, p * PQ:(p + 1) * PQ],
                                       krep[0:KS[l], slot, p, c * KP:c * KP + 128],
                                       qfix[0:KS[l], slot, p * PQ:(p + 1) * PQ], start=True, stop=True)
            ins.then_inc(z["st_ps"], 1)

        def pe_pv(pe, l, j, s_, c):
            z = L[l]
            u = 4 * j + s_
            if c == 0:
                pe.wait_ge(z["comb_ok"], u + CREDIT)
                if s_ % 2 == 0:
                    b = 2 * j + s_ // 2
                    pe.wait_ge(z["v_ok"], 3 * b + 3)
            pe.wait_ge(z["exp_ok"], 12 * u + c + 1)
            hf, par = s_ % 2, (s_ // 2) % 2
            for g in range(4):
                at = VW * (8 * hf + 2 * g)
                ins = nc.tensor.matmul(OUT[32 * g:32 * g + 32, 0:PQ], v9[:, par, c, at:at + 32],
                                       P[:, c % 4, g * PQ:(g + 1) * PQ], start=(c == 0), stop=(c == KC - 1))
            ins.then_inc(z["pv_ok"], 1)

        def pe_attend(pe, l):
            pe.wait_ge(s["identb_ok"], 11)
            for k in range(12 + LEAD):
                pe_row(pe, l, k // 12, k // 12, k % 12, lead=True)
            pe_item(pe, ("M", 0, 0, 0, l), 1, PROLOGUE[-3] if l == 0 else ("D", U - 1, 0, 3, 0))

            z = L[l]

            def body(j):
                last = isinstance(j, int)
                before = [("V", 2 * j, 2, 0, l), ("D", 4 * j - 1, 0, 3, l)]
                order_ = before + full_order(l, j)
                k = 0
                for s_ in range(4):
                    got = items_of(l, j, s_)
                    u = 4 * j + s_
                    for slot in range(14):
                        if slot < 12 and row_of(u, s_, slot):
                            v, v_slot, c = row_of(u, s_, slot)
                            pe_row(pe, l, v, v_slot, c)
                        if slot < 12:
                            for item in got.get(slot, []):
                                pe_item(pe, item, k, order_[k])
                                k += 1
                            pe_st(pe, l, u, s_, slot)
                        if slot >= 2:
                            pe_pv(pe, l, j, s_, slot - 2)
                    for item in got.get(13, []):
                        pe_item(pe, item, k, order_[k])
                        k += 1
                    if last and s_ == 2:
                        if l == 0:
                            pe.wait_ge(s["oT_ok"], 3)
                            pe.wait_ge(s["in_wo"], 16 * IN_WO)
                        else:
                            pe.wait_ge(z["fin_ok"], U - 4 + CREDIT)
                        pe.wait_ge(z["row_max"], 12 * U)
                        project_heads(pe, l, range(TT - 1)).then_inc(s["y_early"], 1)
                assert last or k == 26

            passes(pe, body, 3)

        def act_item(act, item, index):
            kind, n, i, par, l = item
            ps = MISC[index % 2]
            z = L[l]
            act.wait_ge(*filled(item))
            if kind == "T":
                nc.scalar.copy(ctxT[:, par, i * KB:(i + 1) * KB], ps[:, 0:KB]).then_inc(z["t_ok"], 1)
            if kind == "K":
                if i == 0 and l == 1 and isinstance(n, int) and n < 2:
                    act.wait_ge(L[0][f"kw{par}"], 16 * (B // 2))
                elif i == 0 and not (isinstance(n, int) and n < 2):
                    act.wait_ge(z[f"kw{par}"], 16 * (n // 2) if isinstance(n, int) else (n - par) * 8)
                hi = kparts[:, par, 0, i * KB:(i + 1) * KB]
                if l == 0:
                    nc.scalar.activation(hi, ps[:, 0:KB], ACT.Identity, bias=col["ca_bk"][:, 0:1])\
                        .then_inc(z["k_high"], 1)
                else:
                    nc.scalar.copy(hi, ps[:, 0:KB]).then_inc(z["k_high"], 1)
            if kind == "V":
                if i == 0 and l == 1 and isinstance(n, int) and n == 0:
                    act.wait_ge(L[0]["pv_ok"], 12 * (U - 2) + CREDIT)
                elif i == 0 and not (isinstance(n, int) and n < 2):
                    act.wait_ge(z["pv_ok"], 24 * n - 24 + CREDIT)
                nc.scalar.copy(
                    v9[:, par, 4 * i:4 * i + 4, 0:H * VW].rearrange("p c (h w) -> p c h w", w=VW)[:, :, :, 0:HD],
                    ps[0:KP, :].rearrange("p (c h d) -> p c h d", c=4, d=HD)).then_inc(z["v_ok"], 1)
            if kind == "M":
                nc.scalar.copy(qfix[96:100, par, :], ps[96:100, 0:UQ])\
                    .then_inc(z["m_ok"], 1)

        def act_mid(act, l, n, i, par):
            z = L[l]
            act.wait_ge(z["k_res"], 3 * n + i + 1)
            nc.scalar.copy(kparts[:, par, 1, i * KB:(i + 1) * KB], k_rest[:, i * KB:(i + 1) * KB])\
                .then_inc(z["k_mid"], 1)

        def act_attend(act, l):
            z = L[l]
            act_item(act, ("M", 0, 0, 0, l), 1)

            def body(j):
                k = 0
                for s_ in range(4):
                    got = items_of(l, j, s_)
                    u = 4 * j + s_
                    mids = {6: (4, 0), 8: (6, 1), 11: (8, 2)}
                    for slot in range(12):
                        act.wait_ge(z["st_ps"], 12 * u + slot + 1 + CREDIT)
                        if slot >= 4:
                            act.wait_ge(z["pv_ok"], 12 * u + slot - 3 + CREDIT)
                        nc.scalar.activation(P[:, slot % 4, :], SCORES[slot % 3][0:KP, 0:UQ], ACT.Exp,
                                             scale=SCALE).then_inc(z["exp_ok"], 1)
                        for item in got.get(slot, []):
                            if item[0] != "D":
                                act_item(act, item, k)
                            k += 1
                        layer, b = where(l, 2 * j + 2 + s_ // 2)
                        if s_ in (0, 2) and layer < 2 and slot in mids:
                            act_mid(act, layer, b, mids[slot][1], (s_ // 2) % 2)
                    k += len(got.get(13, []))

            passes(act, body, 3)

        def dve_res(dve, l, n, i, par, index):
            z = L[l]
            dve.wait_ge(z["k_high"], 3 * n + i + 1)
            if not (isinstance(n, int) and n == 0):
                dve.wait_ge(z["k_low"], 3 * n + i - 2)
            elif l == 1:
                dve.wait_ge(L[0]["k_low"], 3 * B + i - 2)
            hi = kparts[:, par, 0, i * KB:(i + 1) * KB]
            dst = k_rest[:, i * KB:(i + 1) * KB]
            ps = MISC[index % 2][:, 0:KB]
            if l == 0:
                nc.vector.scalar_tensor_tensor(out=dst, in0=ps, scalar=col["ca_bk"][:, 0:1], in1=hi,
                                               op0=ALU.add, op1=ALU.subtract).then_inc(z["k_res"], 1)
            else:
                nc.vector.tensor_tensor(dst, ps, hi, ALU.subtract).then_inc(z["k_res"], 1)

        def dve_qfix(dve, l, v, slot, rest):
            z = L[l]
            if rest:
                if slot != 3:
                    dve.wait_ge(s["q_rest"], 96 * (l + 1))
                dve.wait_ge(z["st_ps"], 12 * v - 36 + CREDIT)
            hf = slot % 2
            at = slice((v // 2) * PQ, (v // 2 + 1) * PQ) if isinstance(v, int) else bass.ds((v - hf) * S, PQ)
            nc.vector.tensor_copy(qfix[:, slot, :].rearrange("p (a n) -> p a n", n=PQ),
                                  Q[:, PAIRS * hf:PAIRS * (hf + 1), at]).then_inc(z["qfix_ok"], 1)

        def dve_row(dve, l, v, par, c, lead=False):
            z = L[l]
            dve.wait_ge(z["row_ps"], 12 * v + c + 1)
            if c == 0 and not (isinstance(v, int) and v < 2):
                dve.wait_ge(z["m_parts"], v - 1)
            nc.vector.tensor_reduce(mx[:, par, c // NKB, c % NKB:c % NKB + 1],
                                    row_bank(v, c, lead)[0:PQ, 0:KB],
                                    AX.X, ALU.max).then_inc(z["row_max"], 1)
            if c == 11:
                dve.wait_ge(z["row_max"], 12 * v + 12)
                nc.vector.tensor_reduce(row_top[:, par, :], mx[:, par, :, :], AX.X, ALU.max).then_inc(z["top_ok"], 1)

        def dve_comb(dve, l, v):
            z = L[l]
            dve.wait_ge(z["pv_ok"], 12 * v + 12 + CREDIT)
            nc.vector.tensor_scalar(o_first[:, :], OUT[:, 0:S], half_mask[:, 0:1], None, ALU.mult)\
                .then_inc(z["dve_o"], 1)
            dve.wait_ge(z["dve_o"], v + 1)
            dve.wait_ge(z["fin_ok"], v + CREDIT)
            nc.vector.scalar_tensor_tensor(out=comb[:, :], in0=OUT[:, S:PQ], scalar=half_mask[:, 1:2],
                                           in1=o_first[:, :], op0=ALU.mult, op1=ALU.add)\
                .then_inc(z["comb_ok"], 1)

        def dve_recip(dve, l, v, index):
            z = L[l]
            dve.wait_ge(z["bc_ps"], v + 1)
            nc.vector.reciprocal(rec[:, :], MISC[index % 2][:, 0:S]).then_inc(z["bc_ok"], 1)

        def norm_here(layer, n):
            return layer == 1 and not (isinstance(n, int) and n == 2)

        def dve_ss(dve, l, n):
            z = L[l]
            dve.wait_ge(z["sq_ok"], n + 1)
            nc.vector.tensor_reduce(key_ss[:, :], sq[:, :, :], AX.X, ALU.add).then_inc(z["ss_ok"], 1)

        def dve_attend(dve, link, l):
            for k in range(12 + LEAD):
                dve_row(dve, l, k // 12, k // 12, k % 12, lead=True)
                if k == 8:
                    dve.wait_ge(s["q_first"], 96 * (l + 1))
                    dve.wait_ge(L[l]["qfix_ok"], 1)
                    for v in (1, 2):
                        dve_qfix(dve, l, v, v, False)

            def body(j):
                last = isinstance(j, int) and j == 3
                k = 0
                for s_ in range(4):
                    got = items_of(l, j, s_)
                    u = 4 * j + s_
                    if s_ >= 1:
                        dve_comb(dve, l, u - 1)
                    if last and s_ == 3:
                        dve.wait_ge(s["y_early"], l + 1)
                        add_output(dve, link, l, MOST)
                    late = {}
                    for slot in range(13):
                        if slot < 12 and row_of(u, s_, slot):
                            v, v_slot, c = row_of(u, s_, slot)
                            dve_row(dve, l, v, v_slot % 2, c)
                        for kind, n, i, par, layer, index in late.get(slot, []):
                            if kind == "K":
                                dve_res(dve, layer, n, i, par, index)
                            if kind == "D":
                                dve_recip(dve, layer, n, index)
                        for item in got.get(slot, []):
                            if item[0] in "KD":
                                late.setdefault(slot + 1, []).append((*item, k))
                            k += 1
                        if slot == 5 and (not last or s_ == 0):
                            dve_qfix(dve, l, u + 3, (s_ + 3) % 4, True)
                        if slot == 10 and s_ in (0, 2):
                            layer, n = where(l, 2 * j + 3 + s_ // 2)
                            if norm_here(layer, n):
                                dve_ss(dve, layer, n)
                    if last and s_ == 2 and l == 0:
                        dve.wait_ge(L[l]["fin_ok"], U - 4 + CREDIT)
                        value_bias(dve, slice(0, (TT - 1) * TP))
                    if last and s_ == 3:
                        if l == 0:
                            link(normalise(dve, 2, MOST))
                        else:
                            scale_output(dve, link, 6, MOST)
                    if s_ == 3:
                        dve_comb(dve, l, u)
                        dve_recip(dve, l, u, k)
                        k += 1

            passes(dve, body, 2)

        POOL_M = 4

        def pool_mparts(pool, l, v, par):
            z = L[l]
            link = Chain(pool, z["pool_m"], POOL_M * v)
            pool.wait_ge(z["top_ok"], v + 1)
            if not (isinstance(v, int) and v < 2):
                pool.wait_ge(z["m_ps"], v - 1 + CREDIT)
            neg, rest = mt[:, 0, :], mt[:, 1, :]
            part = [mparts[:, par, :, i] for i in range(3)]
            link(nc.gpsimd.tensor_tensor(neg, zero[0:TP, 0:PAIRS], row_top[:, par, :], ALU.subtract))
            link(nc.gpsimd.tensor_tensor(part[0], zero[0:TP, 0:PAIRS], row_top[:, par, :], ALU.subtract))
            link(nc.gpsimd.tensor_tensor(rest, neg, part[0], ALU.subtract))
            link(nc.gpsimd.tensor_tensor(part[1], rest, zero[0:TP, 0:PAIRS], ALU.add))
            nc.gpsimd.tensor_tensor(part[2], rest, part[1], ALU.subtract).then_inc(z["m_parts"], 1)

        def pool_low(pool, l, n, i, par):
            z = L[l]
            pool.wait_ge(z["k_mid"], 3 * n + i + 1)
            cols = slice(i * KB, (i + 1) * KB)
            nc.gpsimd.tensor_tensor(kparts[:, par, 2, cols], k_rest[:, cols], kparts[:, par, 1, cols],
                                    ALU.subtract).then_inc(z["k_low"], 1)

        def pool_fin(pool, l, v, hf):
            z = L[l]
            pool.wait_ge(z["bc_ok"], v + 1 + CREDIT)
            if isinstance(v, int):
                dst = oT9[:, hf, (v // 2) * S:(v // 2 + 1) * S]
            else:
                dst = oT9[:, hf, bass.ds((v - hf) * (S // 2), S)]
            nc.gpsimd.tensor_tensor(dst, comb[:, :], rec[:, :], ALU.mult).then_inc(z["fin_ok"], 1)

        POOL_N = 4

        def pool_squares(pool, l, n, par):
            z = L[l]
            pool.wait_ge(z[f"ctx_in{par}"], 16 * (n // 2 + 1) if isinstance(n, int) else (n - par) * 8 + 16)
            tile = ctx_tile[:, par, :, :]
            nc.gpsimd.tensor_tensor(sq[:, :, :], tile, tile, ALU.mult).then_inc(z["sq_ok"], 1)

        def pool_norm(pool, l, n, par):
            z = L[l]
            link = Chain(pool, z["pool_n"], POOL_N * n)
            tile = ctx_tile[:, par, :, :]
            pool.wait_ge(z["ss_ok"], n + 1)
            link(nc.gpsimd.tensor_tensor(key_rs[:, :], key_ss[:, :], inv_d[0:KP, :], ALU.mult))
            link(nc.gpsimd.tensor_tensor(key_rs[:, :], key_rs[:, :], rms_eps[0:KP, :], ALU.add))
            link(nc.gpsimd.tensor_tensor(key_rs[:, :], key_rs[:, :], neghalf[0:KP, :], ALU.pow))
            mask = mask_col[:, n, :] if isinstance(n, int) else \
                mask_col[:, bass.ds(n, 1), :].rearrange("p o c -> p (o c)")
            link(nc.gpsimd.tensor_tensor(key_rs[:, :], key_rs[:, :], mask, ALU.mult))
            nc.gpsimd.tensor_tensor(tile, tile, wide(key_rs[:, :], 128, 2), ALU.mult).then_inc(z["ctx_ok"], 1)

        def pool_attend(pool, link, l):
            pool_mparts(pool, l, 0, 0)

            def body(j):
                last = isinstance(j, int) and j == 3
                for s_ in range(4):
                    u = 4 * j + s_
                    layer_n, m = where(l, 2 * j + 3 + s_ // 2)
                    if s_ in (0, 2) and norm_here(layer_n, m):
                        pool_squares(pool, layer_n, m, s_ // 2 ^ 1)
                    if s_ in (1, 3) and norm_here(layer_n, m):
                        pool_norm(pool, layer_n, m, s_ // 2 ^ 1)
                    if s_ >= 1:
                        pool_fin(pool, l, u - 1, (s_ - 1) % 2)
                    if last and s_ == 3:
                        pool_rstd(pool, link, (2, 6)[l], (1.0, 1.0 / D)[l], (1e-5, 1e-6)[l], MOST)
                    layer, n = where(l, 2 * j + 2 + s_ // 2)
                    if not (last and s_ == 3):
                        pool_mparts(pool, l, u + 1, (s_ + 1) % 2)
                    for i in range(3) if s_ in (0, 2) and layer < 2 else ():
                        pool_low(pool, layer, n, i, (s_ // 2) % 2)
                pool_fin(pool, l, 4 * j + 3, 1)

            passes(pool, body, 2)

        KREP_INC = [16 * NPROD, 16 * (NPROD + 1)]

        def sp_ctx(sp, l, n, par):
            z = L[l]
            src = a["ctx_1024"][n] if isinstance(n, int) else \
                a["ctx_1024"][bass.ds(n, 1)].rearrange("o k d -> (o k) d")
            sp.dma_start(ctx_tile[:, par, :, :], src.rearrange("(p c) d -> p c d", c=KC))\
                .then_inc(z[f"ctx_in{par}"], 16)

        def k_dram(l, n):
            return k_scratch[l][n] if isinstance(n, int) else \
                k_scratch[l][bass.ds(n, 1)].rearrange("o r p n -> (o r) p n")

        def sp_kwrite(sp, l, n, par):
            z = L[l]
            sp.wait_ge(z["k_low"], 3 * n + 3)
            sp.dma_start(k_dram(l, n).rearrange("r p n -> p r n"), kparts[:, par, :, :]).then_inc(z[f"kw{par}"], 16)

        def sp_krep(sp, l, v, slot, n, par):
            z = L[l]
            hf = slot % 2
            sp.wait_ge(z[f"kw{par}"], 16 * (n // 2 + 1) if isinstance(n, int) else (n - par) * 8 + 16)
            if not (isinstance(v, int) and v < 4):
                sp.wait_ge(z["st_ps"], 12 * v - 36 + CREDIT)
            elif l == 1:
                sp.wait_ge(L[0]["st_ps"], 12 * (v + U) - 36 + CREDIT)
            src = k_dram(l, n)
            for r in range(NPROD):
                sp.dma_start(krep[PR * r:PR * (r + 1), slot, :, 0:SK],
                             src[KPARTS[r], 64 * hf:64 * hf + 64, :].rearrange("(a x) n -> x a n", x=PR))\
                    .then_inc(z[f"krep{slot}"], 16)
            if l == 1:
                m = mask_scratch[n:n + 1] if isinstance(n, int) else mask_scratch[bass.ds(n, 1)]
                sp.dma_start(krep[MROW + 3:MROW + 4, slot, :, 0:SK], m).then_inc(z[f"krep{slot}"], 16)

        def sp_prepare(sp):
            z = L[0]
            sp.wait_ge(z["t_ps"], 3)
            sp_ctx(sp, 0, 2, 0)
            sp.wait_ge(s["zeros_ok"], 4)
            sp_kwrite(sp, 0, 0, 0)
            sp_krep(sp, 0, 0, 0, 0, 0)
            sp_krep(sp, 0, 1, 1, 0, 0)
            sp.wait_ge(z["t_ps"], 6)
            sp_ctx(sp, 0, 3, 1)
            sp_kwrite(sp, 0, 1, 1)
            sp_krep(sp, 0, 2, 2, 1, 1)

        def sp_attend(sp, l):
            def context(n, par):
                layer, b = where(l, n)
                if layer < 2:
                    before, last_b = where(l, n - 2)
                    sp.wait_ge(L[before]["t_ps"], 3 * last_b + 3)
                    sp_ctx(sp, layer, b, par)

            def body(j):
                sp_krep(sp, l, 4 * j + 3, 3, 2 * j + 1, 1)
                layer, n = where(l, 2 * j + 2)
                if layer == 2:
                    return
                v = n * HALVES
                context(2 * j + 4, 0)
                sp_kwrite(sp, layer, n, 0)
                sp_krep(sp, layer, v, 0, n, 0)
                sp_krep(sp, layer, v + 1, 1, n, 0)
                context(2 * j + 5, 1)
                sp_kwrite(sp, layer, n + 1, 1)
                sp_krep(sp, layer, v + 2, 2, n + 1, 1)

            passes(sp, body, 2)


        def pe_xT(pe, src, k):
            for t in range(TT):
                ins = nc.tensor.transpose(bank[0][:, t * TP:(t + 1) * TP], src[:, t, :], cst[0:TP, C_ID:C_ID + TP])
            ins.then_inc(s["xT_ps"], 1)

        def act_xT(act, k, gain=None, bias=None):
            act.wait_ge(s["xT_ps"], k + 1)
            if gain is None:
                nc.scalar.copy(xT[:, :], bank[0][:, 0:TOK]).then_inc(s["xT_ok"], 1)
            else:
                nc.scalar.activation(xT[:, :], bank[0][:, 0:TOK], ACT.Identity, bias=col[bias][:, 0:1],
                                     scale=col[gain][:, 0:1]).then_inc(s["xT_ok"], 1)

        ALL, MOST, LAST = (0, TT), (0, TT - 1), (TT - 1, TT)

        def moments(dve, link, tiles):
            for t in range(*tiles):
                ins = nc.vector.bn_stats(stats[:, t, :], x_new[:, t, :])
            link(ins)
            for t in range(*tiles):
                ins = nc.vector.bn_aggr(mv[:, t, :], stats[:, t, :])
            ins.then_inc(s["var_ok"], 1)

        def normalise(dve, k, tiles):
            dve.wait_ge(s["rstd_ok"], k)
            for t in range(*tiles):
                ins = nc.vector.tensor_scalar(x_new[:, t, :], x_new[:, t, :], mv[:, t, 0:1], rstd[:, t:t + 1],
                                              ALU.subtract, ALU.mult)
            return ins

        def residual(dve, link, g, b, k):
            dve.wait_ge(s["x_ok"], k)
            link(nc.vector.tensor_tensor(x_res[:, :, :], x_new[:, :, :], wide(g[:, :], TT, 1), ALU.mult))
            link(nc.vector.tensor_tensor(x_res[:, :, :], x_res[:, :, :], wide(b[:, :], TT, 1), ALU.add))

        def sumsq(dve, link, tiles):
            at = slice(*tiles)
            link(nc.vector.tensor_tensor(x_new[:, at, :], x_res[:, at, :], x_res[:, at, :], ALU.mult))
            nc.vector.tensor_reduce(mv[:, at, 1], x_new[:, at, :], AX.X, ALU.add).then_inc(s["var_ok"], 1)

        def add_output(dve, link, l, tiles):
            at = slice(*tiles)
            if l == 0:
                link(nc.vector.tensor_tensor(x_new[:, at, :], Y[:, at, :], x_res[:, at, :], ALU.add))
                moments(dve, link, tiles)
            else:
                link(nc.vector.tensor_tensor(x_res[:, at, :], Y[:, at, :], x_res[:, at, :], ALU.add))
                sumsq(dve, link, tiles)

        def scale_output(dve, link, k, tiles):
            at, n = slice(*tiles), tiles[1] - tiles[0]
            dve.wait_ge(s["rstd_ok"], k)
            link(nc.vector.tensor_tensor(x_new[:, at, :], x_res[:, at, :], wide(rstd[:, at], 128, 2), ALU.mult))
            nc.vector.tensor_tensor(x_new[:, at, :], x_new[:, at, :], wide(bc["g_out"][:, :], n, 1), ALU.mult)\
                .then_inc(s["x_ok"], 1)

        def pool_rstd(pool, link, k, scale, eps, tiles=(0, TT)):
            at = slice(*tiles)
            pool.wait_ge(s["var_ok"], k)
            link(nc.gpsimd.tensor_scalar(rstd[:, at], mv[:, at, 1], scale, eps, ALU.mult, ALU.add))
            nc.gpsimd.tensor_tensor(rstd[:, at], rstd[:, at], neghalf[0:TP, at], ALU.pow)\
                .then_inc(s["rstd_ok"], 1)

        Q_CHUNKS = ((0, 2), (2, B))

        def pair_rows(r, hh, lo, hi):
            return (q_wide[:, r, lo:hi, hh, :],
                    q_part[:, r, lo * S:hi * S].rearrange("p (b q) -> p b q", q=S))

        def dve_qparts(dve, link, l):
            lo, hi = Q_CHUNKS[0]
            cols = slice(lo * S, hi * S)
            rest = qsplit[:, cols]

            def part(r, write):
                write.then_inc(s["q_part"], 1)
                dve.wait_ge(s["q_part"], 3 * l + r + 1)
                nc.vector.tensor_scalar(*pair_rows(r, 0, lo, hi), pair_mask[:, 0:1], None, ALU.mult)\
                    .then_inc(s["q_even"], 1)

            dve.wait_ge(s["q_sb"], l + 1)
            part(0, nc.vector.tensor_copy(q_part[:, 0, cols], rest))
            link(nc.vector.tensor_tensor(rest, rest, q_part[:, 0, cols], ALU.subtract))
            part(1, nc.vector.tensor_copy(q_part[:, 1, cols], rest))
            part(2, nc.vector.tensor_tensor(q_part[:, 2, cols], rest, q_part[:, 1, cols], ALU.subtract))

        def pool_qparts(pool, link, l):
            lo, hi = Q_CHUNKS[1]
            cols = slice(lo * S, hi * S)
            rest = qsplit[:, cols]
            none = zero[:, 0:1].to_broadcast([128, (hi - lo) * S])
            pool.wait_ge(s["q_sb"], l + 1)
            nc.gpsimd.tensor_tensor(q_part[:, 0, cols], rest, none, ALU.add).then_inc(s["q_part_b"], 1)
            pool.wait_ge(s["q_part_b"], 3 * l + 1)
            link(nc.gpsimd.tensor_tensor(rest, rest, q_part[:, 0, cols], ALU.subtract))
            nc.gpsimd.tensor_tensor(q_part[:, 1, cols], rest, none, ALU.add).then_inc(s["q_part_b"], 1)
            pool.wait_ge(s["q_part_b"], 3 * l + 2)
            nc.gpsimd.tensor_tensor(q_part[:, 2, cols], rest, q_part[:, 1, cols], ALU.subtract)\
                .then_inc(s["q_part_b"], 1)

        def act_qparts(act, l):
            act.wait_ge(s["q_ps"], l + 1)
            if l == 0:
                nc.scalar.activation(qsplit, bank[1][:, 0:TOK], ACT.Identity, bias=col["ca_bq"][:, 0:1])\
                    .then_inc(s["q_sb"], 1)
            else:
                nc.scalar.copy(qsplit, bank[1][:, 0:TOK]).then_inc(s["q_sb"], 1)
            for r in range(3):
                act.wait_ge(s["q_part"], 3 * l + r + 1)
                nc.scalar.activation(*pair_rows(r, 1, *Q_CHUNKS[0]), ACT.Copy, scale=pair_mask[:, 1:2])\
                    .then_inc(s["q_odd"], 1)
            act.wait_ge(s["q_rows"], 16)
            nc.scalar.copy(qfix[96:100, 0, :].rearrange("p (a n) -> p a n", n=PQ), Q[96:100, 0:PAIRS, 0:PQ])
            act.wait_ge(s["q0_ps"], l + 1)
            nc.scalar.copy(qfix[0:MROW, 0, :], bank[0][0:MROW, 0:UQ]).then_inc(L[l]["qfix_ok"], 1)
            for r in range(3):
                act.wait_ge(s["q_part_b"], 3 * l + r + 1)
                for hh, name in enumerate(("q_even_b", "q_odd_b")):
                    nc.scalar.activation(*pair_rows(r, hh, *Q_CHUNKS[1]), ACT.Copy, scale=pair_mask[:, hh:hh + 1])\
                        .then_inc(s[name], 1)

        def pe_first_queries(pe, l):
            pe.wait_ge(s["selq_ok"], 1)
            pe.wait_ge(s["q_even"], 3 * l + 3)
            pe.wait_ge(s["q_odd"], 3 * l + 3)
            for p in range(PAIRS):
                for i in range(3):
                    ins = nc.tensor.matmul(bank[0][0:MROW, p * PQ:(p + 1) * PQ], selq[:, i, p, :],
                                           q_wide[:, i, 0].rearrange("p h q -> p (h q)"),
                                           start=(i == 0), stop=(i == 2))
            ins.then_inc(s["q0_ps"], 1)

        def sp_qparts(sp, l):
            for n, (lo, hi) in enumerate(Q_CHUNKS):
                cols = slice(lo * PQ, hi * PQ)
                for r in range(3):
                    sp.wait_ge(s[("q_even", "q_even_b")[n]], 3 * l + r + 1)
                    sp.wait_ge(s[("q_odd", "q_odd_b")[n]], 3 * l + r + 1)
                    sp.dma_start(q_scratch[l][r, :, cols], q_wide[:, r, lo:hi].rearrange("p b h q -> p (b h q)"))\
                        .then_inc(s[f"q_written{r}"], 16)
                if l == 1:
                    sp.wait_ge(L[0]["qfix_ok"], U)
                for part in range(3):
                    sp.wait_ge(s[f"q_written{part}"], 16 * (2 * l + n + 1))
                    for r in range(NPROD):
                        if QPARTS[r] == part:
                            sp.dma_start(Q[PR * r:PR * (r + 1), :, cols],
                                         q_scratch[l][part, :, cols].rearrange("(a x) n -> x a n", x=PR))\
                                .then_inc(s[("q_first", "q_rest")[n]], 16)

        def pe_project(pe, lhs, w, tiles):
            for t in tiles:
                for i in range(len(lhs)):
                    ins = nc.tensor.matmul(bank[1][0:TP, t * 128:(t + 1) * 128], lhs[i][:, t * TP:(t + 1) * TP],
                                           w[i], start=(i == 0), stop=(i == len(lhs) - 1))
            return ins

        def project_heads(pe, l, tiles):
            return pe_project(pe, [oT9[:, hf, :] for hf in range(HALVES)],
                              [wo9[l][:, hf, :] for hf in range(HALVES)], tiles)

        def value_bias(dve, cols):
            for hf in range(HALVES):
                ins = nc.vector.tensor_scalar(oT9[:, hf, cols], oT9[:, hf, cols], bv9[:, hf:hf + 1], None, ALU.add)
            ins.then_inc(s["oT_ok"], 1)

        Y = bank[1][0:TP, :].rearrange("p (t d) -> p t d", t=TT)

        def sp_expert(sp, e, r):
            if isinstance(e, int):
                s1, s2 = a["L0_xattn_e_w1"][e], a["L0_xattn_e_w2"][e]
            else:
                s1 = a["L0_xattn_e_w1"][bass.ds(e, 1)].rearrange("o d f -> (o d) f")
                s2 = a["L0_xattn_e_w2"][bass.ds(e, 1)].rearrange("o f d -> (o f) d")
            sp.dma_start(w1[:, r, :], s1).then_inc(s[f"w_in{r}"], 16)
            sp.dma_start(w2[:, r, :, :], s2.rearrange("(f p) d -> p f d", p=128)).then_inc(s[f"w_in{r}"], 16)

        def sp_experts_first(sp):
            for e in range(2):
                sp_expert(sp, e, e)

        def sp_experts(sp):
            with sp.Fori(0, E // 2 - 1) as i:
                for r in range(2):
                    sp.wait_ge(s["y_part"], 8 * i + 4 * r + 4)
                    sp_expert(sp, 2 * i + 2 + r, r)

        @block.sync
        def _(sp):
            sp.dma_start(cst[:, :], a["consts"]).then_inc(s["in_cst"], 16)
            sp.dma_start(x_res[:, :, :], a["x"].rearrange("b q d -> (b q) d").rearrange("(t p) d -> p t d", p=TP))\
                .then_inc(s["in_x"], 16)
            for n in ("sa_wq", "sa_wk", "sa_wv", "sa_wo"):
                sp.dma_start(W[n][:, :], a["L0_xattn_" + n]).then_inc(s["in_sa"], 16)
            for n in ("sa_bq", "sa_bk", "sa_bv"):
                sp.dma_start(col[n][:, :], a["L0_xattn_" + n].rearrange("(p o) -> p o", o=1)).then_inc(s["in_sa"], 16)
            sp_ctx(sp, 0, 0, 0)
            sp.dma_start(k_rest[:, 0:3 * PAIRS * MROW], a["selq"]).then_inc(s["in_selq"], 16)
            sp_ctx(sp, 0, 1, 1)
            for n in ("ca_wq", "ca_wk", "ca_wv"):
                sp.dma_start(W[n][:, :], a["L0_xattn_" + n]).then_inc(s["in_pipe"], 16)
            for n in ("ca_bq", "ca_bk"):
                sp.dma_start(col[n][:, :], a["L0_xattn_" + n].rearrange("(p o) -> p o", o=1))\
                    .then_inc(s["in_pipe"], 16)
            for n in ("Wq", "Wk", "Wv"):
                sp.dma_start(W["l1_" + n.lower()][:, :], a["L1_xattn_" + n]).then_inc(s["in_tail"], 16)
            for n in ("g_q", "g_c"):
                sp.dma_start(col[n][:, :], a["L1_xattn_" + n].rearrange("(p o) -> p o", o=1))\
                    .then_inc(s["in_tail"], 16)
            sp.dma_start(mask_col8[:, :, :], a["mask_col"]).then_inc(s["in_mask"], 16)
            sp.dma_start(mask_row8[:, :], a["mask_row"]).then_inc(s["in_mask"], 16)
            for n in ("ln1_g", "ln1_b", "ln2_g", "ln2_b"):
                sp.dma_start(col[n][:, :], a["L0_xattn_" + n].rearrange("(p o) -> p o", o=1)).then_inc(s["in_wo"], 16)
            for n in ("sa_bo", "ca_bo", "ln1_g", "ln1_b", "ln2_g", "ln2_b", "ln3_g", "ln3_b"):
                sp.dma_start(bc[n][:, :], a["L0_xattn_" + n].rearrange("(o d) -> o d", o=1).to_broadcast([TP, 128]))\
                    .then_inc(s["in_wo"], 16)
            sp.dma_start(bc["g_out"][:, :], a["L1_xattn_g_out"].rearrange("(o d) -> o d", o=1)
                         .to_broadcast([TP, 128])).then_inc(s["in_wo"], 16)
            for l in range(2):
                sp.dma_start(wo9[l][:, :, :], a[f"wo9_{l}"]).then_inc(s["in_wo"], 16)
            sp.dma_start(bv9[:, :], a["bv9"]).then_inc(s["in_wo"], 16)
            sp.dma_start(rw[:, :], a["L0_xattn_router_w"]).then_inc(s["in_wo"], 16)
            sp.dma_start(rb[:, :], a["L0_xattn_router_b"].rearrange("(o d) -> o d", o=1).to_broadcast([TP, E]))\
                .then_inc(s["in_wo"], 16)
            sp.dma_start(b1T[:, :], a["b1T"]).then_inc(s["in_wo"], 16)
            sp.dma_start(b2[:, :], a["L0_xattn_e_b2"]).then_inc(s["in_wo"], 16)
            sp_prepare(sp)
            sp.wait_ge(s["krow_ok"], 1)
            sp.dma_start(Q[MROW:MROW + 4, :, :].rearrange("p a n -> p (a n)").rearrange("p (u n) -> p u n", n=UQ),
                         wide(qrows[:, :], U, 1)).then_inc(s["q_rows"], 16)
            sp.wait_ge(s["mask_ok"], 1)
            sp.dma_start(mask_scratch, wide(mask_row, PAIRS, 1)).then_inc(s["mask_written"], 16)
            sp_qparts(sp, 0)
            sp_experts_first(sp)
            sp.wait_ge(s["mask_written"], 16)
            sp_attend(sp, 0)

            sp_experts(sp)
            sp_qparts(sp, 1)
            sp_attend(sp, 1)
            tiles_out = out.rearrange("b q d -> (b q) d").rearrange("(t p) d -> p t d", p=TP)
            for k, tiles in ((5, MOST), (6, LAST)):
                at = slice(*tiles)
                sp.wait_ge(s["x_ok"], k)
                sp.dma_start(tiles_out[:, at, :], x_new[:, at, :]).then_inc(s["out_done"], 16)
            sp.wait_ge(s["out_done"], 32)

        @block.tensor
        def _(pe):
            give_credits(pe, "pe")
            pe.wait_ge(s["in_cst"], 16)
            pe.wait_ge(s["in_x"], 16)
            pe_xT(pe, x_res, 0)
            pe.wait_ge(s["in_sa"], 16 * 7)
            pe.wait_ge(s["xT_ok"], 1)
            nc.tensor.matmul(bank[1][:, 0:TOK], W["sa_wq"][:, :], xT[:, :], start=True, stop=True)\
                .then_inc(s["sa_proj"], 1)
            nc.tensor.matmul(bank[2][:, 0:TOK], W["sa_wk"][:, :], xT[:, :], start=True, stop=True)\
                .then_inc(s["sa_proj"], 1)
            for h in range(2):
                for i in range(4):
                    b = 4 * h + i
                    ins = nc.tensor.matmul(bank[3 + h][0:S, i * 128:(i + 1) * 128], xT[:, b * S:(b + 1) * S],
                                           W["sa_wv"][:, :], start=True, stop=True)
                ins.then_inc(s["sa_proj"], 1)
            pe.wait_ge(s["in_pipe"], 16 * 5)
            pe.wait_ge(s["vb_zero"], 2)

            def scores(b):
                r = b % 2
                pe.wait_ge(s["qbd_ok"], b + 1)
                if b >= 2:
                    pe.wait_ge(s["s_max"], b - 1)
                for t in range(7):
                    ins = nc.tensor.matmul(
                        bank[1 + r][:, t * S:(t + 1) * S],
                        qbd[:, r].rearrange("p h q -> p (h q)")[:, t * 128:(t + 1) * 128],
                        kT[:, b * S:(b + 1) * S], start=True, stop=True)
                ins.then_inc(s["s_ps"], 1)

            def transposes(b):
                pe.wait_ge(s["s_norm"], b + 1)
                if b >= 1:
                    pe.wait_ge(s["pt_ok"], 2 * b)
                for h, n in enumerate((4, 3)):
                    for t in range(n):
                        at = (4 * h + t) * S
                        ins = nc.tensor.transpose(bank[3 + h][:, t * 128:(t + 1) * 128],
                                                  weights[:, b % 2, at:at + 128], ident)
                    ins.then_inc(s["pt_ps"], 1)

            def outputs(b):
                r = b % 2
                pe.wait_ge(s["vb_ok"], b + 1)
                pe.wait_ge(s["pt_ok"], 2 * b + 2)
                if b >= 1:
                    pe.wait_ge(s["sa_om"], b)
                for g in range(4):
                    ins = nc.tensor.matmul(bank[5][32 * g:32 * g + 32, 0:4 * S], vb[:, r, 32 * g:32 * g + 32],
                                           pT[:, r, g * 4 * S:(g + 1) * 4 * S], start=True, stop=True)
                ins.then_inc(s["sa_o"], 1)

            def item(k):
                pe_item(pe, PROLOGUE[k], k, PROLOGUE[k - 2] if k >= 2 else None)

            pe.wait_ge(s["kT_ok"], 1)
            scores(0)
            scores(1)
            for b in range(B):
                if b + 2 < B:
                    scores(b + 2)
                item(2 * b)
                if b >= 1:
                    outputs(b - 1)
                transposes(b)
                if 2 * b + 1 < len(PROLOGUE) - 1:
                    item(2 * b + 1)
            pe.wait_ge(s["oT_ok"], 1)
            pe.wait_ge(s["s_max"], B - 1)
            pe_project(pe, [oT], [W["sa_wo"][:, :]], range(TT // 2))
            outputs(B - 1)
            pe.wait_ge(s["oT_ok"], 2)
            pe_project(pe, [oT], [W["sa_wo"][:, :]], range(TT // 2, TT)).then_inc(s["y_ps"], 1)
            pe.wait_ge(s["x_ok"], 1)
            pe_xT(pe, x_new, 1)
            pe.wait_ge(s["xT_ok"], 2)
            nc.tensor.matmul(bank[1][:, 0:TOK], W["ca_wq"][:, :], xT[:, :], start=True, stop=True)\
                .then_inc(s["q_ps"], 1)
            pe_first_queries(pe, 0)
            pe.wait_ge(s["q_sb"], 1)
            pe.wait_ge(s["wg_ok"], 3)
            pe_attend(pe, 0)
            pe.wait_ge(s["oT_ok"], 4)
            project_heads(pe, 0, [TT - 1]).then_inc(s["y_ps"], 1)
            pe.wait_ge(s["x_ok"], 2)
            pe_xT(pe, x_new, 2)
            pe.wait_ge(s["xT_ok"], 3)
            def hidden(i, k):
                if k % 4 == 0:
                    pe.wait_ge(s[f"w_in{k // 4}"], 32 * i + 32)
                nc.tensor.matmul(bank[k % 4][:, 0:TOK], w1[:, k // 4, (k % 4) * 128:(k % 4 + 1) * 128],
                                 xT[:, :], start=True, stop=True).then_inc(s["h_ps"], 1)

            def second(i, k):
                if k % 4 == 0:
                    pe.wait_ge(s["y_used"], 2 * i + k // 4 - 1 + 2 * CREDIT)
                pe.wait_ge(s["h_act"], 8 * i + k + 1)
                for t in range(TT):
                    ins = nc.tensor.matmul(bank[4 + k // 4][0:TP, t * 128:(t + 1) * 128],
                                           hid[:, k % 4, t * TP:(t + 1) * TP], w2[:, k // 4, k % 4, :],
                                           start=(k % 4 == 0 and t == 0), stop=(k % 4 == 3), skip_group_check=True)
                ins.then_inc(s["y_part"], 1)

            hidden(0, 0)
            for t in range(TT):
                ins = nc.tensor.matmul(bank[7][0:TP, t * E:(t + 1) * E], xT[:, t * TP:(t + 1) * TP], rw[:, :],
                                       start=True, stop=True)
            ins.then_inc(s["rt_ps"], 1)
            hidden(0, 1)
            with pe.Fori(0, E // 2 - 1) as i:
                for k in range(8):
                    second(i, k)
                    hidden(i + (k + 2) // 8, (k + 2) % 8)
            last = E // 2 - 1
            pe.wait_ge(s["gate_ok"], 1)
            for t in range(TT):
                ins = nc.tensor.transpose(bank[6][0:E, t * TP:(t + 1) * TP], logit[:, t, :],
                                          cst[0:TP, C_ID:C_ID + TP])
            ins.then_inc(s["gT_ps"], 1)
            for k in range(8):
                second(last, k)
                if k < 6:
                    hidden(last, k + 2)
                if k == 3:
                    pe.wait_ge(s["gT_ok"], 1)
                    for t in range(TT):
                        ins = nc.tensor.matmul(bank[7][0:TP, t * 128:(t + 1) * 128], gateT[:, t * TP:(t + 1) * TP],
                                               b2[:, :], start=True, stop=True)
                    ins.then_inc(s["b2_ps"], 1)
            pe.wait_ge(s["x_ok"], 4)
            pe_xT(pe, x_new, 3)
            pe.wait_ge(s["xT_ok"], 4)
            nc.tensor.matmul(bank[1][:, 0:TOK], W["l1_wq"][:, :], xT[:, :], start=True, stop=True)\
                .then_inc(s["q_ps"], 1)
            pe_first_queries(pe, 1)
            pe.wait_ge(s["q_sb"], 2)
            pe_attend(pe, 1)
            pe.wait_ge(L[1]["fin_ok"], U + CREDIT)
            project_heads(pe, 1, [TT - 1]).then_inc(s["y_ps"], 1)

        @block.scalar
        def _(act):
            act_xT(act, 0)
            act.wait_ge(s["in_sa"], 16 * 7)
            act.wait_ge(s["sa_proj"], 1)
            nc.scalar.activation(qT[:, :], bank[1][:, 0:TOK], ACT.Identity, bias=col["sa_bq"][:, 0:1])\
                .then_inc(s["qT_ok"], 1)
            act.wait_ge(s["sa_proj"], 2)
            nc.scalar.activation(kT[:, :], bank[2][:, 0:TOK], ACT.Identity, bias=col["sa_bk"][:, 0:1])\
                .then_inc(s["kT_ok"], 1)
            for h in range(2):
                act.wait_ge(s["sa_proj"], 3 + h)
                nc.scalar.copy(v_all[:, 4 * h:4 * h + 4, :].rearrange("p b d -> p (b d)"), bank[3 + h][0:S, :])\
                    .then_inc(s["v_ok"], 1)
            act.wait_ge(s["zeros_ok"], 4)
            act.wait_ge(s["in_pipe"], 16 * 5)
            act.wait_ge(s["vb_zero"], 2)

            def exp(b):
                act.wait_ge(s["pre_ok"], b + 1)
                rows = sc[:, b % 2].rearrange("p t k -> p (t k)")
                nc.scalar.activation(rows, rows, ACT.Exp, scale=SCALE).then_inc(s["s_exp"], 1)

            def values(b):
                if b >= 2:
                    act.wait_ge(s["sa_o"], b - 1)
                nc.scalar.copy(vb[0:S, b % 2, :], v_all[:, b, :]).then_inc(s["vb_ok"], 1)

            def transposed(b):
                for h, n in enumerate((512, 384)):
                    act.wait_ge(s["pt_ps"], 2 * b + h + 1)
                    nc.scalar.copy(pT[:, b % 2, 512 * h:512 * h + n], bank[3 + h][:, 0:n]).then_inc(s["pt_ok"], 1)

            def item(k):
                act_item(act, PROLOGUE[k], k)
                if k and PROLOGUE[k - 1][0] == "K":
                    act_mid(act, 0, *PROLOGUE[k - 1][1:4])

            act.wait_ge(s["v_ok"], 2)
            act.wait_ge(s["in_selq"], 16)
            nc.scalar.copy(selq[:, :, :, :].rearrange("p i a n -> p (i a n)"), k_rest[:, 0:3 * PAIRS * MROW])\
                .then_inc(s["selq_ok"], 1)
            exp(0)
            exp(1)
            for b in range(B):
                values(b)
                item(2 * b)
                transposed(b)
                if b + 2 < B:
                    exp(b + 2)
                if 2 * b + 1 < len(PROLOGUE) - 1:
                    item(2 * b + 1)
            act.wait_ge(s["in_wo"], 16 * IN_WO)
            act_xT(act, 1, "ln1_g", "ln1_b")
            act_qparts(act, 0)
            act_attend(act, 0)
            act_xT(act, 2, "ln2_g", "ln2_b")
            act.wait_ge(s["rt_ok"], 1)
            nc.scalar.activation(prob[:, :, :], logit[:, :, :], ACT.Exp).then_inc(s["rt_exp"], 1)
            def gelu(i, k):
                v = 8 * i + k
                act.wait_ge(s["h_ps"], v + 1)
                bias = b1T[:, v:v + 1] if isinstance(v, int) else b1T[:, bass.ds(v, 1)]
                nc.scalar.activation(hid[:, k % 4, :], bank[k % 4][:, 0:TOK], ACT.Gelu, bias=bias)\
                    .then_inc(s["h_act"], 1)

            with act.Fori(0, E // 2 - 1) as i:
                for k in range(8):
                    gelu(i, k)
            for k in range(8):
                gelu(E // 2 - 1, k)
                if k == 2:
                    act.wait_ge(s["gT_ps"], 1)
                    nc.scalar.copy(gateT, bank[6][0:E, 0:TOK]).then_inc(s["gT_ok"], 1)
            act_xT(act, 3)
            act_qparts(act, 1)
            act_attend(act, 1)

        @block.vector
        def _(dve):
            give_credits(dve, "dve")
            link = Chain(dve, s["dve_c"])
            nc.vector.memset(krep[96:128, :, :, :].rearrange("p s a n -> p (s a n)").bitcast(F32), TWO_ONES)\
                .then_inc(s["zeros_ok"], 1)
            dve.wait_ge(s["in_cst"], 16)
            nc.vector.tensor_copy(identb[:, :], ident).then_inc(s["identb_ok"], 1)
            dve.wait_ge(s["zeros_ok"], 4)
            dve.wait_ge(s["in_pipe"], 16 * 5)
            def shifted(b):
                rows, top = sc[:, b % 2], row_m[:, b % 2, :]
                if b >= 2:
                    dve.wait_ge(s["s_norm"], b - 1)
                dve.wait_ge(s["s_ps"], b + 1)
                ps = bank[1 + b % 2][:, 0:7 * S].rearrange("p (t k) -> p t k", k=S)
                nc.vector.tensor_tensor(
                    rows, ps, cst[:, C_CAUSAL:C_LANE].rearrange("p (t k) -> p t k", k=S), ALU.add)\
                    .then_inc(s["s_max"], 1)
                dve.wait_ge(s["s_max"], b + 1)
                nc.vector.tensor_reduce(top, rows, AX.X, ALU.max).then_inc(s["row_m_ok"], 1)
                dve.wait_ge(s["row_m_ok"], b + 1)
                nc.vector.tensor_tensor(rows, rows, wide(top, S, 2), ALU.subtract).then_inc(s["pre_ok"], 1)

            def normalised(b):
                rows, total, inverse = sc[:, b % 2], row_s[:, b % 2, :], row_m[:, b % 2, :]
                dve.wait_ge(s["s_exp"], b + 1)
                nc.vector.tensor_reduce(total, rows, AX.X, ALU.add).then_inc(s["sum_ok"], 1)
                dve.wait_ge(s["sum_ok"], 2 * b + 1)
                nc.vector.reciprocal(inverse, total).then_inc(s["sum_ok"], 1)
                dve.wait_ge(s["sum_ok"], 2 * b + 2)
                if b >= 2:
                    dve.wait_ge(s["pt_ps"], 2 * b - 2)
                nc.vector.tensor_tensor(weights[:, b % 2, 0:7 * S].rearrange("p (t k) -> p t k", k=S), rows,
                                        wide(inverse, S, 2), ALU.mult).then_inc(s["s_norm"], 1)

            def own_lanes(b):
                dve.wait_ge(s["sa_o"], b + 1)
                nc.vector.tensor_tensor(om[:, b], bank[5][:, 0:4 * S].rearrange("p (i q) -> p i q", q=S),
                                        wide(cst[:, C_LANE:C_LANE + 4], S, 2), ALU.mult).then_inc(s["sa_om"], 1)

            def half_outputs(h):
                bs, cols = slice(h * B // 2, (h + 1) * B // 2), slice(h * TOK // 2, (h + 1) * TOK // 2)
                dve.wait_ge(s["sa_om"], (h + 1) * B // 2)
                link(nc.vector.tensor_reduce(oT[:, cols].rearrange("p (b q) -> p b q", q=S),
                                             om[:, bs].rearrange("p b i q -> p b q i"), AX.X, ALU.add))
                nc.vector.tensor_scalar(oT[:, cols], oT[:, cols], col["sa_bv"][:, 0:1], None, ALU.add)\
                    .then_inc(s["oT_ok"], 1)

            dve.wait_ge(s["selq_ok"], 1)
            shifted(0)
            shifted(1)
            for b in range(B):
                normalised(b)
                if b + 2 < B:
                    shifted(b + 2)
                if b >= 1:
                    own_lanes(b - 1)
                if b == B // 2 + 1:
                    half_outputs(0)
                for k in (2 * b, 2 * b + 1):
                    if PROLOGUE[k][0] == "K":
                        dve_res(dve, 0, *PROLOGUE[k][1:4], k)
            own_lanes(B - 1)
            half_outputs(1)
            dve.wait_ge(s["in_wo"], 16 * IN_WO)
            dve.wait_ge(s["bias_ok"], 2)
            dve.wait_ge(s["y_ps"], 1)
            link(nc.vector.tensor_tensor(x_new[:, :, :], Y, x_res[:, :, :], ALU.add))
            moments(dve, link, ALL)
            normalise(dve, 1, ALL).then_inc(s["x_ok"], 1)
            residual(dve, link, bc["ln1_g"], bc["ln1_b"], 1)
            dve_qparts(dve, link, 0)
            dve.wait_ge(s["in_tail"], 16 * 5)
            for n, g in (("l1_wq", "g_q"), ("l1_wk", "g_c"), ("l1_wv", "g_c")):
                nc.vector.tensor_scalar(W[n][:, :], W[n][:, :], col[g][:, 0:1], None, ALU.mult)\
                    .then_inc(s["wg_ok"], 1)
            dve.wait_ge(s["q_rows"], 16)
            dve_attend(dve, link, 0)
            dve.wait_ge(L[0]["fin_ok"], U + CREDIT)
            value_bias(dve, slice((TT - 1) * TP, TOK))
            dve.wait_ge(s["y_ps"], 2)
            add_output(dve, link, 0, LAST)
            normalise(dve, 3, LAST).then_inc(s["x_ok"], 1)
            residual(dve, link, bc["ln2_g"], bc["ln2_b"], 2)
            dve.wait_ge(s["identb_ok"], 11)
            dve.wait_ge(s["rt_ps"], 1)
            link(nc.vector.tensor_tensor(logit[:, :, :], bank[7][0:TP, 0:TT * E].rearrange("p (t e) -> p t e", e=E),
                                         wide(rb[:, :], TT, 1), ALU.add))
            link(nc.vector.tensor_reduce(g1[:, 0, :], logit[:, :, :], AX.X, ALU.max))
            nc.vector.tensor_tensor(logit[:, :, :], logit[:, :, :], wide(g1[:, 0, :], E, 2), ALU.subtract)\
                .then_inc(s["rt_ok"], 1)
            dve.wait_ge(s["rt_exp"], 1)
            link(nc.vector.tensor_reduce(g1[:, 1, :], prob[:, :, :], AX.X, ALU.add))
            link(nc.vector.reciprocal(g1[:, 0, :], g1[:, 1, :]))
            link(nc.vector.tensor_tensor(prob[:, :, :], prob[:, :, :], wide(g1[:, 0, :], E, 2), ALU.mult))

            def first_best(one, top):
                link(nc.vector.tensor_reduce(top, prob[:, :, :], AX.X, ALU.max))
                link(nc.vector.tensor_tensor(gtmp[:, :, :], prob[:, :, :], wide(top, E, 2), ALU.is_equal))
                link(nc.vector.tensor_tensor(gtmp[:, :, :], gtmp[:, :, :], order[:, :, :], ALU.mult))
                link(nc.vector.tensor_reduce(g1[:, 7, :], gtmp[:, :, :], AX.X, ALU.max))
                link(nc.vector.tensor_tensor(one[:, :, :], order[:, :, :], wide(g1[:, 7, :], E, 2), ALU.is_equal))

            first_best(one1, g1[:, 4, :])
            link(nc.vector.scalar_tensor_tensor(out=prob[:, :, :], in0=one1[:, :, :], scalar=-2.0,
                                                in1=prob[:, :, :], op0=ALU.mult, op1=ALU.add))
            first_best(one2, g1[:, 5, :])
            nc.vector.tensor_tensor(g1[:, 2, :], g1[:, 5, :], g1[:, 4, :], ALU.subtract).then_inc(s["rt_ok"], 1)
            dve.wait_ge(s["rt_exp"], 2)
            link(nc.vector.tensor_scalar(g1[:, 0, :], g1[:, 3, :], 1.0, None, ALU.add))
            link(nc.vector.reciprocal(g1[:, 6, :], g1[:, 0, :]))
            link(nc.vector.tensor_tensor(g1[:, 1, :], g1[:, 3, :], g1[:, 6, :], ALU.mult))
            link(nc.vector.tensor_tensor(one1[:, :, :], one1[:, :, :], wide(g1[:, 6, :], E, 2), ALU.mult))
            link(nc.vector.tensor_tensor(one2[:, :, :], one2[:, :, :], wide(g1[:, 1, :], E, 2), ALU.mult))
            nc.vector.tensor_tensor(logit[:, :, :], one1[:, :, :], one2[:, :, :], ALU.add).then_inc(s["gate_ok"], 1)
            dve_ss(dve, 1, 2)
            dve.wait_ge(s["xT_ps"], 3)
            nc.vector.tensor_copy(x_new[:, :, :], x_res[:, :, :]).then_inc(s["y_used"], 1)
            dve.wait_ge(s["gate_ok"], 1)

            def add_expert(e, r):
                dve.wait_ge(s["y_used"], e + 2 * CREDIT)
                dve.wait_ge(s["y_part"], 4 * e + 4)
                gate = slice(e, e + 1) if isinstance(e, int) else bass.ds(e, 1)
                for t in range(TT):
                    ins = nc.vector.scalar_tensor_tensor(
                        out=x_new[:, t, :], in0=bank[4 + r][0:TP, t * 128:(t + 1) * 128],
                        scalar=logit[:, t, gate], in1=x_new[:, t, :], op0=ALU.mult, op1=ALU.add)
                ins.then_inc(s["y_used"], 1)

            with dve.Fori(0, E // 2 - 1) as i:
                for r in range(2):
                    add_expert(2 * i + r, r)
            add_expert(E - 2, 0)
            dve.wait_ge(s["b2_ps"], 1)
            dve.wait_ge(s["y_used"], E - 1 + 2 * CREDIT)
            link(nc.vector.tensor_tensor(x_new[:, :, :], bank[7][0:TP, :].rearrange("p (t d) -> p t d", t=TT),
                                         x_new[:, :, :], ALU.add))
            add_expert(E - 1, 1)
            dve.wait_ge(s["y_used"], E + 2 * CREDIT)
            moments(dve, link, ALL)
            normalise(dve, 4, ALL).then_inc(s["x_ok"], 1)
            residual(dve, link, bc["ln3_g"], bc["ln3_b"], 3)
            sumsq(dve, link, ALL)
            dve.wait_ge(s["rstd_ok"], 5)
            nc.vector.tensor_tensor(x_new[:, :, :], x_res[:, :, :], wide(rstd[:, :], 128, 2), ALU.mult)\
                .then_inc(s["x_ok"], 1)
            dve_qparts(dve, link, 1)
            dve_attend(dve, link, 1)
            dve.wait_ge(s["y_ps"], 3)
            add_output(dve, link, 1, LAST)
            scale_output(dve, link, 7, LAST)

        @block.gpsimd
        def _(pool):
            give_credits(pool, "pool")
            link = Chain(pool, s["pool_c"])
            nc.gpsimd.memset(krep[0:96, :, :, SK:KW], 0.0).then_inc(s["zeros_ok"], 1)
            nc.gpsimd.memset(v9[:, :, :, :], 1.0).then_inc(s["zeros_ok"], 1)
            for tile, value in ((neghalf, -0.5), (inv_d, 1.0 / D), (rms_eps, 1e-6), (zero, 0.0),
                                (euler, float(np.e))):
                ins = nc.gpsimd.memset(tile[:, :], value)
            ins.then_inc(s["zeros_ok"], 1)
            nc.gpsimd.memset(mparts[:, :, :, :], 1.0).then_inc(s["identb_ok"], 1)
            for e in range(E):
                nc.gpsimd.memset(order[:, :, e], float(E - e)).then_inc(s["identb_ok"], 1)
            link(nc.gpsimd.memset(qrows[:, :], 1.0))
            nc.gpsimd.memset(qrows[0:3, :], 0.0).then_inc(s["krow_ok"], 1)
            nc.gpsimd.memset(vb[:, :, :], 0.0).then_inc(s["vb_zero"], 1)
            nc.gpsimd.memset(weights[:, :, 7 * S:WT], 0.0).then_inc(s["vb_zero"], 1)
            pool.wait_ge(s["in_cst"], 16)
            pool.wait_ge(s["qT_ok"], 1)

            def block_diagonal(b):
                if b >= 2:
                    pool.wait_ge(s["s_ps"], b - 1)
                nc.gpsimd.tensor_tensor(qbd[:, b % 2], wide(qT[:, b * S:(b + 1) * S], H, 1),
                                        wide(cst[:, C_HEAD:C_HEAD + H], S, 2), ALU.mult).then_inc(s["qbd_ok"], 1)

            block_diagonal(0)
            block_diagonal(1)
            for b in range(B):
                if b + 2 < B:
                    block_diagonal(b + 2)
                for k in (2 * b - 3, 2 * b - 2):
                    if k > 0 and PROLOGUE[k][0] == "K":
                        pool_low(pool, 0, *PROLOGUE[k][1:4])
            pool.wait_ge(s["in_mask"], 32)
            nc.gpsimd.tensor_copy(mask_col[:, :, :], mask_col8[:, :, :]).then_inc(s["identb_ok"], 1)
            nc.gpsimd.tensor_scalar(mask_row, mask_row8[:, :], BIG, -BIG, ALU.mult, ALU.add).then_inc(s["mask_ok"], 1)
            pool.wait_ge(s["in_wo"], 16 * IN_WO)
            pool.wait_ge(s["xT_ps"], 1)
            nc.gpsimd.tensor_tensor(x_res[:, :, :], x_res[:, :, :], wide(bc["sa_bo"][:, :], TT, 1), ALU.add)\
                .then_inc(s["bias_ok"], 1)
            nc.gpsimd.tensor_tensor(bc["ln1_b"][:, :], bc["ln1_b"][:, :], bc["ca_bo"][:, :], ALU.add)\
                .then_inc(s["bias_ok"], 1)
            pool_rstd(pool, link, 1, 1.0, 1e-5)
            pool_qparts(pool, link, 0)
            pool.wait_ge(s["mask_written"], 16)
            pool_attend(pool, link, 0)
            pool_rstd(pool, link, 3, 1.0, 1e-5, LAST)
            pool.wait_ge(s["rt_ok"], 2)
            nc.gpsimd.tensor_tensor(g1[:, 3, :], euler[0:TP, 0:TT], g1[:, 2, :], ALU.pow).then_inc(s["rt_exp"], 1)
            pool_squares(pool, 1, 2, 0)
            pool_norm(pool, 1, 2, 0)
            pool_rstd(pool, link, 4, 1.0, 1e-5)
            pool_rstd(pool, link, 5, 1.0 / D, 1e-6)
            pool_qparts(pool, link, 1)
            pool_attend(pool, link, 1)
            pool_rstd(pool, link, 7, 1.0 / D, 1e-6, LAST)


_INS = ["x", "ctx_1024"] + ["L0_xattn_" + n for n in (
    "sa_wq", "sa_bq", "sa_wk", "sa_bk", "sa_wv", "sa_bv", "sa_wo", "sa_bo", "ca_wq", "ca_bq", "ca_wk", "ca_bk",
    "ca_wv", "ca_bo", "ln1_g", "ln1_b", "ln2_g", "ln2_b", "ln3_g", "ln3_b", "router_w", "router_b",
    "e_w1", "e_w2", "e_b2")] + ["L1_xattn_" + n for n in ("Wq", "Wk", "Wv", "g_q", "g_c", "g_out")]


def _rows9(w):
    out = np.zeros((128, HALVES, w.shape[1]), w.dtype)
    for h in range(H):
        hf, g, j = h // 8, (h % 8) // 2, h % 2
        at = 32 * g + VW * j
        out[at:at + HD, hf] = w[h * HD:(h + 1) * HD]
    return out


def kernel(**inputs):
    import concourse.bacc as _bacc
    from concourse.bass_utils import run_bass_kernel_spmd as _run

    v = {n: np.ascontiguousarray(inputs[n]) for n in _INS}
    mask = np.ascontiguousarray(inputs["mask_BxS2_bf1"]).view(np.uint8).reshape(B, KP, KC)
    v["mask_col"] = np.ascontiguousarray(mask.transpose(1, 0, 2))
    v["mask_row"] = np.ascontiguousarray(mask.transpose(0, 2, 1)).reshape(B, SK)
    v["wo9_0"] = _rows9(np.asarray(inputs["L0_xattn_ca_wo"]))
    v["wo9_1"] = _rows9(np.asarray(inputs["L1_xattn_Wo"]))
    v["bv9"] = np.ascontiguousarray(_rows9(np.asarray(inputs["L0_xattn_ca_bv"]).reshape(128, 1))[:, :, 0])
    v["b1T"] = np.ascontiguousarray(np.asarray(inputs["L0_xattn_e_b1"]).reshape(E * 4, 128).T)
    v["consts"] = constants()
    v["selq"] = query_selection()
    nc = _bacc.Bacc("TRN2", target_bir_lowering=False, num_devices=1)
    arrays, a = {}, {}
    for name, array in v.items():
        arrays[f"in_{name}"] = array
        a[name] = nc.dram_tensor(f"in_{name}", array.shape, mybir.dt.from_np(array.dtype), kind="ExternalInput").ap()
    out = nc.dram_tensor("out_0", (B, S, D), F32, kind="ExternalOutput").ap()
    build_program(nc, a, out)
    r = _run(nc, [arrays], core_ids=[0])
    return r.results[0]["out_0"]
```
